# Optimizing a Trainium2 kernel written in Bass

```python
import numpy as np
import jax
import jax.numpy as jnp

def _softmax(x, axis=-1):
    return jax.nn.softmax(x, axis=axis)

def _gelu(x):
    return jax.nn.gelu(x, approximate=True)

def _silu(x):
    return jax.nn.silu(x)

def _sigmoid(x):
    return jax.nn.sigmoid(x)

def _layernorm(x, axis=-1, eps=1e-05):
    m = jnp.mean(x, axis=axis, keepdims=True)
    v = jnp.var(x, axis=axis, keepdims=True)
    return (x - m) / jnp.sqrt(v + eps)

def _scatter_add(tgt, idx, src, axis=0):
    return tgt.at[idx].add(src)

def _segment_sum(src, seg, n):
    return jax.ops.segment_sum(src, seg, n)
kernel_name = 'mk_decoder_preln_d2_seqx_r8_f1781a'

def setup_inputs(seed: int=0):
    np.random.seed(seed)
    _w = jnp.asarray

    def _rec_inputs():
        import jax
        import jax.numpy as jnp
        _rk = jax.random.key(seed)
        x = -7.109e-05 + 0.9999 * jax.random.normal(jax.random.fold_in(_rk, 1), (4, 256, 256), jnp.float32)
        _lenS = 256 - jax.random.randint(jax.random.fold_in(_rk, 7), (4,), 0, max(1, 256 // 4) + 1, jnp.int32)
        _lenS2 = 256 - jax.random.randint(jax.random.fold_in(_rk, 8), (4,), 0, max(1, 256 // 4) + 1, jnp.int32)
        _ctx_512P = jax.random.normal(jax.random.fold_in(_rk, 11), (4, 16, 64), jnp.float32)
        _ctx_512c = jax.random.dirichlet(jax.random.fold_in(_rk, 511), 0.3 * jnp.ones((16,), jnp.float32), (4, 256))
        _ctx_512t = jnp.einsum('bsk,bkd->bsd', _ctx_512c, _ctx_512P)
        _ctx_512t = _ctx_512t * jax.lax.rsqrt(jnp.mean(jnp.square(_ctx_512t)) + 1e-12) * 0.953939
        ctx_512 = 2.81802e-05 + 1.00001 * (_ctx_512t + 0.3 * jax.random.normal(jax.random.fold_in(_rk, 611), (4, 256, 64), jnp.float32))
        return (x, ctx_512)
    x, ctx_512 = _rec_inputs()

    def _L0_attn_setup():
        import jax, jax.numpy as jnp
        import numpy as np
        EPS = 1e-06

        def _sigma(x):
            return jax.nn.elu(x) + 1.0

        def _reference_tuple_inner(hidden_states, w_q, w_k, w_v, w_o, gate, M, z):
            q = jnp.einsum('bsh,dh->bsd', hidden_states, w_q)
            k = jnp.einsum('bsh,dh->bsd', hidden_states, w_k)
            v = jnp.einsum('bsh,dh->bsd', hidden_states, w_v)
            sq = _sigma(q)
            mem_num = jnp.einsum('bsd,de->bse', sq, M)
            mem_den = jnp.einsum('bsd,d->bs', sq, z) + EPS
            memory_output = mem_num / mem_den[..., None]
            pq, pk = (_sigma(q), _sigma(k))
            kv_cum = jnp.cumsum(jnp.einsum('bsd,bse->bsde', pk, v), axis=1)
            k_cum = jnp.cumsum(pk, axis=1)
            num = jnp.einsum('bsd,bsde->bse', pq, kv_cum)
            den = jnp.einsum('bsd,bsd->bs', pq, k_cum) + EPS
            local_output = num / den[..., None]
            g = jax.nn.sigmoid(gate)
            output = g * memory_output + (1.0 - g) * local_output
            sk = _sigma(k)
            v_ret = jnp.einsum('bsd,de->bse', sk, M) / (jnp.einsum('bsd,d->bs', sk, z) + EPS)[..., None]
            M_new = M + jnp.einsum('bsd,bse->de', sk, v - v_ret)
            z_new = z + jnp.sum(sk, axis=(0, 1))
            out = jnp.einsum('bsd,hd->bsh', output, w_o)
            return (out, M_new, z_new)
        key = jax.random.key(seed)
        ks = jax.random.split(key, 8)
        B, S, H, D = (2, 512, 256, 128)
        sc = 1.0 / np.sqrt(H)
        return {'hidden_states': jax.random.normal(ks[0], (B, S, H), jnp.float32), 'w_q': jax.random.normal(ks[1], (D, H), jnp.float32) * sc, 'w_k': jax.random.normal(ks[2], (D, H), jnp.float32) * sc, 'w_v': jax.random.normal(ks[3], (D, H), jnp.float32) * sc, 'w_o': jax.random.normal(ks[4], (H, D), jnp.float32) * (1.0 / np.sqrt(D)), 'gate': jnp.zeros((1,), jnp.float32), 'M': jax.random.normal(ks[5], (D, D), jnp.float32), 'z': jax.random.uniform(ks[6], (D,), jnp.float32) + 0.5}
    _L0_attn_all = _L0_attn_setup()
    _L0_attn_in = {k: v for k, v in _L0_attn_all.items() if k in ('w_q', 'w_k', 'w_v', 'w_o', 'gate', 'M', 'z')}
    del _L0_attn_all

    def _L0_xattn_setup():
        import jax, jax.numpy as jnp
        import numpy as np
        EPS = 1e-06
        IMAGE_DIMS = 256
        key = jax.random.key(seed)
        k1, k2, k3 = jax.random.split(key, 3)
        B, I, J, D = (16, 256, 256, 64)
        p = jax.random.normal(k1, (B, I, J), dtype=jnp.float32)
        k_v = jax.random.normal(k2, (B, J, D), dtype=jnp.float32)
        W_k = jax.random.normal(k3, (D, D), dtype=jnp.float32) * (1.0 / np.sqrt(D))
        b_k = jnp.zeros((D,), dtype=jnp.float32)
        ln_gamma = jnp.ones((J,), dtype=jnp.float32)
        ln_beta = jnp.zeros((J,), dtype=jnp.float32)
        return {'p': p, 'k_v': k_v, 'W_k': W_k, 'b_k': b_k, 'ln_gamma': ln_gamma, 'ln_beta': ln_beta}
    _L0_xattn_all = _L0_xattn_setup()
    _L0_xattn_in = {k: v for k, v in _L0_xattn_all.items() if k in ('W_k', 'b_k', 'ln_gamma', 'ln_beta')}
    del _L0_xattn_all

    def _L0_ffn_setup():
        import jax, jax.numpy as jnp
        import numpy as np
        Q_MAX = 127.0

        def _ste_round(x):
            return x + jax.lax.stop_gradient(jnp.round(x) - x)
        key = jax.random.key(seed)
        k1, k2 = jax.random.split(key)
        B, S, D_IN, D_OUT = (4, 512, 256, 256)
        x = jax.random.normal(k1, (B, S, D_IN), dtype=jnp.float32)
        weight = jax.random.normal(k2, (D_OUT, D_IN), dtype=jnp.float32) / np.sqrt(D_IN)
        return {'x': x, 'weight': weight}
    _L0_ffn_all = _L0_ffn_setup()
    _L0_ffn_in = {k: v for k, v in _L0_ffn_all.items() if k in ('weight',)}
    del _L0_ffn_all

    def _L1_attn_setup():
        import jax, jax.numpy as jnp
        import numpy as np
        B, T, D = (1, 256, 256)
        H, DK, DV, M = (16, 64, 128, 64)
        KEY_DIM, VALUE_DIM = (H * DK, H * DV)
        EPS = 1e-05
        CLAMP_MIN, CLAMP_MAX = (-32.0, 32.0)
        XAVIER_GAIN = 2.0 ** (-2.5)

        def _chunk_abc(q, k, v, s):
            scale = q.shape[-1] ** (-0.5)
            z = jax.lax.cumlogsumexp(s, axis=2)
            g = jnp.exp(jnp.concatenate([z[:, :, :1], z[:, :, :-1]], axis=2) - z)
            p = jnp.exp(s - z)
            tfirst = lambda x: jnp.moveaxis(x, 2, 0)
            qT, kT, vT, pT, gT = map(tfirst, (q * scale, k, v, p, g))
            b, h = (q.shape[0], q.shape[1])
            hk0 = jnp.zeros((b, h, q.shape[-1], s.shape[-1]), q.dtype)

            def step_k(hk, x):
                q_t, k_t, p_t, g_t = x
                hk = hk * g_t[:, :, None, :] + k_t[..., None] * p_t[:, :, None, :]
                return (hk, jnp.einsum('bhk,bhkm->bhm', q_t, hk))
            _, okT = jax.lax.scan(step_k, hk0, (qT, kT, pT, gT))
            pvT = jax.nn.softmax(okT, axis=-1)
            hv0 = jnp.zeros((b, h, s.shape[-1], v.shape[-1]), q.dtype)

            def step_v(hv, x):
                pv_t, v_t, p_t, g_t = x
                hv = hv * g_t[..., None] + p_t[..., None] * v_t[:, :, None, :]
                return (hv, jnp.einsum('bhm,bhmv->bhv', pv_t, hv))
            _, ovT = jax.lax.scan(step_v, hv0, (pvT, vT, pT, gT))
            return jnp.moveaxis(ovT, 0, 2)
        key = jax.random.key(seed)
        ks = jax.random.split(key, 8)

        def w(k, fan_in, fan_out):
            std = XAVIER_GAIN * np.sqrt(2.0 / (fan_in + fan_out))
            return jax.random.normal(k, (fan_in, fan_out), jnp.float32) * std
        return {'hidden_states': jax.random.normal(ks[0], (B, T, D), jnp.float32), 'Wq': w(ks[1], D, KEY_DIM), 'Wk': w(ks[2], D, KEY_DIM), 'Wv': w(ks[3], D, VALUE_DIM), 'Wg': w(ks[4], D, VALUE_DIM), 'Ws': w(ks[5], D, H * M), 'Wo': w(ks[6], VALUE_DIM, D), 'g_norm_weight': jnp.ones((DV,), jnp.float32)}
    _L1_attn_all = _L1_attn_setup()
    _L1_attn_in = {k: v for k, v in _L1_attn_all.items() if k in ('Wq', 'Wk', 'Wv', 'Wg', 'Ws', 'Wo', 'g_norm_weight')}
    del _L1_attn_all

    def _L1_xattn_setup():
        import jax, jax.numpy as jnp
        import numpy as np
        B, S, L = (2, 128, 128)
        DIM_Q, H, K, D_C, D_CQ, R = (256, 16, 128, 64, 192, 64)

        def _rope_tables(seq_len, dim, dtype):
            inv_freq = 1.0 / 10000.0 ** (jnp.arange(0, dim, 2, dtype=dtype) / dim)
            t = jnp.arange(seq_len, dtype=dtype)
            freqs = t[:, None] * inv_freq[None, :]
            sin = jnp.repeat(jnp.sin(freqs), 2, axis=-1)
            cos = jnp.repeat(jnp.cos(freqs), 2, axis=-1)
            return (sin, cos)

        def _rotate_half(x):
            h = x.shape[-1] // 2
            return jnp.concatenate([-x[..., h:], x[..., :h]], axis=-1)
        key = jax.random.key(seed)
        ks = jax.random.split(key, 8)
        s_in = 1.0 / np.sqrt(DIM_Q)
        s_k = 1.0 / np.sqrt(K)
        s_cq = 1.0 / np.sqrt(D_CQ)
        s_c = 1.0 / np.sqrt(D_C)
        return {'hidden_q': jax.random.normal(ks[0], (B, S, DIM_Q), jnp.float32), 'kv_c': jax.random.normal(ks[1], (B, L, D_C), jnp.float32), 'Wq': jax.random.normal(ks[2], (H * K, DIM_Q), jnp.float32) * s_in, 'w_kc_q': jax.random.normal(ks[3], (H, K, D_CQ), jnp.float32) * s_k, 'w_kc_kv': jax.random.normal(ks[4], (H, K, D_C), jnp.float32) * s_k, 'W_qr': jax.random.normal(ks[5], (H, D_CQ, R), jnp.float32) * s_cq / np.sqrt(R), 'W_kr': jax.random.normal(ks[6], (H, D_C, R), jnp.float32) * s_c, 'Wo': jax.random.normal(ks[7], (DIM_Q, H * K), jnp.float32) * s_k}
    _L1_xattn_all = _L1_xattn_setup()
    _L1_xattn_in = {k: v for k, v in _L1_xattn_all.items() if k in ('Wq', 'w_kc_q', 'w_kc_kv', 'W_qr', 'W_kr', 'Wo')}
    del _L1_xattn_all

    def _L1_ffn_setup():
        import jax, jax.numpy as jnp
        import numpy as np
        B, S, D, F, E, SH, K = (2, 256, 256, 128, 16, 2, 2)

        def _experts_all(x, g, gb, w1, b1, w2, b2):
            y = jax.nn.gelu(jnp.einsum('bsd,edf->bsef', x, g) + gb, approximate=False)
            y = y * (jnp.einsum('bsd,edf->bsef', x, w1) + b1)
            return jnp.einsum('bsef,efd->bsed', y, w2) + b2
        key = jax.random.key(seed)
        ks = jax.random.split(key, 8)
        std = 0.02
        mk = lambda k, sh: jax.random.normal(k, sh, jnp.float32) * std
        return {'x': jax.random.normal(ks[0], (B, S, D), jnp.float32), 'wa': mk(ks[1], (D, E)), 'rg': mk(ks[2], (E, D, F)), 'rgb': jnp.zeros((E, F), jnp.float32), 'rw1': mk(ks[3], (E, D, F)), 'rb1': jnp.zeros((E, F), jnp.float32), 'rw2': mk(ks[4], (E, F, D)), 'rb2': jnp.zeros((E, D), jnp.float32), 'sg': mk(ks[5], (SH, D, F)), 'sgb': jnp.zeros((SH, F), jnp.float32), 'sw1': mk(ks[6], (SH, D, F)), 'sb1': jnp.zeros((SH, F), jnp.float32), 'sw2': mk(ks[7], (SH, F, D)), 'sb2': jnp.zeros((SH, D), jnp.float32)}
    _L1_ffn_all = _L1_ffn_setup()
    _L1_ffn_in = {k: v for k, v in _L1_ffn_all.items() if k in ('wa', 'rg', 'rgb', 'rw1', 'rb1', 'rw2', 'rb2', 'sg', 'sgb', 'sw1', 'sb1', 'sw2', 'sb2')}
    del _L1_ffn_all
    return {'x': x, 'ctx_512': ctx_512, 'L0_attn_w_q': _L0_attn_in['w_q'], 'L0_attn_w_k': _L0_attn_in['w_k'], 'L0_attn_w_v': _L0_attn_in['w_v'], 'L0_attn_w_o': _L0_attn_in['w_o'], 'L0_attn_gate': _L0_attn_in['gate'], 'L0_attn_M': _L0_attn_in['M'], 'L0_attn_z': _L0_attn_in['z'], 'L0_xattn_W_k': _L0_xattn_in['W_k'], 'L0_xattn_b_k': _L0_xattn_in['b_k'], 'L0_xattn_ln_gamma': _L0_xattn_in['ln_gamma'], 'L0_xattn_ln_beta': _L0_xattn_in['ln_beta'], 'L0_ffn_weight': _L0_ffn_in['weight'], 'L1_attn_Wq': _L1_attn_in['Wq'], 'L1_attn_Wk': _L1_attn_in['Wk'], 'L1_attn_Wv': _L1_attn_in['Wv'], 'L1_attn_Wg': _L1_attn_in['Wg'], 'L1_attn_Ws': _L1_attn_in['Ws'], 'L1_attn_Wo': _L1_attn_in['Wo'], 'L1_attn_g_norm_weight': _L1_attn_in['g_norm_weight'], 'L1_xattn_Wq': _L1_xattn_in['Wq'], 'L1_xattn_w_kc_q': _L1_xattn_in['w_kc_q'], 'L1_xattn_w_kc_kv': _L1_xattn_in['w_kc_kv'], 'L1_xattn_W_qr': _L1_xattn_in['W_qr'], 'L1_xattn_W_kr': _L1_xattn_in['W_kr'], 'L1_xattn_Wo': _L1_xattn_in['Wo'], 'L1_ffn_wa': _L1_ffn_in['wa'], 'L1_ffn_rg': _L1_ffn_in['rg'], 'L1_ffn_rgb': _L1_ffn_in['rgb'], 'L1_ffn_rw1': _L1_ffn_in['rw1'], 'L1_ffn_rb1': _L1_ffn_in['rb1'], 'L1_ffn_rw2': _L1_ffn_in['rw2'], 'L1_ffn_rb2': _L1_ffn_in['rb2'], 'L1_ffn_sg': _L1_ffn_in['sg'], 'L1_ffn_sgb': _L1_ffn_in['sgb'], 'L1_ffn_sw1': _L1_ffn_in['sw1'], 'L1_ffn_sb1': _L1_ffn_in['sb1'], 'L1_ffn_sw2': _L1_ffn_in['sw2'], 'L1_ffn_sb2': _L1_ffn_in['sb2']}

def reference(x, ctx_512, L0_attn_w_q, L0_attn_w_k, L0_attn_w_v, L0_attn_w_o, L0_attn_gate, L0_attn_M, L0_attn_z, L0_xattn_W_k, L0_xattn_b_k, L0_xattn_ln_gamma, L0_xattn_ln_beta, L0_ffn_weight, L1_attn_Wq, L1_attn_Wk, L1_attn_Wv, L1_attn_Wg, L1_attn_Ws, L1_attn_Wo, L1_attn_g_norm_weight, L1_xattn_Wq, L1_xattn_w_kc_q, L1_xattn_w_kc_kv, L1_xattn_W_qr, L1_xattn_W_kr, L1_xattn_Wo, L1_ffn_wa, L1_ffn_rg, L1_ffn_rgb, L1_ffn_rw1, L1_ffn_rb1, L1_ffn_rw2, L1_ffn_rb2, L1_ffn_sg, L1_ffn_sgb, L1_ffn_sw1, L1_ffn_sb1, L1_ffn_sw2, L1_ffn_sb2):
    import jax
    import jax.numpy as jnp

    def _L0_attn_ref(hidden_states, w_q, w_k, w_v, w_o, gate, M, z):
        import jax, jax.numpy as jnp
        import numpy as np
        EPS = 1e-06

        def _sigma(x):
            return jax.nn.elu(x) + 1.0

        def _reference_tuple_inner(hidden_states, w_q, w_k, w_v, w_o, gate, M, z):
            q = jnp.einsum('bsh,dh->bsd', hidden_states, w_q)
            k = jnp.einsum('bsh,dh->bsd', hidden_states, w_k)
            v = jnp.einsum('bsh,dh->bsd', hidden_states, w_v)
            sq = _sigma(q)
            mem_num = jnp.einsum('bsd,de->bse', sq, M)
            mem_den = jnp.einsum('bsd,d->bs', sq, z) + EPS
            memory_output = mem_num / mem_den[..., None]
            pq, pk = (_sigma(q), _sigma(k))
            kv_cum = jnp.cumsum(jnp.einsum('bsd,bse->bsde', pk, v), axis=1)
            k_cum = jnp.cumsum(pk, axis=1)
            num = jnp.einsum('bsd,bsde->bse', pq, kv_cum)
            den = jnp.einsum('bsd,bsd->bs', pq, k_cum) + EPS
            local_output = num / den[..., None]
            g = jax.nn.sigmoid(gate)
            output = g * memory_output + (1.0 - g) * local_output
            sk = _sigma(k)
            v_ret = jnp.einsum('bsd,de->bse', sk, M) / (jnp.einsum('bsd,d->bs', sk, z) + EPS)[..., None]
            M_new = M + jnp.einsum('bsd,bse->de', sk, v - v_ret)
            z_new = z + jnp.sum(sk, axis=(0, 1))
            out = jnp.einsum('bsd,hd->bsh', output, w_o)
            return (out, M_new, z_new)
        return _reference_tuple_inner(hidden_states, w_q, w_k, w_v, w_o, gate, M, z)[0]

    def _L0_xattn_ref(p, k_v, W_k, b_k, ln_gamma, ln_beta):
        import jax, jax.numpy as jnp
        import numpy as np
        EPS = 1e-06
        IMAGE_DIMS = 256
        kv = k_v @ W_k.T + b_k
        out = jnp.einsum('bij,bjd->bid', p, kv)
        scale = IMAGE_DIMS ** (-0.5)
        sim = jnp.einsum('bid,bjd->bij', out, kv) * scale
        mu = jnp.mean(sim, axis=-1, keepdims=True)
        var = jnp.var(sim, axis=-1, keepdims=True)
        sim = (sim - mu) * jax.lax.rsqrt(var + EPS) * ln_gamma + ln_beta
        attn = jax.nn.softmax(sim, axis=-1)
        return attn

    def _L0_ffn_ref(x, weight):
        import jax, jax.numpy as jnp
        import numpy as np
        Q_MAX = 127.0

        def _ste_round(x):
            return x + jax.lax.stop_gradient(jnp.round(x) - x)
        w_scale = jnp.maximum(jnp.mean(jnp.abs(weight)), 1e-06)
        w_norm = weight / w_scale
        w_quant = jnp.clip(_ste_round(w_norm), -1.0, 1.0)
        a_scale = jnp.clip(jnp.max(jnp.abs(x), axis=-1, keepdims=True), 1e-08, None)
        x_quant = jnp.clip(_ste_round(x * (Q_MAX / a_scale)), -Q_MAX, Q_MAX)
        y = jnp.einsum('bsi,oi->bso', x_quant, w_quant)
        y = y * (w_scale * (a_scale / Q_MAX))
        return y

    def _L1_attn_ref(hidden_states, Wq, Wk, Wv, Wg, Ws, Wo, g_norm_weight):
        import jax, jax.numpy as jnp
        import numpy as np
        B, T, D = (1, 256, 256)
        H, DK, DV, M = (16, 64, 128, 64)
        KEY_DIM, VALUE_DIM = (H * DK, H * DV)
        EPS = 1e-05
        CLAMP_MIN, CLAMP_MAX = (-32.0, 32.0)
        XAVIER_GAIN = 2.0 ** (-2.5)

        def _chunk_abc(q, k, v, s):
            scale = q.shape[-1] ** (-0.5)
            z = jax.lax.cumlogsumexp(s, axis=2)
            g = jnp.exp(jnp.concatenate([z[:, :, :1], z[:, :, :-1]], axis=2) - z)
            p = jnp.exp(s - z)
            tfirst = lambda x: jnp.moveaxis(x, 2, 0)
            qT, kT, vT, pT, gT = map(tfirst, (q * scale, k, v, p, g))
            b, h = (q.shape[0], q.shape[1])
            hk0 = jnp.zeros((b, h, q.shape[-1], s.shape[-1]), q.dtype)

            def step_k(hk, x):
                q_t, k_t, p_t, g_t = x
                hk = hk * g_t[:, :, None, :] + k_t[..., None] * p_t[:, :, None, :]
                return (hk, jnp.einsum('bhk,bhkm->bhm', q_t, hk))
            _, okT = jax.lax.scan(step_k, hk0, (qT, kT, pT, gT))
            pvT = jax.nn.softmax(okT, axis=-1)
            hv0 = jnp.zeros((b, h, s.shape[-1], v.shape[-1]), q.dtype)

            def step_v(hv, x):
                pv_t, v_t, p_t, g_t = x
                hv = hv * g_t[..., None] + p_t[..., None] * v_t[:, :, None, :]
                return (hv, jnp.einsum('bhm,bhmv->bhv', pv_t, hv))
            _, ovT = jax.lax.scan(step_v, hv0, (pvT, vT, pT, gT))
            return jnp.moveaxis(ovT, 0, 2)
        b, t, _ = hidden_states.shape
        to_heads = lambda x, d: jnp.transpose(x.reshape(b, t, H, d), (0, 2, 1, 3))
        q = to_heads(hidden_states @ Wq, DK)
        k = to_heads(hidden_states @ Wk, DK)
        v = to_heads(hidden_states @ Wv, DV)
        s = jnp.clip(to_heads(hidden_states @ Ws, M), CLAMP_MIN, CLAMP_MAX)
        o = jnp.transpose(_chunk_abc(q, k, v, s), (0, 2, 1, 3))
        g = (hidden_states @ Wg).reshape(b, t, H, DV)
        o = o * jax.lax.rsqrt(jnp.mean(jnp.square(o), axis=-1, keepdims=True) + EPS) * g_norm_weight
        o = o * (g * jax.nn.sigmoid(g))
        return o.reshape(b, t, VALUE_DIM) @ Wo

    def _L1_xattn_ref(hidden_q, kv_c, Wq, w_kc_q, w_kc_kv, W_qr, W_kr, Wo):
        import jax, jax.numpy as jnp
        import numpy as np
        B, S, L = (2, 128, 128)
        DIM_Q, H, K, D_C, D_CQ, R = (256, 16, 128, 64, 192, 64)

        def _rope_tables(seq_len, dim, dtype):
            inv_freq = 1.0 / 10000.0 ** (jnp.arange(0, dim, 2, dtype=dtype) / dim)
            t = jnp.arange(seq_len, dtype=dtype)
            freqs = t[:, None] * inv_freq[None, :]
            sin = jnp.repeat(jnp.sin(freqs), 2, axis=-1)
            cos = jnp.repeat(jnp.cos(freqs), 2, axis=-1)
            return (sin, cos)

        def _rotate_half(x):
            h = x.shape[-1] // 2
            return jnp.concatenate([-x[..., h:], x[..., :h]], axis=-1)
        b, s, _ = hidden_q.shape
        l = kv_c.shape[1]
        q_hk = (hidden_q @ Wq.T).reshape(b, s, H, K)
        q_big = jnp.einsum('bshk,hkq->bshq', q_hk, w_kc_q)
        sin, cos = _rope_tables(l, D_C, kv_c.dtype)
        kv_rope = kv_c * cos[None] + _rotate_half(kv_c) * sin[None]
        q_r = jnp.einsum('bshq,hqr->bhsr', q_big, W_qr)
        k_r = jnp.einsum('bld,hdr->bhlr', kv_rope, W_kr)
        scores = jnp.einsum('bhsr,bhlr->bhsl', q_r, k_r)
        attn = jax.nn.softmax(scores, axis=-1)
        ctx_c = jnp.einsum('bhsl,bld->bhsd', attn, kv_rope)
        ctx_lat = jnp.einsum('bhsd,hkd->bshk', ctx_c, w_kc_kv)
        out = ctx_lat.reshape(b, s, H * K) @ Wo.T
        return out

    def _L1_ffn_ref(x, wa, rg, rgb, rw1, rb1, rw2, rb2, sg, sgb, sw1, sb1, sw2, sb2):
        import jax, jax.numpy as jnp
        import numpy as np
        B, S, D, F, E, SH, K = (2, 256, 256, 128, 16, 2, 2)

        def _experts_all(x, g, gb, w1, b1, w2, b2):
            y = jax.nn.gelu(jnp.einsum('bsd,edf->bsef', x, g) + gb, approximate=False)
            y = y * (jnp.einsum('bsd,edf->bsef', x, w1) + b1)
            return jnp.einsum('bsef,efd->bsed', y, w2) + b2
        aff = jax.nn.sigmoid(jnp.einsum('bsd,de->bse', x, wa))
        topk_p, topk_i = jax.lax.top_k(aff, K)
        topk_p = topk_p / jnp.sum(topk_p, axis=-1, keepdims=True)
        combine = jnp.sum(jax.nn.one_hot(topk_i, E, dtype=x.dtype) * topk_p[..., None], axis=2)
        routed = jnp.einsum('bsed,bse->bsd', _experts_all(x, rg, rgb, rw1, rb1, rw2, rb2), combine)
        shared = jnp.sum(_experts_all(x, sg, sgb, sw1, sb1, sw2, sb2), axis=2)
        return x + shared + routed
    x = x + _L0_attn_ref(_layernorm(x, axis=-1), L0_attn_w_q, L0_attn_w_k, L0_attn_w_v, L0_attn_w_o, L0_attn_gate, L0_attn_M, L0_attn_z)
    x = x + _L0_xattn_ref(_layernorm(x, axis=-1), ctx_512, L0_xattn_W_k, L0_xattn_b_k, L0_xattn_ln_gamma, L0_xattn_ln_beta)
    x = x + _L0_ffn_ref(_layernorm(x, axis=-1), L0_ffn_weight)
    x = x + _L1_attn_ref(_layernorm(x, axis=-1), L1_attn_Wq, L1_attn_Wk, L1_attn_Wv, L1_attn_Wg, L1_attn_Ws, L1_attn_Wo, L1_attn_g_norm_weight)
    x = x + _L1_xattn_ref(_layernorm(x, axis=-1), ctx_512, L1_xattn_Wq, L1_xattn_w_kc_q, L1_xattn_w_kc_kv, L1_xattn_W_qr, L1_xattn_W_kr, L1_xattn_Wo)
    x = x + _L1_ffn_ref(_layernorm(x, axis=-1), L1_ffn_wa, L1_ffn_rg, L1_ffn_rgb, L1_ffn_rw1, L1_ffn_rb1, L1_ffn_rw2, L1_ffn_rb2, L1_ffn_sg, L1_ffn_sgb, L1_ffn_sw1, L1_ffn_sb1, L1_ffn_sw2, L1_ffn_sb2)
    return x

_drawn_inputs = setup_inputs


def setup_inputs(seed=0):
    import zlib

    import numpy as np

    out = dict(_drawn_inputs(seed))
    spreads = {'L0_xattn_b_k': (0.0, 2.0),
     'L0_xattn_ln_gamma': (1.0, 0.6),
     'L0_xattn_ln_beta': (0.0, 0.8),
     'L1_attn_g_norm_weight': (1.0, 0.6),
     'L1_ffn_rgb': (0.0, 0.8),
     'L1_ffn_rb1': (0.0, 0.8),
     'L1_ffn_rb2': (0.0, 1.683),
     'L1_ffn_sgb': (0.0, 0.8),
     'L1_ffn_sb1': (0.0, 0.8),
     'L1_ffn_sb2': (0.0, 0.8)}
    factors = {'L0_attn_w_k': 8.0,
     'L0_attn_z': 32.711,
     'L0_xattn_W_k': 8.0,
     'L1_attn_Wq': 8.0,
     'L1_attn_Wk': 8.0,
     'L1_attn_Wv': 8.0,
     'L1_attn_Wg': 8.0,
     'L1_attn_Ws': 8.0,
     'L1_attn_Wo': 8.0,
     'L1_ffn_rg': 8.0,
     'L1_ffn_rw1': 8.0,
     'L1_ffn_rw2': 8.0,
     'L1_ffn_sg': 8.0,
     'L1_ffn_sw1': 8.0,
     'L1_ffn_sw2': 8.0}
    for name, (base, spread) in spreads.items():
        noise = np.random.default_rng([zlib.crc32(name.encode()), seed]).standard_normal(out[name].shape)
        drawn = base * np.exp(spread * noise) if base else spread * noise
        out[name] = jnp.asarray(drawn.astype(out[name].dtype))
    for name, factor in factors.items():
        out[name] = (out[name] * factor).astype(out[name].dtype)
    return out
```

```python
from contextlib import ExitStack

import numpy as np

import concourse.bass as bass
from concourse import mybir

F32 = mybir.dt.float32
BF16 = mybir.dt.bfloat16
ALU = mybir.AluOpType
ACT = mybir.ActivationFunctionType
AX = mybir.AxisListType
ds = bass.ds

P = 128
MAGIC = 1.5 * 2.0**23


class Banks:

    def __init__(self):
        self.count = [0] * 8
        self.at = {}
        self.order = []
        self.turn = 0

    def line(self, names):
        for name in names:
            bank = self.turn % 8
            self.at[name] = (bank, self.count[bank], None)
            self.order.append(name)
            self.count[bank] += 1
            self.turn += 1

    def loop(self, names, trips, banks=range(8)):
        per = [0] * 8
        for n, name in enumerate(names):
            bank = banks[n % len(banks)]
            self.at[name] = (bank, self.count[bank] + per[bank], per)
            self.order.append(name)
            per[bank] += 1
        self.count = [c + trips * p for c, p in zip(self.count, per)]
        self.turn = 0

    def bank(self, name):
        return self.at[name][0]

    def before(self, name, i=0):
        bank, count, per = self.at[name]
        return count if per is None else i * per[bank] + count

    def after(self, name, i=0):
        bank, count, per = self.at[name]
        return count + 1 if per is None else i * per[bank] + (count + 1)


class Steps:

    def __init__(self, eng, sem):
        self.eng, self.sem, self.n, self.loop, self.last = eng, sem, 0, None, None

    def now(self):
        if self.loop is None:
            return self.n
        i, per, start = self.loop
        return i * per + self.n

    def step(self, ins):
        ins.then_inc(self.sem, 1)
        self.n += 1
        self.last = (self.sem, self.now())

    def mark(self, ins, sem, value):
        ins.then_inc(sem, 1)
        self.last = (sem, value)

    def settle(self):
        self.eng.wait_ge(*self.last)

    def enter(self, i, per):
        self.loop = (i, per, self.n)

    def leave(self, trips):
        _, per, start = self.loop
        assert self.n - start == per, (self.n - start, per)
        self.n = start + trips * per
        self.loop = None
        self.last = (self.sem, self.n)


def decoder_kernel(nc, t, out):
    B, S, D = t["x"].shape
    NT = B * S // P
    TB = S // P
    NTOK = B * S
    C = D // P
    HALF = 512
    DC = t["ctx_512"].shape[2]
    DA = t["L0_attn_w_q"].shape[0]
    H = t["L1_xattn_Wq"].shape[0] // P
    PAIRS = H // 2
    M = t["L1_attn_Ws"].shape[1] // H
    DV = t["L1_attn_Wv"].shape[1] // H
    CQ = t["L1_xattn_w_kc_q"].shape[2]
    R = t["L1_xattn_W_qr"].shape[2]
    QC = CQ // 2
    E = t["L1_ffn_wa"].shape[1]
    SH = t["L1_ffn_sg"].shape[0]
    NE = E + SH
    EPS_LN = 1e-5
    EPS_A = 1e-6
    EPS_SIM = 1e-6
    EPS_RMS = 1e-5

    banks = Banks()
    ht = lambda k: [f"ht{k}_{b}" for b in range(B)]
    banks.line(["w0", "w1", "ctx0", "ctx1", "wk"])
    banks.line(ht(0) + ["aq0", "aq1", "ak0", "ak1", "av0", "av1"])
    banks.line(["kvT0", "kvT1", "kv", "wsum", "wqT"])
    A_ORDER = ["at0", "at1", "ml0", "ml1", "at2", "ml2", "ml3", "ao0", "ax0", "at3", "ml4", "ml5", "ao1", "ax1",
               "ml6", "ml7", "ao2", "ax2", "ao3", "ax3"]
    banks.line(A_ORDER)
    banks.line(["kr0", "kr1"])
    banks.line(ht(1) + [f"bo{b}" for b in range(B)] + [f"bs{b}" for b in range(B)])
    banks.line(ht(2) + [f"cy{b}" for b in range(B)])
    D_BODY = (["s0", "s1", "q0", "q1", "k0", "k1", "v0", "v1", "v2", "v3", "cu0", "cu1", "et0", "et1",
               "g0", "g1", "g2", "g3", "wot"]
              + ["at0", "at1", "at2", "at3", "u0", "ok0", "at4", "at5", "at6", "at7", "u1", "ok1"]
              + ["pt0", "w2", "bt0", "bt1", "bt2", "bt3", "o0", "o1", "pt1", "bt4", "bt5", "bt6", "bt7",
                 "ot0", "ot1", "o2", "o3", "V", "T0", "T1", "ot2", "ot3"])
    D_BODY = ["d." + n for n in D_BODY]
    banks.line(ht(3))
    banks.loop(D_BODY, PAIRS)
    banks.line([f"dx{b}" for b in range(B)] + ht(4))
    E_BODY = ["q0", "q1", "sc00", "sc01", "sc10", "sc11", "pt00", "pt01", "sc20", "cx0", "sc21", "pt10", "pt11",
              "sc30", "cx1", "sc31", "ct0", "pt20", "pt21", "ct1", "pt30", "cx2", "pt31", "ct2", "cx3", "ct3"]
    E_BODY = ["e." + n for n in E_BODY]
    banks.loop(E_BODY, PAIRS)
    banks.line([f"ex{b}" for b in range(B)] + ht(5) + ["lg", "cb0", "cb1"])
    banks.turn = 0
    banks.line([f"acc{b}" for b in range(B)])
    F_TRIPS = NE // 2
    F_BODY = [f"f.{x}{half}{e}" for e in range(2) for x in "gu" for half in range(2)]
    banks.loop(F_BODY, F_TRIPS, banks=(4, 5, 6, 7))

    with ExitStack() as ctx:
        def sb(name, shape, dt=F32):
            return ctx.enter_context(nc.sbuf_tensor(name, shape, dt))

        def sem(name):
            return ctx.enter_context(nc.semaphore(name))

        ps = ctx.enter_context(nc.psum_tensor("ps", [P, 8, 512], F32))

        X = sb("X", [P, NT, D])
        HN = sb("HN", [P, NT, D])
        HT = sb("HT", [P, C, NTOK])
        const = sb("const", [P, 4 * P])
        ident, causal, ones = const[:, 0:P], const[:, P:2 * P], const[:, 2 * P:3 * P]
        mask3 = const[:, P:4 * P]
        identb = sb("identb", [P, P], BF16)
        krT = sb("krT", [P, NTOK])
        kr = sb("kr", [P, NT, 2, DC])
        st6 = sb("st6", [P, NT, 6])
        mv = sb("mv", [P, NT, 2])
        ve = sb("ve", [P, NT])
        guess = sb("guess", [P, NT])
        nt = sb("nt", [P, NT])
        rstd = sb("rstd", [P, NT])
        nmr = sb("nmr", [P, NT])
        gg = sb("gg", [P, 2])
        col = sb("col", [P, 8 * NT])

        ARENA = 37 * 1024 + 256
        arena = sb("arena", [P, ARENA])
        at = [0]

        def carve(*shape, rows=P):
            n = int(np.prod(shape))
            v = arena[0:rows, at[0]:at[0] + n]
            at[0] += n
            assert at[0] <= ARENA
            if len(shape) == 1:
                return v
            names = "abcd"[:len(shape)]
            return v.rearrange(f"p ({' '.join(names)}) -> p {' '.join(names)}", **dict(zip(names, shape)))

        waraw = carve(3, D)
        woraw = carve(2, P)
        WT = carve(8, P)
        MZ = carve(DA + 1)
        ctxn = carve(NT, DC)
        ctxT = carve(NTOK, rows=DC + 1)
        wkraw = carve(DC, rows=DC)
        wkT = carve(DC, rows=DC + 1)
        kvT = carve(NTOK, rows=DC)
        kvn = carve(NT, DC)
        rope = carve(2, TB, DC)
        ropet = carve(NT, DC)
        gamma = carve(D)
        beta = carve(D)
        wf = carve(2, D)
        wq8 = carve(D).bitcast(BF16).rearrange("p (a b) -> p a b", a=2)
        WQT = carve(D).bitcast(BF16).rearrange("p (a b) -> p a b", a=2)
        amin = carve(4, HALF)
        SQ = carve(NTOK)
        SK = carve(NTOK)
        VV = carve(NT, DA + 1)
        AT = carve(2, 3 * P)
        AO = carve(NT, DA)
        AOT = carve(NTOK)
        BO = carve(NTOK, rows=DC)
        SIM = carve(NT, D)
        XQ = carve(NT * D // 2).bitcast(BF16).rearrange("p (a b) -> p a b", a=NT)
        XQT = carve(C * NTOK // 2).bitcast(BF16).rearrange("p (a b) -> p a b", a=C)
        wqk = sb("wqk", [P, 2, C, 2 * M])
        wsv = sb("wsv", [P, C, 2 * M + 2 * DV])
        wg = sb("wg", [P, C, 2 * DV])
        Tall = sb("Tall", [P, PAIRS, C, 2 * DC])
        W2 = sb("W2", [P, PAIRS, D])
        gnorm = sb("gnorm", [P, 1])
        NH = NT * 2
        slotmax = sb("slotmax", [P, NH])
        slotsum = sb("slotsum", [P, NH])
        rs = sb("rs", [P, NH])
        rs2 = sb("rs2", [P, NH])
        sumsq = sb("sumsq", [P, NH])
        rmsv = sb("rmsv", [P, NH])
        rmsl = sb("rmsl", [P, NH])
        coef = sb("coef", [P, NH])

        at[0] = 0
        OT = carve(PAIRS, 2, NTOK)
        WO = carve(H, D)
        qT = carve(NTOK)
        kT = carve(NTOK)
        EM = carve(NT, 2 * M)
        ET = carve(NTOK)
        RC = carve(NT, 2 * M)
        PT = RC.rearrange("p a b -> p (a b)")
        VD = carve(NT, 2 * DV)
        SG = carve(NT, 2 * DV)
        ATd = carve(4, 3 * P)
        BTd = carve(4, 3 * P)
        PM = carve(NT, 2 * M)
        JUNK = carve(4, DV)
        OD = HN
        xwq = carve(2, D)
        xkq = carve(2, CQ)
        xqr = carve(2, 2, R, rows=QC)
        xkr = carve(2, R, rows=DC)
        xkv = carve(2, DC)
        xwo = carve(2, 2 * P)
        WOTe = carve(2, D)
        KRT = carve(DC)
        U = carve(2, 2, D, rows=QC)
        VE = carve(D)

        at[0] = 0
        CT = carve(PAIRS, NTOK)
        QE = carve(NTOK)
        Tcur = carve(C, 2 * DC)
        PX = carve(2, 2, TB, S)
        PXT = carve(2, 2, TB, S)
        CX = carve(NT, 2, DC)
        nmx = carve(NT, 2)
        esum = carve(NT, 2)
        wr = carve(C, E)
        rev = carve(E)
        b2 = carve(D, rows=NE)
        fg = carve(2, C, P)
        fu = carve(2, C, P)
        fo = carve(2, D)
        fgb = carve(2, 1)
        fub = carve(2, 1)
        BC = carve(2, NTOK)
        Y = carve(2, NTOK)
        YC = carve(2, NTOK)
        AFF = carve(NT, E)
        TK = carve(4, NT, E)
        tk = carve(6, NT)
        CB = carve(NT, NE)
        CBT = carve(NTOK, rows=NE)
        comb_dram = nc.dram_tensor("comb_by_expert", [NE, NTOK], F32, kind="Internal").ap()

        filled = [sem(f"filled{b}") for b in range(8)]
        evacuated = [sem(f"evacuated{b}") for b in range(8)]
        loaded_x = sem("loaded_x")
        loaded_const = sem("loaded_const")
        loaded_a = sem("loaded_a")
        loaded_ctx = sem("loaded_ctx")
        loaded_c = sem("loaded_c")
        loaded_b = sem("loaded_b")
        dve_steps = sem("dve_steps")
        act_steps = sem("act_steps")
        var_ready = sem("var_ready")
        guess_ready = sem("guess_ready")
        nmr_ready = sem("nmr_ready")
        h_even = sem("h_even")
        h_odd = sem("h_odd")
        gate_ready = sem("gate_ready")
        ones_ready = sem("ones_ready")
        identb_ready = sem("identb_ready")
        kr_ready = sem("kr_ready")
        wabs_ready = sem("wabs_ready")
        wq8_ready = sem("wq8_ready")
        amin_ready = sem("amin_ready")
        aexp_ready = sem("aexp_ready")
        ao_ready = sem("ao_ready")
        simmax_ready = sem("simmax_ready")
        simexp_ready = sem("simexp_ready")
        xq_ready = sem("xq_ready")
        stored = sem("stored")
        x_final = sem("x_final")
        x_after_c = sem("x_after_c")
        x_after_d = sem("x_after_d")
        loaded_wqk = sem("loaded_wqk")
        loaded_wsv = sem("loaded_wsv")
        loaded_wg = sem("loaded_wg")
        loaded_wo = sem("loaded_wo")
        loaded_comp = sem("loaded_comp")
        loaded_T = sem("loaded_T")
        loaded_router = sem("loaded_router")
        loaded_fin = [sem(f"loaded_fin{e}") for e in range(2)]
        loaded_fout = [sem(f"loaded_fout{e}") for e in range(2)]
        loaded_bc = [sem(f"loaded_bc{e}") for e in range(2)]
        wo_scaled = sem("wo_scaled")
        em_exp = sem("em_exp")
        rc_ready = sem("rc_ready")
        ok_shifted = sem("ok_shifted")
        ok_exp = sem("ok_exp")
        p_ready = sem("p_ready")
        sumsq_ready = sem("sumsq_ready")
        rmsv_ready = sem("rmsv_ready")
        rms_guess = sem("rms_guess")
        emax_ready = sem("emax_ready")
        comb_ready = sem("comb_ready")
        shares_ready = sem("shares_ready")
        comb_stored = sem("comb_stored")
        yc_ready = sem("yc_ready")
        expert_out = [sem(f"expert_out{e}") for e in range(2)]

        block = ctx.enter_context(nc.Block())

        tile = lambda n: slice(n * P, (n + 1) * P)

        @block.sync
        def _(sp):
            xv = t["x"].rearrange("b (h p) d -> p (b h) d", p=P)
            sp.dma_start(X[:], xv).then_inc(loaded_x, 16)
            sp.dma_start(const[:], t["const"]).then_inc(loaded_const, 16)
            for n, w in enumerate(("w_q", "w_k", "w_v")):
                sp.dma_start(waraw[:, n, :], t["L0_attn_" + w]).then_inc(loaded_a, 16)
            sp.dma_start(woraw, t["L0_attn_w_o"].rearrange("(n p) d -> p n d", p=P)).then_inc(loaded_a, 16)
            sp.dma_start(MZ[:, 0:DA], t["L0_attn_M"]).then_inc(loaded_a, 16)
            sp.dma_start(MZ[:, DA:DA + 1], t["L0_attn_z"].rearrange("(d o) -> d o", o=1)).then_inc(loaded_a, 16)
            sp.dma_start(gg[:, 0:1], t["L0_attn_gate"].partition_broadcast(P)).then_inc(loaded_a, 16)
            sp.dma_start(ctxn, t["ctx_512"].rearrange("b (h p) d -> p (b h) d", p=P)).then_inc(loaded_ctx, 16)
            sp.dma_start(rope, t["rope"].rearrange("a (h p) d -> p a h d", p=P)).then_inc(loaded_ctx, 16)
            sp.dma_start(wkraw, t["L0_xattn_W_k"]).then_inc(loaded_ctx, 16)
            sp.dma_start(wkT[DC:DC + 1, :], t["L0_xattn_b_k"].unsqueeze(0)).then_inc(loaded_ctx, 16)
            sp.dma_start(wf, t["L0_ffn_weight"].rearrange("(n p) d -> p n d", p=P)).then_inc(loaded_c, 16)
            sp.dma_start(gamma, t["L0_xattn_ln_gamma"].partition_broadcast(P)).then_inc(loaded_b, 16)
            sp.dma_start(beta, t["L0_xattn_ln_beta"].partition_broadcast(P)).then_inc(loaded_b, 16)
            def after(semaphore, value):
                sp.wait_ge(semaphore, value)
                sp.wait_ge(loaded_const, 16)


            def load_wqk(i):
                for n, w in enumerate(("Wq", "Wk")):
                    v = t["L1_attn_" + w].rearrange("(c p) n -> p c n", p=P)
                    sp.dma_start(wqk[:, n, :, :], v[:, :, ds(i * 2 * M, 2 * M)]).then_inc(loaded_wqk, 16)

            def load_wsv(i):
                v = t["L1_attn_Ws"].rearrange("(c p) n -> p c n", p=P)
                sp.dma_start(wsv[:, :, 0:2 * M], v[:, :, ds(i * 2 * M, 2 * M)]).then_inc(loaded_wsv, 16)
                v = t["L1_attn_Wv"].rearrange("(c p) n -> p c n", p=P)
                sp.dma_start(wsv[:, :, 2 * M:], v[:, :, ds(i * 2 * DV, 2 * DV)]).then_inc(loaded_wsv, 16)

            def load_wg(i):
                v = t["L1_attn_Wg"].rearrange("(c p) n -> p c n", p=P)
                sp.dma_start(wg[:], v[:, :, ds(i * 2 * DV, 2 * DV)]).then_inc(loaded_wg, 16)

            def load_comp(i):
                two = lambda a: a[ds(i * 2, 2)]
                sp.dma_start(xwq, t["L1_xattn_Wq"].rearrange("(h k) d -> k h d", k=P)[:, ds(i * 2, 2), :]).then_inc(loaded_comp, 16)
                sp.dma_start(xkq, t["L1_xattn_w_kc_q"].rearrange("h k q -> k h q")[:, ds(i * 2, 2), :]).then_inc(loaded_comp, 16)
                qr = t["L1_xattn_W_qr"].rearrange("h (a q) r -> q h a r", q=QC)
                for a in range(2):
                    sp.dma_start(xqr[:, a], qr[:, ds(i * 2, 2), a, :]).then_inc(loaded_comp, 16)
                sp.dma_start(xkr, t["L1_xattn_W_kr"].rearrange("h c r -> c h r")[:, ds(i * 2, 2), :]).then_inc(loaded_comp, 16)
                sp.dma_start(xkv, t["L1_xattn_w_kc_kv"].rearrange("h k c -> k h c")[:, ds(i * 2, 2), :]).then_inc(loaded_comp, 16)
                sp.dma_start(xwo, t["L1_xattn_Wo"].rearrange("(a n) k -> n a k", n=P)[:, :, ds(i * 2 * P, 2 * P)])\
                    .then_inc(loaded_comp, 16)

            load_wqk(0)
            load_wsv(0)
            load_wg(0)
            sp.dma_start(gnorm[:], t["L1_attn_g_norm_weight"].unsqueeze(1)).then_inc(loaded_wo, 16)
            sp.wait_ge(x_after_c, 1)
            load_comp(0)
            sp.dma_start(WO, t["L1_attn_Wo"].rearrange("(h p) n -> p h n", p=P)).then_inc(loaded_wo, 16)
            with sp.Fori(0, PAIRS - 1) as i:
                after(filled[banks.bank("d.k1")], banks.after("d.k1", i))
                load_wqk(i + 1)
                after(filled[banks.bank("d.v3")], banks.after("d.v3", i))
                load_wsv(i + 1)
                after(filled[banks.bank("d.g3")], banks.after("d.g3", i))
                load_wg(i + 1)
                after(filled[banks.bank("d.V")], banks.after("d.V", i))
                load_comp(i + 1)
            sp.wait_ge(x_after_d, 1)
            sp.dma_start(wr, t["L1_ffn_wa"].rearrange("(c p) e -> p c e", p=P)).then_inc(loaded_router, 16)
            sp.dma_start(rev, t["rev"].partition_broadcast(P)).then_inc(loaded_router, 16)
            sp.dma_start(b2[0:E, :], t["L1_ffn_rb2"]).then_inc(loaded_router, 16)
            sp.dma_start(b2[E:NE, :], t["L1_ffn_sb2"]).then_inc(loaded_router, 16)

            def load_T(i):
                sp.dma_start(Tcur.rearrange("p c n -> p (c n)"),
                             Tall[:, ds(i, 1), :, :].rearrange("p i c n -> p (i c n)")).then_inc(loaded_T, 16)

            load_T(0)
            with sp.Fori(0, PAIRS - 1) as i:
                after(filled[banks.bank("e.q1")], banks.after("e.q1", i))
                load_T(i + 1)

            def load_in(e, g, u, gb, ub, row):
                for dst, w in ((fg, g), (fu, u)):
                    sp.dma_start(dst[:, e], w.rearrange("e (c p) f -> p (e c) f", p=P)[:, ds(row * C, C), :])\
                        .then_inc(loaded_fin[e], 16)
                for dst, w in ((fgb, gb), (fub, ub)):
                    sp.dma_start(dst[:, e], w.rearrange("e f -> f e")[:, ds(row, 1)]).then_inc(loaded_fin[e], 16)

            def load_out(e, o, row):
                sp.dma_start(fo[:, e], o.rearrange("e f n -> f e n")[:, ds(row, 1), :].rearrange("f e n -> f (e n)"))\
                    .then_inc(loaded_fout[e], 16)

            def load_bc(e, row):
                sp.dma_start(BC[:, e], comb_dram[ds(row, 1), :].rearrange("a n -> (a n)").partition_broadcast(P))\
                    .then_inc(loaded_bc[e], 16)

            routed = [t["L1_ffn_" + n] for n in ("rg", "rw1", "rgb", "rb1")]
            shared = [t["L1_ffn_" + n] for n in ("sg", "sw1", "sgb", "sb1")]
            for e in range(2):
                load_in(e, *routed, e)
                load_out(e, t["L1_ffn_rw2"], e)
            sp.wait_ge(comb_ready, 1)
            sp.dma_start(comb_dram, CBT).then_inc(comb_stored, 16)
            sp.wait_ge(comb_stored, 16)
            for e in range(2):
                load_bc(e, e)

            def next_experts(i, ins, out, row):
                for e in range(2):
                    after(yc_ready, 4 * i + 2 * e + 2)
                    load_in(e, *ins, row + e)
                    load_bc(e, row + e if ins is routed else E + e)
                for e in range(2):
                    after(expert_out[e], i + 1)
                    load_out(e, out, row + e)

            with sp.Fori(0, E // 2 - 1) as i:
                next_experts(i, routed, t["L1_ffn_rw2"], i * 2 + 2)
            next_experts(E // 2 - 1, shared, t["L1_ffn_sw2"], 0)
            ov = out.rearrange("b (h p) d -> p (b h) d", p=P)
            sp.wait_ge(x_final, 1)
            sp.dma_start(ov, X[:]).then_inc(stored, 16)
            sp.wait_ge(stored, 16)

        @block.tensor
        def _(pe):
            def fill(name, i=0):
                if not (banks.at[name][2] is None and banks.before(name) == 0):
                    pe.wait_ge(evacuated[banks.bank(name)], banks.before(name, i))
                return ps[:, banks.bank(name), :]

            def full(ins, name):
                ins.then_inc(filled[banks.bank(name)], 1)

            def evac(name, i=0):
                pe.wait_ge(evacuated[banks.bank(name)], banks.after(name, i))

            def transpose_h(b, dst, bf16=False):
                src, idn = (XQ, identb[:]) if bf16 else (HN, ident)
                for n in range(TB):
                    for c in range(C):
                        last = pe.transpose(dst[:, c * S + n * P:c * S + (n + 1) * P],
                                            src[:, b * TB + n, c * P:(c + 1) * P], idn)
                return last

            pe.wait_ge(loaded_const, 16)
            pe.wait_ge(loaded_a, 16 * 7)
            for half, name in enumerate(("w0", "w1")):
                pb = fill(name)
                for j in range(4):
                    n = half * 4 + j
                    src = waraw[:, n // 2, (n % 2) * P:(n % 2 + 1) * P] if n < 6 else woraw[:, n - 6, :]
                    last = pe.transpose(pb[:, j * P:(j + 1) * P], src, ident)
                full(last, name)
            pe.wait_ge(loaded_ctx, 16 * 4)
            for half, name in enumerate(("ctx0", "ctx1")):
                pb = fill(name)
                for j in range(4):
                    last = pe.transpose(pb[0:DC, j * P:(j + 1) * P], ctxn[:, half * 4 + j, :], ident)
                full(last, name)
            pb = fill("wk")
            full(pe.transpose(pb[0:DC, 0:DC], wkraw, ident[0:DC, 0:DC]), "wk")

            def layer_norm_T(k):
                for b in range(B):
                    pb = fill(f"ht{k}_{b}")
                    pe.wait_ge(h_even, k * B + b + 1)
                    pe.wait_ge(h_odd, k * B + b + 1)
                    full(transpose_h(b, pb), f"ht{k}_{b}")

            layer_norm_T(0)
            evac("w0")
            evac("w1")
            for b in range(B):
                evac(f"ht0_{b}")
            for n, q in enumerate("qk"):
                for half in range(2):
                    name = f"a{q}{half}"
                    pb = fill(name)
                    for c in range(C):
                        last = pe.matmul(pb, WT[:, 2 * n + c, :], HT[:, c, half * HALF:(half + 1) * HALF],
                                         start=(c == 0), stop=(c == C - 1))
                    full(last, name)
            for half in range(2):
                name = f"av{half}"
                pb = fill(name)
                for j in range(4):
                    n = half * 4 + j
                    for c in range(C):
                        last = pe.matmul(pb[:, j * P:(j + 1) * P], HT[:, c, tile(n)], WT[:, 4 + c, :],
                                         start=(c == 0), stop=(c == C - 1))
                full(last, name)
            evac("ctx0")
            evac("ctx1")
            evac("wk")
            pe.wait_ge(ones_ready, 2)
            for half in range(2):
                name = f"kvT{half}"
                pb = fill(name)
                full(pe.matmul(pb[0:DC, :], wkT, ctxT[:, half * HALF:(half + 1) * HALF], start=True, stop=True), name)
            pb = fill("kv")
            for n in range(NT):
                last = pe.matmul(pb[:, n * DC:(n + 1) * DC], ctxT[:, tile(n)], wkT, start=True, stop=True)
            full(last, "kv")
            pe.wait_ge(wabs_ready, 1)
            pb = fill("wsum")
            full(pe.matmul(pb[:, 0:1], ones, col[:, 0:1], start=True, stop=True), "wsum")
            pe.wait_ge(wq8_ready, 1)
            pe.wait_ge(identb_ready, 1)
            pb = fill("wqT").bitcast(BF16)
            for c in range(C):
                for o in range(2):
                    last = pe.transpose(pb[:, c * D + o * P:c * D + (o + 1) * P], wq8[:, o, c * P:(c + 1) * P],
                                        identb[:])
            full(last, "wqT")

            def scores(b):
                pb = fill(f"at{b}")
                k0, k1 = tile(b * TB), tile(b * TB + 1)
                pe.matmul(pb[:, 0:2 * P], SK[:, k0], SQ[:, b * S:(b + 1) * S], start=True, stop=True)
                full(pe.matmul(pb[:, 2 * P:3 * P], SK[:, k1], SQ[:, k1], start=True, stop=True), f"at{b}")

            def memory_and_local(n):
                pb = fill(f"ml{n}")
                evac(f"at{n // TB}")
                w = DA + 1
                pe.matmul(pb[:, 0:w], SQ[:, tile(n)], MZ, start=True, stop=True)
                a = AT[:, (n // TB) % 2, :]
                if n % TB == 0:
                    last = pe.matmul(pb[:, w:2 * w], a[:, 0:P], VV[:, n, :], start=True, stop=True)
                else:
                    pe.matmul(pb[:, w:2 * w], a[:, P:2 * P], VV[:, n - 1, :], start=True, stop=False)
                    last = pe.matmul(pb[:, w:2 * w], a[:, 2 * P:3 * P], VV[:, n, :], start=False, stop=True)
                full(last, f"ml{n}")

            def output_T(b):
                pb = fill(f"ao{b}")
                evac(f"ml{b * TB + 1}")
                for n in range(TB):
                    last = pe.transpose(pb[:, n * P:(n + 1) * P], AO[:, b * TB + n, :], ident)
                full(last, f"ao{b}")

            def project_out(b):
                pb = fill(f"ax{b}")
                evac(f"ao{b}")
                for n in range(TB):
                    last = pe.matmul(pb[:, n * D:(n + 1) * D], AOT[:, tile(b * TB + n)],
                                     WT[:, 6:8, :].rearrange("p a b -> p (a b)"), start=True, stop=True)
                full(last, f"ax{b}")

            for name in ("aq0", "aq1", "ak0", "ak1", "av0", "av1"):
                evac(name)
            pe.wait_ge(ones_ready, 2)
            step_of = {"at": scores, "ml": memory_and_local, "ao": output_T, "ax": project_out}
            for name in A_ORDER:
                step_of[name[:2]](int(name[2:]))

            pe.wait_ge(kr_ready, 1)
            for half in range(2):
                name = f"kr{half}"
                pb = fill(name)
                for j in range(4):
                    last = pe.transpose(pb[:, j * P:(j + 1) * P],
                                        kr[:, half * 4 + j, :, :].rearrange("p a b -> p (a b)"), ident)
                full(last, name)

            layer_norm_T(1)
            for b in range(B):
                pb = fill(f"bo{b}")
                evac(f"ht1_{b}")
                for c in range(C):
                    last = pe.matmul(pb[0:DC, 0:S], kvn[:, b * TB + c, :], HT[:, c, b * S:(b + 1) * S],
                                     start=(c == 0), stop=(c == C - 1))
                full(last, f"bo{b}")
            for b in range(B):
                pb = fill(f"bs{b}")
                evac(f"bo{b}")
                for n in range(TB):
                    last = pe.matmul(pb[:, n * S:(n + 1) * S], BO[:, tile(b * TB + n)], kvT[:, b * S:(b + 1) * S],
                                     start=True, stop=True)
                full(last, f"bs{b}")

            evac("wqT")
            for b in range(B):
                pb = fill(f"ht2_{b}").bitcast(BF16)
                pe.wait_ge(xq_ready, 1)
                full(transpose_h(b, pb, bf16=True), f"ht2_{b}")
            for b in range(B):
                pb = fill(f"cy{b}")
                evac(f"ht2_{b}")
                for n in range(TB):
                    for c in range(C):
                        last = pe.matmul(pb[:, n * D:(n + 1) * D], XQT[:, c, tile(b * TB + n)], WQT[:, c, :],
                                         start=(c == 0), stop=(c == C - 1))
                full(last, f"cy{b}")
            layer_norm_T(3)
            for b in range(B):
                evac(f"ht3_{b}")
            with pe.Fori(0, PAIRS) as i:
                def project_T(name, w):
                    for half in range(2):
                        pb = fill(f"{name}{half}", i)
                        for c in range(C):
                            last = pe.matmul(pb, w[:, c, :], HT[:, c, half * HALF:(half + 1) * HALF],
                                             start=(c == 0), stop=(c == C - 1))
                        full(last, f"{name}{half}")

                def project(name, count, w, width):
                    per = 512 // width
                    for j in range(count):
                        pb = fill(f"{name}{j}", i)
                        for m in range(per):
                            for c in range(C):
                                last = pe.matmul(pb[:, m * width:(m + 1) * width], HT[:, c, tile(j * per + m)], w[:, c, :],
                                                 start=(c == 0), stop=(c == C - 1))
                        full(last, f"{name}{j}")

                pe.wait_ge(loaded_wsv, i * 32 + 32)
                project("d.s", 2, wsv[:, :, 0:2 * M], 2 * M)
                pe.wait_ge(loaded_wqk, i * 32 + 32)
                project_T("d.q", wqk[:, 0])
                project_T("d.k", wqk[:, 1])
                project("d.v", 4, wsv[:, :, 2 * M:], 2 * DV)
                for g in range(2):
                    pe.wait_ge(em_exp, i * 2 + (g + 1))
                    pb = fill(f"d.cu{g}", i)
                    w = 2 * M
                    pe.matmul(pb, causal, EM[:, 4 * g:4 * g + 4, :].rearrange("p a b -> p (a b)"), start=True, stop=True)
                    odd = pb.rearrange("p (a b) -> p a b", a=4)[:, 1:4:2, :]
                    full(pe.matmul(odd, ones, EM[:, 4 * g:4 * g + 4:2, :], start=False, stop=True, skip_group_check=True),
                         f"d.cu{g}")
                for g in range(2):
                    pb = fill(f"d.et{g}", i)
                    for j in range(4):
                        last = pe.transpose(pb[:, j * P:(j + 1) * P], EM[:, 4 * g + j, :], ident)
                    full(last, f"d.et{g}")
                pe.wait_ge(loaded_wg, i * 16 + 16)
                project("d.g", 4, wg[:], 2 * DV)

                pe.wait_ge(loaded_comp, i * (16 * 7) + 16 * 7)
                pb = fill("d.wot", i)
                for h in range(2):
                    for a in range(2):
                        last = pe.transpose(pb[:, h * D + a * P:h * D + (a + 1) * P], xwo[:, a, h * P:(h + 1) * P], ident)
                full(last, "d.wot")

                def weights_u(h):
                    pb = fill(f"d.u{h}", i)
                    for a in range(2):
                        last = pe.matmul(pb[0:QC, a * D:(a + 1) * D], xkq[:, h, a * QC:(a + 1) * QC], xwq[:, h, :],
                                         start=True, stop=True)
                    full(last, f"d.u{h}")

                def weights_v():
                    evac("d.u0", i)
                    evac("d.u1", i)
                    pb = fill("d.V", i)
                    for h in range(2):
                        for a in range(2):
                            last = pe.matmul(pb[h * R:(h + 1) * R, 0:D], xqr[:, a, h, :], U[:, h, a, :],
                                             start=(a == 0), stop=(a == 1))
                    full(last, "d.V")

                def weights_t():
                    evac("d.V", i)
                    evac("d.w2", i)
                    for h in range(2):
                        pb = fill(f"d.T{h}", i)
                        for c in range(C):
                            last = pe.matmul(pb[:, c * DC:(c + 1) * DC], VE[h * R:(h + 1) * R, c * P:(c + 1) * P],
                                             KRT[h * R:(h + 1) * R, :], start=True, stop=True)
                        full(last, f"d.T{h}")

                def weights_2():
                    evac("d.wot", i)
                    pb = fill("d.w2", i)
                    for h in range(2):
                        pe.matmul(pb[h * DC:(h + 1) * DC, 0:D], xkv[:, h, :], WOTe[:, h, :], start=True, stop=True)
                    full(pe.transpose(pb[:, D:D + DC], xkr.rearrange("p a b -> p (a b)"), ident[0:DC, 0:DC]), "d.w2")

                def pairwise(name, j, left, right):
                    b, h = j // 2, j % 2
                    rows = slice(h * M, (h + 1) * M)
                    pb = fill(f"d.{name}{j}", i)
                    pe.matmul(pb[:, 0:2 * P], left[rows, tile(b * TB)], right[rows, b * S:(b + 1) * S], start=True, stop=True)
                    full(pe.matmul(pb[:, 2 * P:3 * P], left[rows, tile(b * TB + 1)], right[rows, tile(b * TB + 1)],
                                   start=True, stop=True), f"d.{name}{j}")

                def apply(pb, at_col, a, n, rhs):
                    w = rhs(n).shape[-1]
                    dst = pb[:, at_col:at_col + w]
                    if n % TB == 0:
                        return pe.matmul(dst, a[:, 0:P], rhs(n), start=True, stop=True)
                    pe.matmul(dst, a[:, P:2 * P], rhs(n - 1), start=True, stop=False)
                    return pe.matmul(dst, a[:, 2 * P:3 * P], rhs(n), start=False, stop=True)

                def slots(g):
                    pb = fill(f"d.ok{g}", i)
                    for j in range(4):
                        evac(f"d.at{4 * g + j}", i)
                    for n in range(4):
                        for h in range(2):
                            last = apply(pb, n * 2 * M + h * M, ATd[:, (n // TB) * 2 + h, :], 4 * g + n,
                                         lambda m: EM[:, m, h * M:(h + 1) * M])
                    full(last, f"d.ok{g}")

                def slots_T(g):
                    pb = fill(f"d.pt{g}", i)
                    pe.wait_ge(p_ready, i * 2 + (g + 1))
                    for j in range(4):
                        last = pe.transpose(pb[:, j * P:(j + 1) * P], PM[:, 4 * g + j, :], ident)
                    full(last, f"d.pt{g}")

                def values(b):
                    pb = fill(f"d.o{b}", i)
                    evac(f"d.bt{2 * b}", i)
                    evac(f"d.bt{2 * b + 1}", i)
                    for n in range(TB):
                        for h in range(2):
                            last = apply(pb, (n * 2 + h) * DV, BTd[:, (b % 2) * 2 + h, :], b * TB + n,
                                         lambda m: VD[:, m, h * DV:(h + 1) * DV])
                    full(last, f"d.o{b}")

                def outputs_T(b):
                    pb = fill(f"d.ot{b}", i)
                    evac(f"d.o{b}", i)
                    for h in range(2):
                        for n in range(TB):
                            last = pe.transpose(pb[:, h * S + n * P:h * S + (n + 1) * P],
                                                OD[:, b * TB + n, h * DV:(h + 1) * DV], ident)
                    full(last, f"d.ot{b}")

                for name in ("q0", "q1", "k0", "k1", "v0", "v1", "v2", "v3", "et0", "et1"):
                    evac("d." + name, i)
                for g in range(2):
                    for j in range(4 * g, 4 * g + 4):
                        pairwise("at", j, kT, qT)
                    weights_u(g)
                    slots(g)
                for g in range(2):
                    slots_T(g)
                    if g == 0:
                        weights_2()
                    evac(f"d.pt{g}", i)
                    for j in range(4 * g, 4 * g + 4):
                        pairwise("bt", j, ET, PT)
                    if g == 0:
                        values(0)
                        values(1)
                    else:
                        outputs_T(0)
                        outputs_T(1)
                        values(2)
                        values(3)
                        weights_v()
                        weights_t()
                        outputs_T(2)
                        outputs_T(3)

            pe.wait_ge(wo_scaled, 1)
            for b in range(B):
                pb = fill(f"dx{b}")
                if b == 0:
                    for j in range(B):
                        evac(f"d.ot{j}", PAIRS - 1)
                for n in range(TB):
                    for h in range(H):
                        last = pe.matmul(pb[:, n * D:(n + 1) * D], OT[:, h // 2, h % 2, tile(b * TB + n)], WO[:, h, :],
                                         start=(h == 0), stop=(h == H - 1))
                full(last, f"dx{b}")

            layer_norm_T(4)
            for b in range(B):
                evac(f"ht4_{b}")
            evac("kr0")
            evac("kr1")
            with pe.Fori(0, PAIRS) as i:
                pe.wait_ge(loaded_T, i * 16 + 16)
                for half in range(2):
                    pb = fill(f"e.q{half}", i)
                    for c in range(C):
                        last = pe.matmul(pb, Tcur[:, c, :], HT[:, c, half * HALF:(half + 1) * HALF],
                                         start=(c == 0), stop=(c == C - 1))
                    full(last, f"e.q{half}")

                def e_scores(b, h):
                    name = f"e.sc{b}{h}"
                    pb = fill(name, i)
                    if h == 0 and b % 2 == 0:
                        evac(f"e.q{b // 2}", i)
                    rows = slice(h * DC, (h + 1) * DC)
                    for n in range(TB):
                        last = pe.matmul(pb[:, n * S:(n + 1) * S], QE[rows, tile(b * TB + n)], krT[rows, b * S:(b + 1) * S],
                                         start=True, stop=True)
                    full(last, name)

                def e_probs_T(b, h):
                    name = f"e.pt{b}{h}"
                    pb = fill(name, i)
                    evac(f"e.sc{b}{h}", i)
                    for c in range(TB):
                        for n in range(TB):
                            last = pe.transpose(pb[:, c * S + n * P:c * S + (n + 1) * P],
                                                PX[:, b % 2, h, n, c * P:(c + 1) * P], ident)
                    full(last, name)

                def e_context(b):
                    name = f"e.cx{b}"
                    pb = fill(name, i)
                    evac(f"e.pt{b}0", i)
                    evac(f"e.pt{b}1", i)
                    for n in range(TB):
                        for h in range(2):
                            for c in range(TB):
                                last = pe.matmul(pb[:, (n * 2 + h) * DC:(n * 2 + h + 1) * DC],
                                                 PXT[:, b % 2, h, c, n * P:(n + 1) * P], kr[:, b * TB + c, 0, :],
                                                 start=(c == 0), stop=(c == TB - 1))
                    full(last, name)

                def e_context_T(b):
                    name = f"e.ct{b}"
                    pb = fill(name, i)
                    evac(f"e.cx{b}", i)
                    for n in range(TB):
                        last = pe.transpose(pb[:, n * P:(n + 1) * P], CX[:, b * TB + n, :, :].rearrange("p a b -> p (a b)"), ident)
                    full(last, name)

                e_step = {"sc": e_scores, "pt": e_probs_T, "cx": e_context, "ct": e_context_T}
                for name in E_BODY[2:]:
                    e_step[name[2:4]](*(int(x) for x in name[4:]))
            for b in range(B):
                pb = fill(f"ex{b}")
                if b == 0:
                    for j in range(B):
                        evac(f"e.ct{j}", PAIRS - 1)
                for n in range(TB):
                    for p in range(PAIRS):
                        last = pe.matmul(pb[:, n * D:(n + 1) * D], CT[:, p, tile(b * TB + n)], W2[:, p, :],
                                         start=(p == 0), stop=(p == PAIRS - 1))
                full(last, f"ex{b}")

            layer_norm_T(5)
            pe.wait_ge(loaded_router, 16 * 4)
            pb = fill("lg")
            for n in range(NT):
                evac(f"ht5_{n // TB}")
                for c in range(C):
                    last = pe.matmul(pb[:, n * E:(n + 1) * E], HT[:, c, tile(n)], wr[:, c, :], start=(c == 0), stop=(c == C - 1))
            full(last, "lg")

            pe.wait_ge(shares_ready, 1)
            for half in range(2):
                pb = fill(f"cb{half}")
                for j in range(4):
                    last = pe.transpose(pb[0:NE, j * P:(j + 1) * P], CB[:, half * 4 + j, :], ident)
                full(last, f"cb{half}")
            evac("cb0")
            evac("cb1")
            for b in range(B):
                pb = fill(f"acc{b}")
                for n in range(TB):
                    last = pe.matmul(pb[:, n * D:(n + 1) * D], CBT[:, tile(b * TB + n)], b2, start=(n == 0), stop=True,
                                     skip_group_check=True)
            with pe.Fori(0, F_TRIPS) as i:
                for e in range(2):
                    pe.wait_ge(loaded_fin[e], i * 64 + 64)
                    for x, w in (("g", fg), ("u", fu)):
                        for half in range(2):
                            name = f"f.{x}{half}{e}"
                            pb = fill(name, i)
                            for c in range(C):
                                last = pe.matmul(pb, w[:, e, c, :], HT[:, c, half * HALF:(half + 1) * HALF],
                                                 start=(c == 0), stop=(c == C - 1))
                            full(last, name)
                for e in range(2):
                    pe.wait_ge(loaded_fout[e], i * 16 + 16)
                    for half in range(2):
                        pe.wait_ge(yc_ready, i * 4 + (2 * e + half + 1))
                        for n in range(4 * half, 4 * half + 4):
                            b = n // TB
                            last = pe.matmul(ps[:, banks.bank(f"acc{b}"), (n % TB) * D:(n % TB + 1) * D], YC[:, e, tile(n)],
                                             fo[:, e, :], start=False, stop=True, skip_group_check=True)
                    last.then_inc(expert_out[e], 1)

        @block.scalar
        def _(act):
            own = Steps(act, act_steps)

            def full(name, i=0):
                act.wait_ge(filled[banks.bank(name)], banks.after(name, i))
                return ps[:, banks.bank(name), :]

            def evac(ins, name, i=0):
                own.mark(ins, evacuated[banks.bank(name)], banks.after(name, i))

            def inverse_root(rank):
                act.wait_ge(var_ready, rank + 1)
                own.step(act.activation(nt[:], ve[:], ACT.Ln))
                own.settle()
                own.mark(act.activation(guess[:], nt[:], ACT.Exp, scale=-0.5), guess_ready, rank + 1)

            def normalize_odd(k):
                act.wait_ge(nmr_ready, k + 1)
                for b in range(B):
                    n = 2 * b + 1
                    own.mark(act.activation(HN[:, n, :], X[:, n, :], ACT.Identity, bias=nmr[:, n:n + 1],
                                              scale=rstd[:, n:n + 1]), h_odd, k * B + b + 1)

            def evac_ht(k, dst, odd_only=True, bf16=False):
                for b in range(1, B, 2) if odd_only else range(B):
                    pb = full(f"ht{k}_{b}")
                    pb = pb.bitcast(BF16) if bf16 else pb
                    src = pb[:, 0:C * S].rearrange("p (c s) -> p c s", c=C)
                    evac(act.copy(dst[:, :, b * S:(b + 1) * S], src), f"ht{k}_{b}")

            act.wait_ge(loaded_a, 16 * 7)
            own.mark(act.activation(gg[:, 0:1], gg[:, 0:1], ACT.Sigmoid), gate_ready, 1)
            inverse_root(0)
            for half, name in enumerate(("w0", "w1")):
                evac(act.copy(WT[:, half * 4:half * 4 + 4, :].rearrange("p a b -> p (a b)"), full(name)), name)
            for half, name in enumerate(("ctx0", "ctx1")):
                evac(act.copy(ctxT[0:DC, half * HALF:(half + 1) * HALF], full(name)[0:DC, :]), name)
            evac(act.copy(wkT[0:DC, :], full("wk")[0:DC, 0:DC]), "wk")
            normalize_odd(0)
            evac_ht(0, HT)
            for n in range(4):
                act.wait_ge(amin_ready, n + 1)
                own.mark(act.activation(amin[:, n, :], amin[:, n, :], ACT.Exp), aexp_ready, n + 1)
            for half in range(2):
                evac(act.copy(VV[:, half * 4:half * 4 + 4, 0:DA],
                              full(f"av{half}").rearrange("p (n d) -> p n d", n=4)), f"av{half}")
            for half in range(2):
                evac(act.copy(kvT[:, half * HALF:(half + 1) * HALF], full(f"kvT{half}")[0:DC, :]), f"kvT{half}")
            evac(act.copy(kvn.rearrange("p a b -> p (a b)"), full("kv")), "kv")
            evac(act.copy(WQT.rearrange("p a b -> p (a b)"), full("wqT").bitcast(BF16)[:, 0:C * D]), "wqT")
            for b in range(B):
                evac(act.copy(AOT[:, b * S:(b + 1) * S], full(f"ao{b}")[:, 0:S]), f"ao{b}")
            for half in range(2):
                evac(act.copy(krT[:, half * HALF:(half + 1) * HALF], full(f"kr{half}")), f"kr{half}")

            inverse_root(1)
            normalize_odd(1)
            evac_ht(1, HT)
            for b in range(B):
                evac(act.mul(BO[:, b * S:(b + 1) * S], full(f"bo{b}")[0:DC, 0:S], D ** -0.5), f"bo{b}")
            inverse_root(2)
            for n in range(NT):
                act.wait_ge(simmax_ready, n // TB + 1)
                own.mark(act.activation(SIM[:, n, :], SIM[:, n, :], ACT.Exp, bias=col[:, NT + n:NT + n + 1],
                                          accum_out=col[:, 2 * NT + n:2 * NT + n + 1]), simexp_ready, n + 1)
            inverse_root(3)
            normalize_odd(2)
            evac_ht(2, XQT, odd_only=False, bf16=True)
            inverse_root(4)
            normalize_odd(3)
            evac_ht(3, HT)
            with act.Fori(0, PAIRS) as i:
                own.enter(i, 1 + 4 * 4)
                act.preload_act_table_set("natural_log_exp_and_others")
                for g in range(2):
                    act.wait_ge(evacuated[banks.bank(f"d.s{g}")], banks.after(f"d.s{g}", i))
                    em = EM[:, 4 * g:4 * g + 4, :]
                    own.mark(act.activation(em, em, ACT.Exp), em_exp, i * 2 + (g + 1))
                for half in range(2):
                    evac(act.copy(qT[:, half * HALF:(half + 1) * HALF], full(f"d.q{half}", i)), f"d.q{half}", i)
                for b in range(B):
                    evac(act.copy(VD[:, b * TB:(b + 1) * TB, :].rearrange("p a b -> p (a b)"), full(f"d.v{b}", i)), f"d.v{b}", i)
                for g in range(2):
                    rc = RC[:, 4 * g:4 * g + 4, :].rearrange("p a b -> p (a b)")
                    evac(act.activation(rc, full(f"d.cu{g}", i), ACT.Ln), f"d.cu{g}", i)
                own.settle()
                for g in range(2):
                    rc = RC[:, 4 * g:4 * g + 4, :].rearrange("p a b -> p (a b)")
                    own.mark(act.activation(rc, rc, ACT.Exp, scale=-1.0), rc_ready, i * 2 + (g + 1))
                for b in range(B):
                    sg = SG[:, b * TB:(b + 1) * TB, :].rearrange("p a b -> p (a b)")
                    evac(act.activation(sg, full(f"d.g{b}", i), ACT.Silu), f"d.g{b}", i)
                act.preload_act_table_set("natural_log_exp_and_others")
                evac(act.copy(WOTe.rearrange("p a b -> p (a b)"), full("d.wot", i)), "d.wot", i)

                def exp_slots(g):
                    act.wait_ge(ok_shifted, i * 2 + (g + 1))
                    pm = PM[:, 4 * g:4 * g + 4, :]
                    own.mark(act.activation(pm, pm, ACT.Exp, scale=M ** -0.5), ok_exp, i * 2 + (g + 1))

                def root_mean_squares(b):
                    pb = full(f"d.o{b}", i)
                    for j in range(4):
                        k = b * 4 + j
                        ins = act.activation(JUNK[:, j], pb[:, j * DV:(j + 1) * DV], ACT.Square, accum_out=sumsq[:, k:k + 1])
                        if j == 3:
                            own.mark(ins, sumsq_ready, i * B + (b + 1))
                        else:
                            own.step(ins)
                    act.wait_ge(rmsv_ready, i * B + (b + 1))
                    sl = slice(4 * b, 4 * b + 4)
                    own.step(act.activation(rmsl[:, sl], rmsv[:, sl], ACT.Ln))
                    own.settle()
                    own.mark(act.activation(rmsl[:, sl], rmsl[:, sl], ACT.Exp, scale=-0.5), rms_guess, i * B + (b + 1))

                def outputs_T(b):
                    dst = OT[:, ds(i, 1), :, b * S:(b + 1) * S].rearrange("p i h s -> p (i h) s")
                    evac(act.copy(dst, full(f"d.ot{b}", i).rearrange("p (h s) -> p h s", h=2)), f"d.ot{b}", i)

                evac(act.copy(U[:, 0, :, :].rearrange("p a b -> p (a b)"), full("d.u0", i)[0:QC, :]), "d.u0", i)
                exp_slots(0)
                evac(act.copy(U[:, 1, :, :].rearrange("p a b -> p (a b)"), full("d.u1", i)[0:QC, :]), "d.u1", i)
                evac(act.copy(PT[:, 0:HALF], full("d.pt0", i)), "d.pt0", i)
                exp_slots(1)
                w2 = W2[:, ds(i, 1), :].rearrange("p i n -> p (i n)")
                own.step(act.copy(w2, full("d.w2", i)[:, 0:D]))
                evac(act.copy(KRT, full("d.w2", i)[:, D:D + DC]), "d.w2", i)
                root_mean_squares(0)
                root_mean_squares(1)
                evac(act.copy(PT[:, HALF:], full("d.pt1", i)), "d.pt1", i)
                outputs_T(0)
                outputs_T(1)
                root_mean_squares(2)
                root_mean_squares(3)
                evac(act.copy(VE, full("d.V", i)[:, 0:D]), "d.V", i)
                for h in range(2):
                    dst = Tall[:, ds(i, 1), :, h * DC:(h + 1) * DC].rearrange("p i c n -> p (i c) n")
                    src = full(f"d.T{h}", i)[:, 0:C * DC].rearrange("p (c n) -> p c n", c=C)
                    evac(act.copy(dst, src), f"d.T{h}", i)
                outputs_T(2)
                outputs_T(3)
                own.leave(PAIRS)

            inverse_root(5)
            normalize_odd(4)
            evac_ht(4, HT)
            with act.Fori(0, PAIRS) as i:
                evac(act.copy(QE[:, 0:HALF], full("e.q0", i)), "e.q0", i)

                def e_exp(b, h):
                    pb = full(f"e.sc{b}{h}", i)
                    act.wait_ge(emax_ready, i * 8 + (2 * b + h + 1))
                    for n in range(TB):
                        k = b * TB + n
                        ins = act.activation(PX[:, b % 2, h, n, :], pb[:, n * S:(n + 1) * S], ACT.Exp, bias=nmx[:, k, h:h + 1],
                                             accum_out=esum[:, k, h:h + 1])
                        if n == TB - 1:
                            evac(ins, f"e.sc{b}{h}", i)
                        else:
                            own.step(ins)

                own.enter(i, 8)
                for name in E_BODY[2:]:
                    kind, at_ = name[2:4], name[4:]
                    if kind == "sc":
                        e_exp(int(at_[0]), int(at_[1]))
                    elif kind == "pt" and at_[1] == "0":
                        b = int(at_[0])
                        evac(act.copy(PXT[:, b % 2, 0, :, :].rearrange("p a b -> p (a b)"), full(name, i)), name, i)
                    elif kind == "ct":
                        b = int(at_)
                        dst = CT[:, ds(i, 1), b * S:(b + 1) * S].rearrange("p i s -> p (i s)")
                        evac(act.copy(dst, full(name, i)[:, 0:S]), name, i)
                own.leave(PAIRS)

            inverse_root(6)
            normalize_odd(5)
            evac_ht(5, HT)
            evac(act.activation(AFF.rearrange("p a b -> p (a b)"), full("lg")[:, 0:NT * E], ACT.Sigmoid), "lg")
            with act.Fori(0, F_TRIPS) as i:
                for e in range(2):
                    act.wait_ge(loaded_fin[e], i * 64 + 64)
                    for half in range(2):
                        name = f"f.g{half}{e}"
                        evac(act.activation(Y[:, e, half * HALF:(half + 1) * HALF], full(name, i), ACT.Gelu,
                                            bias=fgb[:, e]), name, i)

        @block.gpsimd
        def _(pool):
            pool.memset(ctxT[DC:DC + 1, :], 1.0).then_inc(ones_ready, 1)
            pool.wait_ge(ones_ready, 1)
            pool.memset(VV[:, :, DA:DA + 1], 1.0).then_inc(ones_ready, 1)


        @block.vector
        def _(dve):
            own = Steps(dve, dve_steps)

            def full(name, i=0):
                dve.wait_ge(filled[banks.bank(name)], banks.after(name, i))
                return ps[:, banks.bank(name), :]

            def evac(ins, name, i=0):
                own.mark(ins, evacuated[banks.bank(name)], banks.after(name, i))

            def inverse_root(rank, eps):
                own.settle()
                own.mark(dve.tensor_scalar(ve[:], mv[:, :, 1], eps, None, ALU.add), var_ready, rank + 1)
                dve.wait_ge(guess_ready, rank + 1)
                own.step(dve.tensor_tensor(rstd[:], guess[:], guess[:], ALU.mult))
                own.settle()
                own.step(dve.tensor_tensor(rstd[:], rstd[:], ve[:], ALU.mult))
                own.settle()
                own.step(dve.tensor_scalar(rstd[:], rstd[:], -0.5, 1.5, ALU.mult, ALU.add))
                own.settle()
                own.step(dve.tensor_tensor(rstd[:], rstd[:], guess[:], ALU.mult))
                own.settle()

            def layer_norm(k, rank):
                for n in range(NT):
                    own.step(dve.bn_stats(st6[:, n, :], X[:, n, :]))
                own.settle()
                for n in range(NT):
                    own.step(dve.bn_aggr(mv[:, n, :], st6[:, n, :]))
                inverse_root(rank, EPS_LN)
                own.mark(dve.scalar_tensor_tensor(out=nmr[:], in0=mv[:, :, 0], scalar=-1.0, in1=rstd[:],
                                                    op0=ALU.mult, op1=ALU.mult), nmr_ready, k + 1)
                own.settle()
                for b in range(B):
                    n = 2 * b
                    own.mark(dve.tensor_scalar(HN[:, n, :], X[:, n, :], rstd[:, n:n + 1], nmr[:, n:n + 1],
                                                 ALU.mult, ALU.add), h_even, k * B + b + 1)

            def evac_ht(k, dst):
                for b in range(0, B, 2):
                    src = full(f"ht{k}_{b}")[:, 0:C * S].rearrange("p (c s) -> p c s", c=C)
                    evac(dve.tensor_copy(dst[:, :, b * S:(b + 1) * S], src), f"ht{k}_{b}")

            dve.wait_ge(loaded_x, 16)
            layer_norm(0, 0)
            dve.wait_ge(loaded_const, 16)
            own.mark(dve.tensor_copy(identb[:], ident), identb_ready, 1)
            dve.wait_ge(loaded_ctx, 16 * 4)
            hd = DC // 2
            cv = ctxn.rearrange("p (b n) d -> p b n d", b=B)
            rv = ropet.rearrange("p (b n) d -> p b n d", b=B)
            for n in range(TB):
                for lo, hi in ((0, hd), (hd, DC)):
                    src = (lo + hd) % DC
                    own.step(dve.tensor_tensor(rv[:, :, n, lo:hi], cv[:, :, n, src:src + hd],
                                               rope[:, 1:2, n, lo:hi].to_broadcast([P, B, hd]), ALU.mult))
            krv = kr[:].rearrange("p (b n) a d -> p b n a d", b=B)
            for n in range(TB):
                own.step(dve.tensor_tensor(krv[:, :, n, 0, :], cv[:, :, n, :],
                                           rope[:, 0:1, n, :].to_broadcast([P, B, DC]), ALU.mult))
            own.settle()
            own.step(dve.tensor_tensor(kr[:, :, 0, :], kr[:, :, 0, :], ropet, ALU.add))
            own.settle()
            own.mark(dve.tensor_copy(kr[:, :, 1, :], kr[:, :, 0, :]), kr_ready, 1)
            evac_ht(0, HT)
            for n in range(4):
                name = f"a{'qk'[n // 2]}{n % 2}"
                own.mark(dve.tensor_scalar(amin[:, n, :], full(name), 0.0, None, ALU.min), amin_ready, n + 1)
            for n in range(4):
                name = f"a{'qk'[n // 2]}{n % 2}"
                dve.wait_ge(aexp_ready, n + 1)
                dst = (SQ, SK)[n // 2][:, (n % 2) * HALF:(n % 2 + 1) * HALF]
                evac(dve.scalar_tensor_tensor(out=dst, in0=full(name), scalar=0.0, in1=amin[:, n, :],
                                              op0=ALU.max, op1=ALU.add), name)
            dve.wait_ge(loaded_c, 16)
            own.mark(dve.tensor_reduce(col[:, 0:1], wf, AX.XY, ALU.add, apply_absolute_value=True), wabs_ready, 1)
            evac(dve.tensor_scalar(col[:, 1:2], full("wsum")[:, 0:1], 1.0 / (D * D), 1e-6, ALU.mult, ALU.max), "wsum")
            own.settle()
            own.step(dve.reciprocal(col[:, 2:3], col[:, 1:2]))
            own.settle()
            own.step(dve.tensor_scalar(wf, wf, col[:, 2:3], MAGIC, ALU.mult, ALU.add))
            own.settle()
            own.step(dve.tensor_scalar(wf, wf, -MAGIC, 1.0, ALU.add, ALU.min))
            own.settle()
            own.mark(dve.tensor_scalar(wq8, wf, -1.0, None, ALU.max), wq8_ready, 1)
            own.step(dve.tensor_scalar(col[:, 3:4], col[:, 1:2], 1.0 / 127.0, None, ALU.mult))
            dve.wait_ge(gate_ready, 1)
            own.step(dve.tensor_scalar(gg[:, 1:2], gg[:, 0:1], -1.0, 1.0, ALU.mult, ALU.add))
            own.settle()

            def mask_scores(b):
                evac(dve.tensor_tensor(AT[:, b % 2, :], full(f"at{b}")[:, 0:3 * P], mask3, ALU.mult), f"at{b}")

            def gated_output(n):
                pb = full(f"ml{n}")
                w = DA + 1
                den = col[:, 8 + 2 * n:10 + 2 * n]
                own.step(dve.tensor_scalar(den, pb[:, DA:2 * w:w], EPS_A, None, ALU.add))
                own.settle()
                own.step(dve.reciprocal(den, den))
                own.settle()
                own.step(dve.tensor_tensor(den, den, gg[:], ALU.mult))
                own.settle()
                own.step(dve.tensor_scalar(AO[:, n, :], pb[:, 0:DA], den[:, 0:1], None, ALU.mult))
                own.settle()
                evac(dve.scalar_tensor_tensor(out=AO[:, n, :], in0=pb[:, w:w + DA], scalar=den[:, 1:2],
                                              in1=AO[:, n, :], op0=ALU.mult, op1=ALU.add), f"ml{n}")

            def add_to_x(name, b):
                xb = X[:, b * TB:(b + 1) * TB, :].rearrange("p n d -> p (n d)")
                evac(dve.tensor_tensor(xb, full(name), xb, ALU.add), name)

            for name in A_ORDER:
                n = int(name[2:])
                if name[:2] == "at":
                    mask_scores(n)
                elif name[:2] == "ml":
                    gated_output(n)
                elif name[:2] == "ax":
                    add_to_x(name, n)

            own.settle()
            layer_norm(1, 1)
            evac_ht(1, HT)
            for n in range(NT):
                own.step(dve.bn_stats(st6[:, n, :], full(f"bs{n // TB}")[:, (n % TB) * S:(n % TB + 1) * S]))
            own.settle()
            for n in range(NT):
                own.step(dve.bn_aggr(mv[:, n, :], st6[:, n, :]))
            inverse_root(2, EPS_SIM)
            dve.wait_ge(loaded_b, 32)
            for n in range(NT):
                ins = dve.tensor_scalar(SIM[:, n, :], full(f"bs{n // TB}")[:, (n % TB) * S:(n % TB + 1) * S],
                                        mv[:, n, 0:1], rstd[:, n:n + 1], ALU.subtract, ALU.mult)
                if n % TB == TB - 1:
                    evac(ins, f"bs{n // TB}")
                else:
                    own.step(ins)
            for b in range(B):
                sl = slice(b * TB, (b + 1) * TB)
                own.settle()
                own.step(dve.tensor_tensor(SIM[:, sl, :], SIM[:, sl, :],
                                           gamma.unsqueeze(1).to_broadcast([P, TB, D]), ALU.mult))
                own.settle()
                own.step(dve.tensor_tensor(SIM[:, sl, :], SIM[:, sl, :],
                                           beta.unsqueeze(1).to_broadcast([P, TB, D]), ALU.add))
                own.settle()
                own.mark(dve.tensor_reduce(col[:, NT + b * TB:NT + (b + 1) * TB], SIM[:, sl, :], AX.X, ALU.max,
                                             negate=True), simmax_ready, b + 1)
            for b in range(B):
                dve.wait_ge(simexp_ready, (b + 1) * TB)
                c0 = 2 * NT + b * TB
                own.step(dve.reciprocal(col[:, c0:c0 + TB], col[:, c0:c0 + TB]))
                own.settle()
                for n in range(b * TB, (b + 1) * TB):
                    own.step(dve.scalar_tensor_tensor(out=X[:, n, :], in0=SIM[:, n, :],
                                                      scalar=col[:, 2 * NT + n:2 * NT + n + 1], in1=X[:, n, :],
                                                      op0=ALU.mult, op1=ALU.add))
            own.settle()

            layer_norm(2, 3)
            dve.wait_ge(h_odd, 3 * B)
            own.settle()
            amax = col[:, 4 * NT:5 * NT]
            qs = col[:, 5 * NT:6 * NT]
            own.step(dve.tensor_reduce(amax, HN[:], AX.X, ALU.max, apply_absolute_value=True))
            own.settle()
            own.step(dve.tensor_scalar(amax, amax, 1e-8, None, ALU.max))
            own.settle()
            own.step(dve.reciprocal(qs, amax))
            own.settle()
            own.step(dve.tensor_scalar(qs, qs, 127.0, None, ALU.mult))
            own.step(dve.tensor_scalar(amax, amax, col[:, 3:4], None, ALU.mult))
            own.settle()
            for n in range(NT):
                own.step(dve.tensor_scalar(HN[:, n, :], HN[:, n, :], qs[:, n:n + 1], MAGIC, ALU.mult, ALU.add))
            own.settle()
            own.step(dve.tensor_scalar(HN[:], HN[:], -MAGIC, 127.0, ALU.add, ALU.min))
            own.settle()
            own.mark(dve.tensor_scalar(XQ, HN[:], -127.0, None, ALU.max), xq_ready, 1)
            for b in range(B):
                for n in range(b * TB, (b + 1) * TB):
                    ins = dve.scalar_tensor_tensor(out=X[:, n, :], in0=full(f"cy{b}")[:, (n % TB) * D:(n % TB + 1) * D],
                                                   scalar=amax[:, n:n + 1], in1=X[:, n, :], op0=ALU.mult, op1=ALU.add)
                    if n % TB == TB - 1:
                        evac(ins, f"cy{b}")
                    else:
                        own.step(ins)
            own.settle()
            own.mark(dve.tensor_copy(col[:, 0:1], col[:, 1:2]), x_after_c, 1)

            layer_norm(3, 4)
            evac_ht(3, HT)
            dve.wait_ge(loaded_wo, 32)
            own.mark(dve.tensor_scalar(WO, WO, gnorm[:, 0:1], None, ALU.mult), wo_scaled, 1)
            with dve.Fori(0, PAIRS) as i:
                own.enter(i, 2 * (1 + 3) + 4 * (2 + 3))
                for g in range(2):
                    name = f"d.s{g}"
                    evac(dve.tensor_scalar(EM[:, 4 * g:4 * g + 4, :].rearrange("p a b -> p (a b)"), full(name, i), 32.0, -32.0,
                                           ALU.min, ALU.max), name, i)
                for half in range(2):
                    evac(dve.tensor_copy(kT[:, half * HALF:(half + 1) * HALF], full(f"d.k{half}", i)), f"d.k{half}", i)
                for g in range(2):
                    evac(dve.tensor_copy(ET[:, g * HALF:(g + 1) * HALF], full(f"d.et{g}", i)), f"d.et{g}", i)

                def mask(name, dst, j):
                    name = f"d.{name}{j}"
                    evac(dve.tensor_tensor(dst[:, j % 4, :], full(name, i)[:, 0:3 * P], mask3, ALU.mult), name, i)

                def softmax_in(g):
                    sl = slice(4 * g, 4 * g + 4)
                    pm = PM[:, sl, :].rearrange("p a b -> p (a b)")
                    heads = PM[:, sl, :].rearrange("p n (h m) -> p (n h) m", h=2)
                    mx = slotmax[:, 8 * g:8 * g + 8]
                    dve.wait_ge(rc_ready, i * 2 + (g + 1))
                    evac(dve.tensor_tensor(pm, full(f"d.ok{g}", i), RC[:, sl, :].rearrange("p a b -> p (a b)"), ALU.mult),
                         f"d.ok{g}", i)
                    own.settle()
                    own.step(dve.tensor_reduce(mx, heads, AX.X, ALU.max))
                    own.settle()
                    own.mark(dve.tensor_tensor(heads, heads, mx.unsqueeze(2).to_broadcast([P, 8, M]), ALU.subtract),
                               ok_shifted, i * 2 + (g + 1))

                def softmax_out(g):
                    sl = slice(4 * g, 4 * g + 4)
                    pm = PM[:, sl, :]
                    heads = pm.rearrange("p n (h m) -> p (n h) m", h=2)
                    s8 = slice(8 * g, 8 * g + 8)
                    dve.wait_ge(ok_exp, i * 2 + (g + 1))
                    own.step(dve.tensor_reduce(slotsum[:, s8], heads, AX.X, ALU.add))
                    own.settle()
                    own.mark(dve.tensor_tensor(pm, pm, RC[:, sl, :], ALU.mult), p_ready, i * 2 + (g + 1))
                    own.step(dve.reciprocal(rs[:, s8], slotsum[:, s8]))
                    own.settle()
                    own.step(dve.tensor_tensor(rs2[:, s8], rs[:, s8], rs[:, s8], ALU.mult))

                def gate_outputs(b):
                    s4 = slice(4 * b, 4 * b + 4)
                    dve.wait_ge(sumsq_ready, i * B + (b + 1))
                    own.step(dve.tensor_tensor(rmsv[:, s4], sumsq[:, s4], rs2[:, s4], ALU.mult))
                    own.settle()
                    own.mark(dve.tensor_scalar(rmsv[:, s4], rmsv[:, s4], 1.0 / DV, EPS_RMS, ALU.mult, ALU.add),
                             rmsv_ready, i * B + (b + 1))
                    dve.wait_ge(rms_guess, i * B + (b + 1))
                    own.step(dve.tensor_tensor(coef[:, s4], rmsl[:, s4], rs[:, s4], ALU.mult))
                    own.settle()
                    pb = full(f"d.o{b}", i)
                    for j in range(4):
                        n, h = b * TB + j // 2, j % 2
                        hv = slice(h * DV, (h + 1) * DV)
                        ins = dve.scalar_tensor_tensor(out=OD[:, n, hv], in0=pb[:, j * DV:(j + 1) * DV],
                                                       scalar=coef[:, b * 4 + j:b * 4 + j + 1], in1=SG[:, n, hv],
                                                       op0=ALU.mult, op1=ALU.mult)
                        if j == 3:
                            evac(ins, f"d.o{b}", i)
                        else:
                            own.step(ins)

                for j in range(4):
                    mask("at", ATd, j)
                softmax_in(0)
                for j in range(4, 8):
                    mask("at", ATd, j)
                softmax_out(0)
                softmax_in(1)
                for j in range(2):
                    mask("bt", BTd, j)
                softmax_out(1)
                for j in range(2, 4):
                    mask("bt", BTd, j)
                gate_outputs(0)
                gate_outputs(1)
                for j in range(4, 8):
                    mask("bt", BTd, j)
                gate_outputs(2)
                gate_outputs(3)
                own.leave(PAIRS)
            for b in range(B):
                add_to_x(f"dx{b}", b)
            own.settle()
            own.mark(dve.tensor_copy(col[:, 0:1], col[:, 1:2]), x_after_d, 1)

            layer_norm(4, 5)
            evac_ht(4, HT)
            with dve.Fori(0, PAIRS) as i:
                own.enter(i, 4)
                evac(dve.tensor_copy(QE[:, HALF:], full("e.q1", i)), "e.q1", i)
                for name in E_BODY[2:]:
                    kind, at_ = name[2:4], name[4:]
                    b = int(at_[0])
                    if kind == "sc":
                        h = int(at_[1])
                        own.mark(dve.tensor_reduce(nmx[:, b * TB:(b + 1) * TB, h], full(name, i).rearrange("p (n s) -> p n s", n=TB),
                                                     AX.X, ALU.max, negate=True), emax_ready, i * 8 + (2 * b + h + 1))
                    elif kind == "pt" and at_[1] == "1":
                        evac(dve.tensor_copy(PXT[:, b % 2, 1, :, :].rearrange("p a b -> p (a b)"), full(name, i)), name, i)
                    elif kind == "cx":
                        es = esum[:, b * TB:(b + 1) * TB, :].rearrange("p n h -> p (n h)")
                        for h in range(2):
                            dve.wait_ge(evacuated[banks.bank(f"e.sc{b}{h}")], banks.after(f"e.sc{b}{h}", i))
                        own.step(dve.reciprocal(es, es))
                        own.settle()
                        dst = CX[:, b * TB:(b + 1) * TB, :, :].rearrange("p n h c -> p (n h) c")
                        evac(dve.tensor_tensor(dst, full(name, i)[:, 0:4 * DC].rearrange("p (n c) -> p n c", n=4),
                                               es.unsqueeze(2).to_broadcast([P, 4, DC]), ALU.mult), name, i)
                own.leave(PAIRS)
            for b in range(B):
                add_to_x(f"ex{b}", b)
            own.settle()

            layer_norm(5, 6)
            evac_ht(5, HT)
            dve.wait_ge(loaded_router, 16 * 4)
            dve.wait_ge(evacuated[banks.bank("lg")], banks.after("lg"))
            revb = rev.unsqueeze(1).to_broadcast([P, NT, E])
            bcast = lambda v: v.unsqueeze(2).to_broadcast([P, NT, E])
            src = AFF
            for k in range(2):
                best, first = tk[:, 2 * k, :], tk[:, 2 * k + 1, :]
                pick = TK[:, k, :, :]
                own.step(dve.tensor_reduce(best, src, AX.X, ALU.max))
                own.settle()
                own.step(dve.tensor_tensor(pick, src, bcast(best), ALU.is_equal))
                own.settle()
                own.step(dve.tensor_tensor(pick, pick, revb, ALU.mult))
                own.settle()
                own.step(dve.tensor_reduce(first, pick, AX.X, ALU.max))
                own.settle()
                own.step(dve.tensor_tensor(pick, pick, bcast(first), ALU.is_equal))
                own.settle()
                if k == 0:
                    own.step(dve.scalar_tensor_tensor(out=TK[:, 2, :, :], in0=pick, scalar=-4.0, in1=AFF, op0=ALU.mult,
                                                      op1=ALU.add))
                    own.settle()
                    src = TK[:, 2, :, :]
            own.step(dve.tensor_tensor(tk[:, 4, :], tk[:, 0, :], tk[:, 2, :], ALU.add))
            own.settle()
            own.step(dve.reciprocal(tk[:, 4, :], tk[:, 4, :]))
            own.settle()
            for k in range(2):
                own.step(dve.tensor_tensor(tk[:, 2 * k, :], tk[:, 2 * k, :], tk[:, 4, :], ALU.mult))
            own.settle()
            for k in range(2):
                own.step(dve.tensor_tensor(TK[:, k, :, :], TK[:, k, :, :], bcast(tk[:, 2 * k, :]), ALU.mult))
            own.step(dve.memset(CB[:, :, E:NE], 1.0))
            own.settle()
            own.mark(dve.tensor_tensor(CB[:, :, 0:E], TK[:, 0, :, :], TK[:, 1, :, :], ALU.add), shares_ready, 1)
            evac(dve.tensor_copy(CBT[:, 0:HALF], full("cb0")[0:NE, :]), "cb0")
            evac(dve.tensor_copy(CBT[:, HALF:], full("cb1")[0:NE, :]), "cb1")
            own.settle()
            own.mark(dve.tensor_copy(col[:, 0:1], col[:, 1:2]), comb_ready, 1)
            own.step(dve.tensor_tensor(X[:], X[:], HN[:], ALU.add))
            with dve.Fori(0, F_TRIPS) as i:
                for e in range(2):
                    dve.wait_ge(loaded_fin[e], i * 64 + 64)
                    for half in range(2):
                        sl = slice(half * HALF, (half + 1) * HALF)
                        g_name, name = f"f.g{half}{e}", f"f.u{half}{e}"
                        dve.wait_ge(evacuated[banks.bank(g_name)], banks.after(g_name, i))
                        evac(dve.scalar_tensor_tensor(out=YC[:, e, sl], in0=full(name, i), scalar=fub[:, e], in1=Y[:, e, sl],
                                                      op0=ALU.add, op1=ALU.mult), name, i)
                        if half == 0:
                            dve.wait_ge(loaded_bc[e], i * 16 + 16)
                        own.settle()
                        own.mark(dve.tensor_tensor(YC[:, e, sl], YC[:, e, sl], BC[:, e, sl], ALU.mult), yc_ready,
                                   i * 4 + (2 * e + half + 1))
            dve.wait_ge(expert_out[1], F_TRIPS)
            for b in range(B):
                xb = X[:, b * TB:(b + 1) * TB, :].rearrange("p n d -> p (n d)")
                own.step(dve.tensor_tensor(xb, ps[:, banks.bank(f"acc{b}"), :], xb, ALU.add))
            own.settle()
            own.mark(dve.tensor_copy(col[:, 0:1], col[:, 1:2]), x_final, 1)


def constants(ctx_shape, experts):
    _, length, dim = ctx_shape
    i = np.arange(P)
    ident = (i[:, None] == i[None, :]).astype(np.float32)
    causal = (i[:, None] <= i[None, :]).astype(np.float32)
    const = np.concatenate([ident, causal, np.ones((P, P), np.float32), causal], axis=1)
    one = np.float32(1.0)
    inv = one / np.float32(10000.0) ** (np.arange(0, dim, 2, dtype=np.float32) / np.float32(dim))
    freqs = np.arange(length, dtype=np.float32)[:, None] * inv[None, :].astype(np.float32)
    cos = np.repeat(np.cos(freqs), 2, axis=-1)
    sin = np.repeat(np.sin(freqs), 2, axis=-1)
    sin[:, : dim // 2] *= -1
    return {"const": const, "rope": np.stack([cos, sin]).astype(np.float32),
            "rev": np.arange(experts, 0, -1).astype(np.float32)}


def kernel(**inputs):
    import numpy as _np
    import concourse.bacc as _bacc
    from concourse import mybir as _mybir
    from concourse.bass_utils import run_bass_kernel_spmd as _run

    nc = _bacc.Bacc("TRN2", target_bir_lowering=False, num_devices=1)
    arrays = {n: _np.ascontiguousarray(a) for n, a in inputs.items()}
    arrays.update(constants(arrays["ctx_512"].shape, arrays["L1_ffn_wa"].shape[1]))
    aps = {n: nc.dram_tensor(f"in_{n}", a.shape, _mybir.dt.from_np(a.dtype), kind="ExternalInput").ap()
           for n, a in arrays.items()}
    shape = arrays["x"].shape
    out = nc.dram_tensor("out_x", shape, _mybir.dt.float32, kind="ExternalOutput").ap()
    decoder_kernel(nc, aps, out)
    r = _run(nc, [{f"in_{n}": a for n, a in arrays.items()}], core_ids=[0])
    return r.results[0]["out_x"]
```

```python
from contextlib import ExitStack

import numpy as np

import concourse.bass as bass
from concourse import mybir

F32 = mybir.dt.float32
BF16 = mybir.dt.bfloat16
ALU = mybir.AluOpType
ACT = mybir.ActivationFunctionType
AX = mybir.AxisListType
ds = bass.ds

P = 128
MAGIC = 1.5 * 2.0**23


class Banks:

    def __init__(self):
        self.count = [0] * 8
        self.at = {}
        self.order = []
        self.turn = 0

    def line(self, names):
        for name in names:
            bank = self.turn % 8
            self.at[name] = (bank, self.count[bank], None)
            self.order.append(name)
            self.count[bank] += 1
            self.turn += 1

    def loop(self, names, trips, banks=range(8), not_in_last=()):
        per = [0] * 8
        for n, name in enumerate(names):
            bank = banks[n % len(banks)]
            self.at[name] = (bank, self.count[bank] + per[bank], per)
            self.order.append(name)
            per[bank] += 1
        self.count = [c + trips * p for c, p in zip(self.count, per)]
        for name in not_in_last:
            self.count[self.bank(name)] -= 1
        self.turn = 0

    def bank(self, name):
        return self.at[name][0]

    def before(self, name, i=0):
        bank, count, per = self.at[name]
        return count if per is None else i * per[bank] + count

    def after(self, name, i=0):
        bank, count, per = self.at[name]
        return count + 1 if per is None else i * per[bank] + (count + 1)

    def after_previous(self, name, i):
        bank, count, per = self.at[name]
        assert count + 1 - per[bank] > 0
        return i * per[bank] + (count + 1 - per[bank])


class Steps:

    def __init__(self, eng, sem):
        self.eng, self.sem, self.n, self.loop, self.last = eng, sem, 0, None, None

    def now(self):
        if self.loop is None:
            return self.n
        i, per, start = self.loop
        return i * per + self.n

    def step(self, ins):
        ins.then_inc(self.sem, 1)
        self.n += 1
        self.last = (self.sem, self.now())

    def mark(self, ins, sem, value):
        ins.then_inc(sem, 1)
        self.last = (sem, value)

    def settle(self):
        self.eng.wait_ge(*self.last)

    def enter(self, i, per):
        self.loop = (i, per, self.n)

    def leave(self, trips):
        _, per, start = self.loop
        assert self.n - start == per, (self.n - start, per)
        self.n = start + trips * per
        self.loop = None
        self.last = (self.sem, self.n)


def decoder_kernel(nc, t, out):
    B, S, D = t["x"].shape
    NT = B * S // P
    TB = S // P
    NTOK = B * S
    C = D // P
    HALF = 512
    DC = t["ctx_512"].shape[2]
    DA = t["L0_attn_w_q"].shape[0]
    H = t["L1_xattn_Wq"].shape[0] // P
    PAIRS = H // 2
    M = t["L1_attn_Ws"].shape[1] // H
    DV = t["L1_attn_Wv"].shape[1] // H
    CQ = t["L1_xattn_w_kc_q"].shape[2]
    R = t["L1_xattn_W_qr"].shape[2]
    QC = CQ // 2
    E = t["L1_ffn_wa"].shape[1]
    SH = t["L1_ffn_sg"].shape[0]
    NE = E + SH
    EPS_LN = 1e-5
    EPS_A = 1e-6
    EPS_SIM = 1e-6
    EPS_RMS = 1e-5

    banks = Banks()
    ht = lambda k: [f"ht{k}_{b}" for b in range(B)]
    banks.line(["w0", "w1", "ctx0", "ctx1", "wk"])
    banks.line(ht(0) + ["aq0", "aq1", "ak0", "ak1", "av0", "av1"])
    banks.line(["kvT0", "kvT1", "kv", "wsum", "wqT"])
    A_ORDER = ["at0", "at1", "ml0", "ml1", "at2", "ml2", "ml3", "ao0", "ax0", "at3", "ml4", "ml5", "ao1", "ax1",
               "ml6", "ml7", "ao2", "ax2", "ao3", "ax3"]
    banks.line(A_ORDER)
    banks.line(["kr0", "kr1"])
    banks.line(ht(1) + [f"bo{b}" for b in range(B)] + [f"bs{b}" for b in range(B)])
    banks.line(ht(2) + [f"cy{b}" for b in range(B)])
    D_BODY = (["q0", "q1", "k0", "k1", "v0", "v1", "cu0", "cu1", "et0", "et1",
               "g0", "g1", "g2", "g3", "wot"]
              + ["at0", "at1", "at2", "at3", "u0", "v2", "ok0", "at4", "at5", "at6", "at7", "u1", "v3", "ok1"]
              + ["pt0", "w2", "bt0", "bt1", "bt2", "bt3", "o0", "pt1", "o1", "bt4", "bt5", "bt6", "bt7",
                 "ot0", "ot1", "V", "o2", "T0", "T1", "o3", "s0", "s1", "ot2", "ot3"])
    D_BODY = ["d." + n for n in D_BODY]
    banks.line(ht(3) + ["first_s0", "first_s1"])
    banks.loop(D_BODY, PAIRS, not_in_last=("d.s0", "d.s1"))
    banks.line(["dx0", "dx1", "dx2", "ht4_0", "ht4_1", "dx3", "ht4_2", "first_q0", "ht4_3", "first_q1"])
    E_BODY = ["sc00", "sc01", "sc10", "sc11", "pt00", "pt01", "sc20", "sc21", "cx0", "pt10", "pt11", "sc30", "ct0",
              "sc31", "cx1", "pt20", "pt21", "ct1", "pt30", "cx2", "pt31", "q0", "ct2", "cx3", "q1", "ct3"]
    E_BODY = ["e." + n for n in E_BODY]
    E_BANKS = (0, 1, 2, 3, 4, 5, 0, 1, 6, 7, 2, 3, 4, 0, 1, 5, 6, 7, 2, 0, 1, 3, 4, 5, 6, 7)
    assert len(E_BANKS) == len(E_BODY)
    banks.loop(E_BODY, PAIRS, banks=E_BANKS, not_in_last=("e.q0", "e.q1"))
    banks.line(["ex0", "ex1", "ex2", "ht5_0", "ht5_1", "ex3", "ht5_2", "ht5_3"])
    banks.turn = 0
    banks.line(["lg", "cb0", "cb1"])
    banks.turn = 0
    banks.line([f"acc{b}" for b in range(B)])
    F_TRIPS = NE // 2
    F_BODY = [f"f.{x}{half}{e}" for e in range(2) for x in "gu" for half in range(2)]
    banks.loop(F_BODY, F_TRIPS, banks=(4, 5, 6, 7))

    with ExitStack() as ctx:
        def sb(name, shape, dt=F32):
            return ctx.enter_context(nc.sbuf_tensor(name, shape, dt))

        def sem(name):
            return ctx.enter_context(nc.semaphore(name))

        ps = ctx.enter_context(nc.psum_tensor("ps", [P, 8, 512], F32))

        X = sb("X", [P, NT, D])
        HN = sb("HN", [P, NT, D])
        HT = sb("HT", [P, C, NTOK])
        const = sb("const", [P, 4 * P])
        ident, causal, ones = const[:, 0:P], const[:, P:2 * P], const[:, 2 * P:3 * P]
        mask3 = const[:, P:4 * P]
        identb = sb("identb", [P, P], BF16)
        krT = sb("krT", [P, NTOK])
        kr = sb("kr", [P, NT, 2, DC])
        st6 = sb("st6", [P, NT, 6])
        mv = sb("mv", [P, NT, 2])
        ve = sb("ve", [P, NT])
        guess = sb("guess", [P, NT])
        nt = sb("nt", [P, NT])
        rstd = sb("rstd", [P, NT])
        nmr = sb("nmr", [P, NT])
        gg = sb("gg", [P, 2])
        col = sb("col", [P, 8 * NT])

        ARENA = 37 * 1024 + 256
        arena = sb("arena", [P, ARENA])
        at = [0]

        def carve(*shape, rows=P):
            n = int(np.prod(shape))
            v = arena[0:rows, at[0]:at[0] + n]
            at[0] += n
            assert at[0] <= ARENA
            if len(shape) == 1:
                return v
            names = "abcd"[:len(shape)]
            return v.rearrange(f"p ({' '.join(names)}) -> p {' '.join(names)}", **dict(zip(names, shape)))

        waraw = carve(3, D)
        woraw = carve(2, P)
        WT = carve(8, P)
        MZ = carve(DA + 1)
        ctxn = carve(NT, DC)
        ctxT = carve(NTOK, rows=DC + 1)
        wkraw = carve(DC, rows=DC)
        wkT = carve(DC, rows=DC + 1)
        kvT = carve(NTOK, rows=DC)
        kvn = carve(NT, DC)
        rope = carve(2, TB, DC)
        ropet = carve(NT, DC)
        gamma = carve(D)
        beta = carve(D)
        wf = carve(2, D)
        wq8 = carve(D).bitcast(BF16).rearrange("p (a b) -> p a b", a=2)
        WQT = carve(D).bitcast(BF16).rearrange("p (a b) -> p a b", a=2)
        amin = carve(4, HALF)
        SQ = carve(NTOK)
        SK = carve(NTOK)
        VV = carve(NT, DA + 1)
        AT = carve(2, 3 * P)
        AO = carve(NT, DA)
        AOT = carve(NTOK)
        BO = carve(NTOK, rows=DC)
        SIM = carve(NT, D)
        XQ = carve(NT * D // 2).bitcast(BF16).rearrange("p (a b) -> p a b", a=NT)
        XQT = carve(C * NTOK // 2).bitcast(BF16).rearrange("p (a b) -> p a b", a=C)
        wqk = sb("wqk", [P, 2, C, 2 * M])
        wsv = sb("wsv", [P, C, 2 * M + 2 * DV])
        wg = sb("wg", [P, C, 2 * DV])
        Tall = sb("Tall", [P, PAIRS, C, 2 * DC])
        W2 = sb("W2", [P, PAIRS, D])
        gnorm = sb("gnorm", [P, 1])
        NH = NT * 2
        slotmax = sb("slotmax", [P, NH])
        slotsum = sb("slotsum", [P, NH])
        rs = sb("rs", [P, NH])
        rs2 = sb("rs2", [P, NH])
        sumsq = sb("sumsq", [P, NH])
        rmsv = sb("rmsv", [P, NH])
        rmsl = sb("rmsl", [P, NH])
        coef = sb("coef", [P, NH])

        at[0] = 0
        OT = carve(PAIRS, 2, NTOK)
        WO = carve(H, D)
        qT = carve(NTOK)
        kT = carve(NTOK)
        EM = carve(NT, 2 * M)
        ET = carve(NTOK)
        RC = carve(NT, 2 * M)
        PT = RC.rearrange("p a b -> p (a b)")
        VD = carve(NT, 2 * DV)
        SG = carve(NT, 2 * DV)
        ATd = carve(4, 3 * P)
        BTd = carve(4, 3 * P)
        PM = carve(NT, 2 * M)
        JUNK = carve(4, DV)
        OD = HN
        xwq = carve(2, D)
        xkq = carve(2, CQ)
        xqr = carve(2, 2, R, rows=QC)
        xkr = carve(2, R, rows=DC)
        xkv = carve(2, DC)
        xwo = carve(2, 2 * P)
        WOTe = carve(2, D)
        KRT = carve(DC)
        U = carve(2, 2, D, rows=QC)
        VE = carve(D)

        at[0] = 0
        CT = carve(PAIRS, NTOK)
        QE = carve(NTOK)
        Tcur = carve(C, 2 * DC)
        PX = carve(2, 2, TB, S)
        PXT = carve(2, 2, TB, S)
        CX = carve(NT, 2, DC)
        nmx = carve(NT, 2)
        esum = carve(NT, 2)
        wr = carve(C, E)
        rev = carve(E)
        b2 = carve(D, rows=NE)
        fg = carve(2, C, P)
        fu = carve(2, C, P)
        fo = carve(2, D)
        fgb = carve(2, 1)
        fub = carve(2, 1)
        BC = carve(2, NTOK)
        Y = carve(2, NTOK)
        YC = carve(2, NTOK)
        AFF = carve(NT, E)
        TK = carve(4, NT, E)
        tk = carve(6, NT)
        CB = carve(NT, NE)
        CBT = carve(NTOK, rows=NE)
        comb_dram = nc.dram_tensor("comb_by_expert", [NE, NTOK], F32, kind="Internal").ap()

        filled = [sem(f"filled{b}") for b in range(8)]
        evacuated = [sem(f"evacuated{b}") for b in range(8)]
        loaded_x = sem("loaded_x")
        loaded_const = sem("loaded_const")
        loaded_a = sem("loaded_a")
        loaded_ctx = sem("loaded_ctx")
        loaded_c = sem("loaded_c")
        loaded_b = sem("loaded_b")
        dve_steps = sem("dve_steps")
        act_steps = sem("act_steps")
        var_ready = sem("var_ready")
        guess_ready = sem("guess_ready")
        nmr_ready = sem("nmr_ready")
        h_even = sem("h_even")
        h_odd = sem("h_odd")
        gate_ready = sem("gate_ready")
        ones_ready = sem("ones_ready")
        identb_ready = sem("identb_ready")
        kr_ready = sem("kr_ready")
        wabs_ready = sem("wabs_ready")
        wq8_ready = sem("wq8_ready")
        amin_ready = sem("amin_ready")
        aexp_ready = sem("aexp_ready")
        ao_ready = sem("ao_ready")
        simmax_ready = sem("simmax_ready")
        simexp_ready = sem("simexp_ready")
        xq_ready = sem("xq_ready")
        stored = sem("stored")
        x_final = sem("x_final")
        x_after_c = sem("x_after_c")
        x_after_d = sem("x_after_d")
        loaded_wqk = sem("loaded_wqk")
        loaded_wsv = sem("loaded_wsv")
        loaded_wg = sem("loaded_wg")
        loaded_wo = sem("loaded_wo")
        loaded_comp = sem("loaded_comp")
        loaded_T = sem("loaded_T")
        loaded_router = sem("loaded_router")
        loaded_fin = [sem(f"loaded_fin{e}") for e in range(2)]
        loaded_fout = [sem(f"loaded_fout{e}") for e in range(2)]
        loaded_bc = [sem(f"loaded_bc{e}") for e in range(2)]
        wo_scaled = sem("wo_scaled")
        em_exp = sem("em_exp")
        rc_ready = sem("rc_ready")
        ok_shifted = sem("ok_shifted")
        ok_exp = sem("ok_exp")
        p_ready = sem("p_ready")
        sumsq_ready = sem("sumsq_ready")
        rmsv_ready = sem("rmsv_ready")
        rms_guess = sem("rms_guess")
        emax_ready = sem("emax_ready")
        comb_ready = sem("comb_ready")
        shares_ready = sem("shares_ready")
        comb_stored = sem("comb_stored")
        yc_ready = sem("yc_ready")
        expert_out = [sem(f"expert_out{e}") for e in range(2)]

        block = ctx.enter_context(nc.Block())

        tile = lambda n: slice(n * P, (n + 1) * P)

        @block.sync
        def _(sp):
            xv = t["x"].rearrange("b (h p) d -> p (b h) d", p=P)
            sp.dma_start(X[:], xv).then_inc(loaded_x, 16)
            sp.dma_start(const[:], t["const"]).then_inc(loaded_const, 16)
            for n, w in enumerate(("w_q", "w_k", "w_v")):
                sp.dma_start(waraw[:, n, :], t["L0_attn_" + w]).then_inc(loaded_a, 16)
            sp.dma_start(woraw, t["L0_attn_w_o"].rearrange("(n p) d -> p n d", p=P)).then_inc(loaded_a, 16)
            sp.dma_start(MZ[:, 0:DA], t["L0_attn_M"]).then_inc(loaded_a, 16)
            sp.dma_start(MZ[:, DA:DA + 1], t["L0_attn_z"].rearrange("(d o) -> d o", o=1)).then_inc(loaded_a, 16)
            sp.dma_start(gg[:, 0:1], t["L0_attn_gate"].partition_broadcast(P)).then_inc(loaded_a, 16)
            sp.dma_start(ctxn, t["ctx_512"].rearrange("b (h p) d -> p (b h) d", p=P)).then_inc(loaded_ctx, 16)
            sp.dma_start(rope, t["rope"].rearrange("a (h p) d -> p a h d", p=P)).then_inc(loaded_ctx, 16)
            sp.dma_start(wkraw, t["L0_xattn_W_k"]).then_inc(loaded_ctx, 16)
            sp.dma_start(wkT[DC:DC + 1, :], t["L0_xattn_b_k"].unsqueeze(0)).then_inc(loaded_ctx, 16)
            sp.dma_start(wf, t["L0_ffn_weight"].rearrange("(n p) d -> p n d", p=P)).then_inc(loaded_c, 16)
            sp.dma_start(gamma, t["L0_xattn_ln_gamma"].partition_broadcast(P)).then_inc(loaded_b, 16)
            sp.dma_start(beta, t["L0_xattn_ln_beta"].partition_broadcast(P)).then_inc(loaded_b, 16)
            def after(semaphore, value):
                sp.wait_ge(semaphore, value)
                sp.wait_ge(loaded_const, 16)


            def load_wqk(i):
                for n, w in enumerate(("Wq", "Wk")):
                    v = t["L1_attn_" + w].rearrange("(c p) n -> p c n", p=P)
                    sp.dma_start(wqk[:, n, :, :], v[:, :, ds(i * 2 * M, 2 * M)]).then_inc(loaded_wqk, 16)

            def load_wsv(i):
                v = t["L1_attn_Ws"].rearrange("(c p) n -> p c n", p=P)
                sp.dma_start(wsv[:, :, 0:2 * M], v[:, :, ds(i * 2 * M, 2 * M)]).then_inc(loaded_wsv, 16)
                v = t["L1_attn_Wv"].rearrange("(c p) n -> p c n", p=P)
                sp.dma_start(wsv[:, :, 2 * M:], v[:, :, ds(i * 2 * DV, 2 * DV)]).then_inc(loaded_wsv, 16)

            def load_wg(i):
                v = t["L1_attn_Wg"].rearrange("(c p) n -> p c n", p=P)
                sp.dma_start(wg[:], v[:, :, ds(i * 2 * DV, 2 * DV)]).then_inc(loaded_wg, 16)

            def load_comp(i):
                two = lambda a: a[ds(i * 2, 2)]
                sp.dma_start(xwq, t["L1_xattn_Wq"].rearrange("(h k) d -> k h d", k=P)[:, ds(i * 2, 2), :]).then_inc(loaded_comp, 16)
                sp.dma_start(xkq, t["L1_xattn_w_kc_q"].rearrange("h k q -> k h q")[:, ds(i * 2, 2), :]).then_inc(loaded_comp, 16)
                qr = t["L1_xattn_W_qr"].rearrange("h (a q) r -> q h a r", q=QC)
                for a in range(2):
                    sp.dma_start(xqr[:, a], qr[:, ds(i * 2, 2), a, :]).then_inc(loaded_comp, 16)
                sp.dma_start(xkr, t["L1_xattn_W_kr"].rearrange("h c r -> c h r")[:, ds(i * 2, 2), :]).then_inc(loaded_comp, 16)
                sp.dma_start(xkv, t["L1_xattn_w_kc_kv"].rearrange("h k c -> k h c")[:, ds(i * 2, 2), :]).then_inc(loaded_comp, 16)
                sp.dma_start(xwo, t["L1_xattn_Wo"].rearrange("(a n) k -> n a k", n=P)[:, :, ds(i * 2 * P, 2 * P)])\
                    .then_inc(loaded_comp, 16)

            load_wqk(0)
            load_wsv(0)
            load_wg(0)
            sp.dma_start(gnorm[:], t["L1_attn_g_norm_weight"].unsqueeze(1)).then_inc(loaded_wo, 16)
            sp.wait_ge(x_after_c, 1)
            load_comp(0)
            sp.dma_start(WO, t["L1_attn_Wo"].rearrange("(h p) n -> p h n", p=P)).then_inc(loaded_wo, 16)
            with sp.Fori(0, PAIRS - 1) as i:
                after(filled[banks.bank("d.k1")], banks.after("d.k1", i))
                load_wqk(i + 1)
                after(filled[banks.bank("d.v3")], banks.after("d.v3", i))
                load_wsv(i + 1)
                after(filled[banks.bank("d.g3")], banks.after("d.g3", i))
                load_wg(i + 1)
                after(filled[banks.bank("d.V")], banks.after("d.V", i))
                load_comp(i + 1)
            sp.wait_ge(x_after_d, 1)
            sp.dma_start(wr, t["L1_ffn_wa"].rearrange("(c p) e -> p c e", p=P)).then_inc(loaded_router, 16)
            sp.dma_start(rev, t["rev"].partition_broadcast(P)).then_inc(loaded_router, 16)
            sp.dma_start(b2[0:E, :], t["L1_ffn_rb2"]).then_inc(loaded_router, 16)
            sp.dma_start(b2[E:NE, :], t["L1_ffn_sb2"]).then_inc(loaded_router, 16)

            def load_T(i):
                sp.dma_start(Tcur.rearrange("p c n -> p (c n)"),
                             Tall[:, ds(i, 1), :, :].rearrange("p i c n -> p (i c n)")).then_inc(loaded_T, 16)

            load_T(0)
            sp.wait_ge(filled[banks.bank("first_q1")], banks.after("first_q1"))
            load_T(1)
            with sp.Fori(0, PAIRS - 2) as i:
                after(filled[banks.bank("e.q1")], banks.after("e.q1", i))
                load_T(i + 2)

            def load_in(e, g, u, gb, ub, row):
                for dst, w in ((fg, g), (fu, u)):
                    sp.dma_start(dst[:, e], w.rearrange("e (c p) f -> p (e c) f", p=P)[:, ds(row * C, C), :])\
                        .then_inc(loaded_fin[e], 16)
                for dst, w in ((fgb, gb), (fub, ub)):
                    sp.dma_start(dst[:, e], w.rearrange("e f -> f e")[:, ds(row, 1)]).then_inc(loaded_fin[e], 16)

            def load_out(e, o, row):
                sp.dma_start(fo[:, e], o.rearrange("e f n -> f e n")[:, ds(row, 1), :].rearrange("f e n -> f (e n)"))\
                    .then_inc(loaded_fout[e], 16)

            def load_bc(e, row):
                sp.dma_start(BC[:, e], comb_dram[ds(row, 1), :].rearrange("a n -> (a n)").partition_broadcast(P))\
                    .then_inc(loaded_bc[e], 16)

            routed = [t["L1_ffn_" + n] for n in ("rg", "rw1", "rgb", "rb1")]
            shared = [t["L1_ffn_" + n] for n in ("sg", "sw1", "sgb", "sb1")]
            for e in range(2):
                load_in(e, *routed, e)
                load_out(e, t["L1_ffn_rw2"], e)
            sp.wait_ge(comb_ready, 1)
            sp.dma_start(comb_dram, CBT).then_inc(comb_stored, 16)
            sp.wait_ge(comb_stored, 16)
            for e in range(2):
                load_bc(e, e)

            def next_experts(i, ins, out, row):
                for e in range(2):
                    after(yc_ready, 4 * i + 2 * e + 2)
                    load_in(e, *ins, row + e)
                    load_bc(e, row + e if ins is routed else E + e)
                for e in range(2):
                    after(expert_out[e], i + 1)
                    load_out(e, out, row + e)

            with sp.Fori(0, E // 2 - 1) as i:
                next_experts(i, routed, t["L1_ffn_rw2"], i * 2 + 2)
            next_experts(E // 2 - 1, shared, t["L1_ffn_sw2"], 0)
            ov = out.rearrange("b (h p) d -> p (b h) d", p=P)
            sp.wait_ge(x_final, 1)
            sp.dma_start(ov, X[:]).then_inc(stored, 16)
            sp.wait_ge(stored, 16)

        @block.tensor
        def _(pe):
            def fill(name, i=0):
                if not (banks.at[name][2] is None and banks.before(name) == 0):
                    pe.wait_ge(evacuated[banks.bank(name)], banks.before(name, i))
                return ps[:, banks.bank(name), :]

            def full(ins, name):
                ins.then_inc(filled[banks.bank(name)], 1)

            def evac(name, i=0):
                pe.wait_ge(evacuated[banks.bank(name)], banks.after(name, i))

            def transpose_h(b, dst, bf16=False):
                src, idn = (XQ, identb[:]) if bf16 else (HN, ident)
                for n in range(TB):
                    for c in range(C):
                        last = pe.transpose(dst[:, c * S + n * P:c * S + (n + 1) * P],
                                            src[:, b * TB + n, c * P:(c + 1) * P], idn)
                return last

            pe.wait_ge(loaded_const, 16)
            pe.wait_ge(loaded_a, 16 * 7)
            for half, name in enumerate(("w0", "w1")):
                pb = fill(name)
                for j in range(4):
                    n = half * 4 + j
                    src = waraw[:, n // 2, (n % 2) * P:(n % 2 + 1) * P] if n < 6 else woraw[:, n - 6, :]
                    last = pe.transpose(pb[:, j * P:(j + 1) * P], src, ident)
                full(last, name)
            pe.wait_ge(loaded_ctx, 16 * 4)
            for half, name in enumerate(("ctx0", "ctx1")):
                pb = fill(name)
                for j in range(4):
                    last = pe.transpose(pb[0:DC, j * P:(j + 1) * P], ctxn[:, half * 4 + j, :], ident)
                full(last, name)
            pb = fill("wk")
            full(pe.transpose(pb[0:DC, 0:DC], wkraw, ident[0:DC, 0:DC]), "wk")

            def layer_norm_T(k, batches=range(B)):
                for b in batches:
                    pb = fill(f"ht{k}_{b}")
                    pe.wait_ge(h_even, k * B + b + 1)
                    pe.wait_ge(h_odd, k * B + b + 1)
                    full(transpose_h(b, pb), f"ht{k}_{b}")

            layer_norm_T(0)
            evac("w0")
            evac("w1")
            for b in range(B):
                evac(f"ht0_{b}")
            for n, q in enumerate("qk"):
                for half in range(2):
                    name = f"a{q}{half}"
                    pb = fill(name)
                    for c in range(C):
                        last = pe.matmul(pb, WT[:, 2 * n + c, :], HT[:, c, half * HALF:(half + 1) * HALF],
                                         start=(c == 0), stop=(c == C - 1))
                    full(last, name)
            for half in range(2):
                name = f"av{half}"
                pb = fill(name)
                for j in range(4):
                    n = half * 4 + j
                    for c in range(C):
                        last = pe.matmul(pb[:, j * P:(j + 1) * P], HT[:, c, tile(n)], WT[:, 4 + c, :],
                                         start=(c == 0), stop=(c == C - 1))
                full(last, name)
            evac("ctx0")
            evac("ctx1")
            evac("wk")
            pe.wait_ge(ones_ready, 2)
            for half in range(2):
                name = f"kvT{half}"
                pb = fill(name)
                full(pe.matmul(pb[0:DC, :], wkT, ctxT[:, half * HALF:(half + 1) * HALF], start=True, stop=True), name)
            pb = fill("kv")
            for n in range(NT):
                last = pe.matmul(pb[:, n * DC:(n + 1) * DC], ctxT[:, tile(n)], wkT, start=True, stop=True)
            full(last, "kv")
            pe.wait_ge(wabs_ready, 1)
            pb = fill("wsum")
            full(pe.matmul(pb[:, 0:1], ones, col[:, 0:1], start=True, stop=True), "wsum")
            pe.wait_ge(wq8_ready, 1)
            pe.wait_ge(identb_ready, 1)
            pb = fill("wqT").bitcast(BF16)
            for c in range(C):
                for o in range(2):
                    last = pe.transpose(pb[:, c * D + o * P:c * D + (o + 1) * P], wq8[:, o, c * P:(c + 1) * P],
                                        identb[:])
            full(last, "wqT")

            def scores(b):
                pb = fill(f"at{b}")
                k0, k1 = tile(b * TB), tile(b * TB + 1)
                pe.matmul(pb[:, 0:2 * P], SK[:, k0], SQ[:, b * S:(b + 1) * S], start=True, stop=True)
                full(pe.matmul(pb[:, 2 * P:3 * P], SK[:, k1], SQ[:, k1], start=True, stop=True), f"at{b}")

            def memory_and_local(n):
                pb = fill(f"ml{n}")
                evac(f"at{n // TB}")
                w = DA + 1
                pe.matmul(pb[:, 0:w], SQ[:, tile(n)], MZ, start=True, stop=True)
                a = AT[:, (n // TB) % 2, :]
                if n % TB == 0:
                    last = pe.matmul(pb[:, w:2 * w], a[:, 0:P], VV[:, n, :], start=True, stop=True)
                else:
                    pe.matmul(pb[:, w:2 * w], a[:, P:2 * P], VV[:, n - 1, :], start=True, stop=False)
                    last = pe.matmul(pb[:, w:2 * w], a[:, 2 * P:3 * P], VV[:, n, :], start=False, stop=True)
                full(last, f"ml{n}")

            def output_T(b):
                pb = fill(f"ao{b}")
                evac(f"ml{b * TB + 1}")
                for n in range(TB):
                    last = pe.transpose(pb[:, n * P:(n + 1) * P], AO[:, b * TB + n, :], ident)
                full(last, f"ao{b}")

            def project_out(b):
                pb = fill(f"ax{b}")
                evac(f"ao{b}")
                for n in range(TB):
                    last = pe.matmul(pb[:, n * D:(n + 1) * D], AOT[:, tile(b * TB + n)],
                                     WT[:, 6:8, :].rearrange("p a b -> p (a b)"), start=True, stop=True)
                full(last, f"ax{b}")

            for name in ("aq0", "aq1", "ak0", "ak1", "av0", "av1"):
                evac(name)
            pe.wait_ge(ones_ready, 2)
            step_of = {"at": scores, "ml": memory_and_local, "ao": output_T, "ax": project_out}
            for name in A_ORDER:
                step_of[name[:2]](int(name[2:]))

            pe.wait_ge(kr_ready, 1)
            for half in range(2):
                name = f"kr{half}"
                pb = fill(name)
                for j in range(4):
                    last = pe.transpose(pb[:, j * P:(j + 1) * P],
                                        kr[:, half * 4 + j, :, :].rearrange("p a b -> p (a b)"), ident)
                full(last, name)

            layer_norm_T(1)
            for b in range(B):
                pb = fill(f"bo{b}")
                evac(f"ht1_{b}")
                for c in range(C):
                    last = pe.matmul(pb[0:DC, 0:S], kvn[:, b * TB + c, :], HT[:, c, b * S:(b + 1) * S],
                                     start=(c == 0), stop=(c == C - 1))
                full(last, f"bo{b}")
            for b in range(B):
                pb = fill(f"bs{b}")
                evac(f"bo{b}")
                for n in range(TB):
                    last = pe.matmul(pb[:, n * S:(n + 1) * S], BO[:, tile(b * TB + n)], kvT[:, b * S:(b + 1) * S],
                                     start=True, stop=True)
                full(last, f"bs{b}")

            evac("wqT")
            for b in range(B):
                pb = fill(f"ht2_{b}").bitcast(BF16)
                pe.wait_ge(xq_ready, 1)
                full(transpose_h(b, pb, bf16=True), f"ht2_{b}")
            for b in range(B):
                pb = fill(f"cy{b}")
                evac(f"ht2_{b}")
                for n in range(TB):
                    for c in range(C):
                        last = pe.matmul(pb[:, n * D:(n + 1) * D], XQT[:, c, tile(b * TB + n)], WQT[:, c, :],
                                         start=(c == 0), stop=(c == C - 1))
                full(last, f"cy{b}")
            layer_norm_T(3)
            for b in range(B):
                evac(f"ht3_{b}")

            def project(name, steps, w, width, i=0):
                per = 512 // width
                for j in steps:
                    pb = fill(f"{name}{j}", i)
                    for m in range(per):
                        for c in range(C):
                            last = pe.matmul(pb[:, m * width:(m + 1) * width], HT[:, c, tile(j * per + m)], w[:, c, :],
                                             start=(c == 0), stop=(c == C - 1))
                    full(last, f"{name}{j}")

            def slot_attention_trip(i, last_trip=False):
                def project_T(name, w):
                    for half in range(2):
                        pb = fill(f"{name}{half}", i)
                        for c in range(C):
                            last = pe.matmul(pb, w[:, c, :], HT[:, c, half * HALF:(half + 1) * HALF],
                                             start=(c == 0), stop=(c == C - 1))
                        full(last, f"{name}{half}")

                pe.wait_ge(loaded_wqk, i * 32 + 32)
                project_T("d.q", wqk[:, 0])
                project_T("d.k", wqk[:, 1])
                project("d.v", range(2), wsv[:, :, 2 * M:], 2 * DV, i)
                for g in range(2):
                    pe.wait_ge(em_exp, i * 2 + (g + 1))
                    pb = fill(f"d.cu{g}", i)
                    w = 2 * M
                    pe.matmul(pb, causal, EM[:, 4 * g:4 * g + 4, :].rearrange("p a b -> p (a b)"), start=True, stop=True)
                    odd = pb.rearrange("p (a b) -> p a b", a=4)[:, 1:4:2, :]
                    full(pe.matmul(odd, ones, EM[:, 4 * g:4 * g + 4:2, :], start=False, stop=True, skip_group_check=True),
                         f"d.cu{g}")
                for g in range(2):
                    pb = fill(f"d.et{g}", i)
                    for j in range(4):
                        last = pe.transpose(pb[:, j * P:(j + 1) * P], EM[:, 4 * g + j, :], ident)
                    full(last, f"d.et{g}")
                pe.wait_ge(loaded_wg, i * 16 + 16)
                project("d.g", range(4), wg[:], 2 * DV, i)

                pe.wait_ge(loaded_comp, i * (16 * 7) + 16 * 7)
                pb = fill("d.wot", i)
                for h in range(2):
                    for a in range(2):
                        last = pe.transpose(pb[:, h * D + a * P:h * D + (a + 1) * P], xwo[:, a, h * P:(h + 1) * P], ident)
                full(last, "d.wot")

                def weights_u(h):
                    pb = fill(f"d.u{h}", i)
                    for a in range(2):
                        last = pe.matmul(pb[0:QC, a * D:(a + 1) * D], xkq[:, h, a * QC:(a + 1) * QC], xwq[:, h, :],
                                         start=True, stop=True)
                    full(last, f"d.u{h}")

                def weights_v():
                    evac("d.u0", i)
                    evac("d.u1", i)
                    pb = fill("d.V", i)
                    for h in range(2):
                        for a in range(2):
                            last = pe.matmul(pb[h * R:(h + 1) * R, 0:D], xqr[:, a, h, :], U[:, h, a, :],
                                             start=(a == 0), stop=(a == 1))
                    full(last, "d.V")

                def weights_t():
                    assert banks.bank("d.bt4") == banks.bank("d.w2")
                    evac("d.V", i)
                    for h in range(2):
                        pb = fill(f"d.T{h}", i)
                        for c in range(C):
                            last = pe.matmul(pb[:, c * DC:(c + 1) * DC], VE[h * R:(h + 1) * R, c * P:(c + 1) * P],
                                             KRT[h * R:(h + 1) * R, :], start=True, stop=True)
                        full(last, f"d.T{h}")

                def weights_2():
                    evac("d.wot", i)
                    pb = fill("d.w2", i)
                    for h in range(2):
                        pe.matmul(pb[h * DC:(h + 1) * DC, 0:D], xkv[:, h, :], WOTe[:, h, :], start=True, stop=True)
                    full(pe.transpose(pb[:, D:D + DC], xkr.rearrange("p a b -> p (a b)"), ident[0:DC, 0:DC]), "d.w2")

                def pairwise(name, j, left, right):
                    b, h = j // 2, j % 2
                    rows = slice(h * M, (h + 1) * M)
                    pb = fill(f"d.{name}{j}", i)
                    pe.matmul(pb[:, 0:2 * P], left[rows, tile(b * TB)], right[rows, b * S:(b + 1) * S], start=True, stop=True)
                    full(pe.matmul(pb[:, 2 * P:3 * P], left[rows, tile(b * TB + 1)], right[rows, tile(b * TB + 1)],
                                   start=True, stop=True), f"d.{name}{j}")

                def apply(pb, at_col, a, n, rhs):
                    w = rhs(n).shape[-1]
                    dst = pb[:, at_col:at_col + w]
                    if n % TB == 0:
                        return pe.matmul(dst, a[:, 0:P], rhs(n), start=True, stop=True)
                    pe.matmul(dst, a[:, P:2 * P], rhs(n - 1), start=True, stop=False)
                    return pe.matmul(dst, a[:, 2 * P:3 * P], rhs(n), start=False, stop=True)

                def slots(g):
                    pb = fill(f"d.ok{g}", i)
                    for j in range(4):
                        evac(f"d.at{4 * g + j}", i)
                    for n in range(4):
                        for h in range(2):
                            last = apply(pb, n * 2 * M + h * M, ATd[:, (n // TB) * 2 + h, :], 4 * g + n,
                                         lambda m: EM[:, m, h * M:(h + 1) * M])
                    full(last, f"d.ok{g}")

                def slots_T(g):
                    pb = fill(f"d.pt{g}", i)
                    pe.wait_ge(p_ready, i * 2 + (g + 1))
                    for j in range(4):
                        last = pe.transpose(pb[:, j * P:(j + 1) * P], PM[:, 4 * g + j, :], ident)
                    full(last, f"d.pt{g}")

                def values(b):
                    pb = fill(f"d.o{b}", i)
                    evac(f"d.bt{2 * b}", i)
                    evac(f"d.bt{2 * b + 1}", i)
                    for n in range(TB):
                        for h in range(2):
                            last = apply(pb, (n * 2 + h) * DV, BTd[:, (b % 2) * 2 + h, :], b * TB + n,
                                         lambda m: VD[:, m, h * DV:(h + 1) * DV])
                    full(last, f"d.o{b}")

                def outputs_T(b):
                    pb = fill(f"d.ot{b}", i)
                    evac(f"d.o{b}", i)
                    for h in range(2):
                        for n in range(TB):
                            last = pe.transpose(pb[:, h * S + n * P:h * S + (n + 1) * P],
                                                OD[:, b * TB + n, h * DV:(h + 1) * DV], ident)
                    full(last, f"d.ot{b}")

                for n, name in enumerate(("q0", "q1", "k0", "k1", "v0", "v1")):
                    next_in_bank = ("et0", "et1", "g0", "g1", "g2", "g3")[n]
                    assert banks.bank("d." + name) == banks.bank("d." + next_in_bank)
                evac("d.et0", i)
                evac("d.et1", i)
                for g in range(2):
                    for j in range(4 * g, 4 * g + 4):
                        pairwise("at", j, kT, qT)
                    weights_u(g)
                    project("d.v", [2 + g], wsv[:, :, 2 * M:], 2 * DV, i)
                    slots(g)
                for g in range(2):
                    slots_T(g)
                    if g == 0:
                        weights_2()
                    if g == 1:
                        values(1)
                    evac(f"d.pt{g}", i)
                    for j in range(4 * g, 4 * g + 4):
                        pairwise("bt", j, ET, PT)
                    if g == 0:
                        values(0)
                    else:
                        outputs_T(0)
                        outputs_T(1)
                        weights_v()
                        values(2)
                        weights_t()
                        values(3)
                        if not last_trip:
                            pe.wait_ge(loaded_wsv, i * 32 + 64)
                            project("d.s", range(2), wsv[:, :, 0:2 * M], 2 * M, i)
                        outputs_T(2)
                        outputs_T(3)

            pe.wait_ge(loaded_wsv, 32)
            project("first_s", range(2), wsv[:, :, 0:2 * M], 2 * M)
            with pe.Fori(0, PAIRS - 1) as i:
                slot_attention_trip(i)
            slot_attention_trip(PAIRS - 1, last_trip=True)

            pe.wait_ge(wo_scaled, 1)

            def slots_project_out(b):
                pb = fill(f"dx{b}")
                if b == 0:
                    for j in range(B):
                        evac(f"d.ot{j}", PAIRS - 1)
                for n in range(TB):
                    for h in range(H):
                        last = pe.matmul(pb[:, n * D:(n + 1) * D], OT[:, h // 2, h % 2, tile(b * TB + n)], WO[:, h, :],
                                         start=(h == 0), stop=(h == H - 1))
                full(last, f"dx{b}")

            for b in range(3):
                slots_project_out(b)

            layer_norm_T(4, (0, 1))
            slots_project_out(3)
            layer_norm_T(4, (2,))
            evac("kr0")
            evac("kr1")

            def context_queries(name, half, i=0):
                pb = fill(f"{name}{half}", i)
                for c in range(C):
                    last = pe.matmul(pb, Tcur[:, c, :], HT[:, c, half * HALF:(half + 1) * HALF],
                                     start=(c == 0), stop=(c == C - 1))
                full(last, f"{name}{half}")

            def context_attention_trip(i, last_trip=False):

                def e_scores(b, h):
                    name = f"e.sc{b}{h}"
                    pb = fill(name, i)
                    if h == 0 and b % 2 == 0:
                        pe.wait_ge(evacuated[banks.bank(f"e.q{b // 2}")], banks.after_previous(f"e.q{b // 2}", i))
                    rows = slice(h * DC, (h + 1) * DC)
                    for n in range(TB):
                        last = pe.matmul(pb[:, n * S:(n + 1) * S], QE[rows, tile(b * TB + n)], krT[rows, b * S:(b + 1) * S],
                                         start=True, stop=True)
                    full(last, name)

                def e_probs_T(b, h):
                    name = f"e.pt{b}{h}"
                    pb = fill(name, i)
                    evac(f"e.sc{b}{h}", i)
                    for c in range(TB):
                        for n in range(TB):
                            last = pe.transpose(pb[:, c * S + n * P:c * S + (n + 1) * P],
                                                PX[:, b % 2, h, n, c * P:(c + 1) * P], ident)
                    full(last, name)

                def e_context(b):
                    name = f"e.cx{b}"
                    pb = fill(name, i)
                    evac(f"e.pt{b}0", i)
                    evac(f"e.pt{b}1", i)
                    for n in range(TB):
                        for h in range(2):
                            for c in range(TB):
                                last = pe.matmul(pb[:, (n * 2 + h) * DC:(n * 2 + h + 1) * DC],
                                                 PXT[:, b % 2, h, c, n * P:(n + 1) * P], kr[:, b * TB + c, 0, :],
                                                 start=(c == 0), stop=(c == TB - 1))
                    full(last, name)

                def e_context_T(b):
                    name = f"e.ct{b}"
                    pb = fill(name, i)
                    evac(f"e.cx{b}", i)
                    for n in range(TB):
                        last = pe.transpose(pb[:, n * P:(n + 1) * P], CX[:, b * TB + n, :, :].rearrange("p a b -> p (a b)"), ident)
                    full(last, name)

                e_step = {"sc": e_scores, "pt": e_probs_T, "cx": e_context, "ct": e_context_T}
                for name in E_BODY:
                    if name[2:3] == "q":
                        if not last_trip:
                            if name == "e.q0":
                                pe.wait_ge(loaded_T, i * 16 + 32)
                            context_queries("e.q", int(name[3]), i)
                    elif name[2:4] in e_step:
                        e_step[name[2:4]](*(int(x) for x in name[4:]))

            pe.wait_ge(loaded_T, 16)
            evac("ht4_0")
            evac("ht4_1")
            context_queries("first_q", 0)
            layer_norm_T(4, (3,))
            evac("ht4_2")
            evac("ht4_3")
            context_queries("first_q", 1)
            for half in range(2):
                evac(f"first_q{half}")
            with pe.Fori(0, PAIRS - 1) as i:
                context_attention_trip(i)
            context_attention_trip(PAIRS - 1, last_trip=True)

            def context_project_out(b):
                pb = fill(f"ex{b}")
                if b == 0:
                    for j in range(B):
                        evac(f"e.ct{j}", PAIRS - 1)
                for n in range(TB):
                    for p in range(PAIRS):
                        last = pe.matmul(pb[:, n * D:(n + 1) * D], CT[:, p, tile(b * TB + n)], W2[:, p, :],
                                         start=(p == 0), stop=(p == PAIRS - 1))
                full(last, f"ex{b}")

            for b in range(3):
                context_project_out(b)

            layer_norm_T(5, (0, 1))
            context_project_out(3)
            layer_norm_T(5, (2, 3))
            pe.wait_ge(loaded_router, 16 * 4)
            pb = fill("lg")
            for n in range(NT):
                if n % TB == 0:
                    evac(f"ht5_{n // TB}")
                for c in range(C):
                    last = pe.matmul(pb[:, n * E:(n + 1) * E], HT[:, c, tile(n)], wr[:, c, :], start=(c == 0), stop=(c == C - 1))
            full(last, "lg")

            def start_sums():
                pe.wait_ge(shares_ready, 1)
                for half in range(2):
                    pb = fill(f"cb{half}")
                    for j in range(4):
                        last = pe.transpose(pb[0:NE, j * P:(j + 1) * P], CB[:, half * 4 + j, :], ident)
                    full(last, f"cb{half}")
                evac("cb0")
                evac("cb1")
                for b in range(B):
                    pb = fill(f"acc{b}")
                    for n in range(TB):
                        last = pe.matmul(pb[:, n * D:(n + 1) * D], CBT[:, tile(b * TB + n)], b2, start=(n == 0), stop=True,
                                         skip_group_check=True)

            def experts_trip(i, first_trip=False):
                for e in range(2):
                    pe.wait_ge(loaded_fin[e], i * 64 + 64)
                    for x, w in (("g", fg), ("u", fu)):
                        for half in range(2):
                            name = f"f.{x}{half}{e}"
                            pb = fill(name, i)
                            for c in range(C):
                                last = pe.matmul(pb, w[:, e, c, :], HT[:, c, half * HALF:(half + 1) * HALF],
                                                 start=(c == 0), stop=(c == C - 1))
                            full(last, name)
                    if first_trip and e == 0:
                        start_sums()
                for e in range(2):
                    pe.wait_ge(loaded_fout[e], i * 16 + 16)
                    for half in range(2):
                        pe.wait_ge(yc_ready, i * 4 + (2 * e + half + 1))
                        for n in range(4 * half, 4 * half + 4):
                            b = n // TB
                            last = pe.matmul(ps[:, banks.bank(f"acc{b}"), (n % TB) * D:(n % TB + 1) * D], YC[:, e, tile(n)],
                                             fo[:, e, :], start=False, stop=True, skip_group_check=True)
                    last.then_inc(expert_out[e], 1)

            experts_trip(0, first_trip=True)
            with pe.Fori(0, F_TRIPS - 1) as i:
                experts_trip(i + 1)

        @block.scalar
        def _(act):
            own = Steps(act, act_steps)

            def full(name, i=0):
                act.wait_ge(filled[banks.bank(name)], banks.after(name, i))
                return ps[:, banks.bank(name), :]

            def evac(ins, name, i=0):
                own.mark(ins, evacuated[banks.bank(name)], banks.after(name, i))

            roots, norms = [0], [0]

            def inverse_root(batches=range(B)):
                roots[0] += 1
                tt = slice(batches[0] * TB, (batches[-1] + 1) * TB)
                act.wait_ge(var_ready, roots[0])
                own.step(act.activation(nt[:, tt], ve[:, tt], ACT.Ln))
                own.settle()
                own.mark(act.activation(guess[:, tt], nt[:, tt], ACT.Exp, scale=-0.5), guess_ready, roots[0])

            def normalize_odd(k, batches=range(B)):
                norms[0] += 1
                act.wait_ge(nmr_ready, norms[0])
                for b in batches:
                    n = 2 * b + 1
                    own.mark(act.activation(HN[:, n, :], X[:, n, :], ACT.Identity, bias=nmr[:, n:n + 1],
                                              scale=rstd[:, n:n + 1]), h_odd, k * B + b + 1)

            def evac_ht(k, dst, batches=range(1, B, 2), bf16=False):
                for b in batches:
                    pb = full(f"ht{k}_{b}")
                    pb = pb.bitcast(BF16) if bf16 else pb
                    src = pb[:, 0:C * S].rearrange("p (c s) -> p c s", c=C)
                    evac(act.copy(dst[:, :, b * S:(b + 1) * S], src), f"ht{k}_{b}")

            act.wait_ge(loaded_a, 16 * 7)
            own.mark(act.activation(gg[:, 0:1], gg[:, 0:1], ACT.Sigmoid), gate_ready, 1)
            act.preload_act_table_set("natural_log_exp_and_others")
            inverse_root()
            for half, name in enumerate(("w0", "w1")):
                evac(act.copy(WT[:, half * 4:half * 4 + 4, :].rearrange("p a b -> p (a b)"), full(name)), name)
            for half, name in enumerate(("ctx0", "ctx1")):
                evac(act.copy(ctxT[0:DC, half * HALF:(half + 1) * HALF], full(name)[0:DC, :]), name)
            evac(act.copy(wkT[0:DC, :], full("wk")[0:DC, 0:DC]), "wk")
            normalize_odd(0)
            evac_ht(0, HT)
            for n in range(4):
                act.wait_ge(amin_ready, n + 1)
                own.mark(act.activation(amin[:, n, :], amin[:, n, :], ACT.Exp), aexp_ready, n + 1)
            for half in range(2):
                evac(act.copy(VV[:, half * 4:half * 4 + 4, 0:DA],
                              full(f"av{half}").rearrange("p (n d) -> p n d", n=4)), f"av{half}")
            for half in range(2):
                evac(act.copy(kvT[:, half * HALF:(half + 1) * HALF], full(f"kvT{half}")[0:DC, :]), f"kvT{half}")
            evac(act.copy(kvn.rearrange("p a b -> p (a b)"), full("kv")), "kv")
            evac(act.copy(WQT.rearrange("p a b -> p (a b)"), full("wqT").bitcast(BF16)[:, 0:C * D]), "wqT")
            for b in range(B):
                evac(act.copy(AOT[:, b * S:(b + 1) * S], full(f"ao{b}")[:, 0:S]), f"ao{b}")
            for half in range(2):
                evac(act.copy(krT[:, half * HALF:(half + 1) * HALF], full(f"kr{half}")), f"kr{half}")

            inverse_root()
            normalize_odd(1)
            evac_ht(1, HT)
            for b in range(B):
                evac(act.mul(BO[:, b * S:(b + 1) * S], full(f"bo{b}")[0:DC, 0:S], D ** -0.5), f"bo{b}")
            inverse_root()
            for n in range(NT):
                act.wait_ge(simmax_ready, n // TB + 1)
                own.mark(act.activation(SIM[:, n, :], SIM[:, n, :], ACT.Exp, bias=col[:, NT + n:NT + n + 1],
                                          accum_out=col[:, 2 * NT + n:2 * NT + n + 1]), simexp_ready, n + 1)
            inverse_root()
            normalize_odd(2)
            evac_ht(2, XQT, range(B), bf16=True)
            inverse_root()
            normalize_odd(3)
            evac_ht(3, HT)

            def exp_s(name, i, trip):
                for g in range(2):
                    act.wait_ge(evacuated[banks.bank(f"{name}{g}")], banks.after(f"{name}{g}", i))
                    em = EM[:, 4 * g:4 * g + 4, :]
                    own.mark(act.activation(em, em, ACT.Exp), em_exp, trip * 2 + (g + 1))

            def slot_attention_trip(i, last_trip=False):
                for half in range(2):
                    evac(act.copy(qT[:, half * HALF:(half + 1) * HALF], full(f"d.q{half}", i)), f"d.q{half}", i)

                def values_out(b):
                    evac(act.copy(VD[:, b * TB:(b + 1) * TB, :].rearrange("p a b -> p (a b)"), full(f"d.v{b}", i)), f"d.v{b}", i)

                values_out(0)
                values_out(1)
                for g in range(2):
                    rc = RC[:, 4 * g:4 * g + 4, :].rearrange("p a b -> p (a b)")
                    evac(act.activation(rc, full(f"d.cu{g}", i), ACT.Ln), f"d.cu{g}", i)
                own.settle()
                for g in range(2):
                    rc = RC[:, 4 * g:4 * g + 4, :].rearrange("p a b -> p (a b)")
                    own.mark(act.activation(rc, rc, ACT.Exp, scale=-1.0), rc_ready, i * 2 + (g + 1))
                for b in range(B):
                    sg = SG[:, b * TB:(b + 1) * TB, :].rearrange("p a b -> p (a b)")
                    evac(act.activation(sg, full(f"d.g{b}", i), ACT.Silu), f"d.g{b}", i)
                act.preload_act_table_set("natural_log_exp_and_others")
                evac(act.copy(WOTe.rearrange("p a b -> p (a b)"), full("d.wot", i)), "d.wot", i)

                def exp_slots(g):
                    act.wait_ge(ok_shifted, i * 2 + (g + 1))
                    pm = PM[:, 4 * g:4 * g + 4, :]
                    own.mark(act.activation(pm, pm, ACT.Exp, scale=M ** -0.5), ok_exp, i * 2 + (g + 1))

                def root_mean_squares(b):
                    pb = full(f"d.o{b}", i)
                    for j in range(4):
                        k = b * 4 + j
                        ins = act.activation(JUNK[:, j], pb[:, j * DV:(j + 1) * DV], ACT.Square, accum_out=sumsq[:, k:k + 1])
                        if j == 3:
                            own.mark(ins, sumsq_ready, i * B + (b + 1))
                        else:
                            own.step(ins)
                    act.wait_ge(rmsv_ready, i * B + (b + 1))
                    sl = slice(4 * b, 4 * b + 4)
                    own.step(act.activation(rmsl[:, sl], rmsv[:, sl], ACT.Ln))
                    own.settle()
                    own.mark(act.activation(rmsl[:, sl], rmsl[:, sl], ACT.Exp, scale=-0.5), rms_guess, i * B + (b + 1))

                def outputs_T(b):
                    dst = OT[:, ds(i, 1), :, b * S:(b + 1) * S].rearrange("p i h s -> p (i h) s")
                    evac(act.copy(dst, full(f"d.ot{b}", i).rearrange("p (h s) -> p h s", h=2)), f"d.ot{b}", i)

                evac(act.copy(U[:, 0, :, :].rearrange("p a b -> p (a b)"), full("d.u0", i)[0:QC, :]), "d.u0", i)
                values_out(2)
                exp_slots(0)
                evac(act.copy(U[:, 1, :, :].rearrange("p a b -> p (a b)"), full("d.u1", i)[0:QC, :]), "d.u1", i)
                values_out(3)
                evac(act.copy(PT[:, 0:HALF], full("d.pt0", i)), "d.pt0", i)
                exp_slots(1)
                w2 = W2[:, ds(i, 1), :].rearrange("p i n -> p (i n)")
                own.step(act.copy(w2, full("d.w2", i)[:, 0:D]))
                evac(act.copy(KRT, full("d.w2", i)[:, D:D + DC]), "d.w2", i)
                root_mean_squares(0)
                evac(act.copy(PT[:, HALF:], full("d.pt1", i)), "d.pt1", i)
                root_mean_squares(1)
                outputs_T(0)
                outputs_T(1)
                evac(act.copy(VE, full("d.V", i)[:, 0:D]), "d.V", i)
                root_mean_squares(2)
                root_mean_squares(3)
                if not last_trip:
                    exp_s("d.s", i, i + 1)
                for h in range(2):
                    dst = Tall[:, ds(i, 1), :, h * DC:(h + 1) * DC].rearrange("p i c n -> p (i c) n")
                    src = full(f"d.T{h}", i)[:, 0:C * DC].rearrange("p (c n) -> p c n", c=C)
                    evac(act.copy(dst, src), f"d.T{h}", i)
                outputs_T(2)
                outputs_T(3)

            exp_s("first_s", 0, 0)
            act.preload_act_table_set("natural_log_exp_and_others")
            with act.Fori(0, PAIRS - 1) as i:
                own.enter(i, 1 + 4 * 4)
                slot_attention_trip(i)
                own.leave(PAIRS - 1)
            slot_attention_trip(PAIRS - 1, last_trip=True)

            def normalize(k):
                for batches in ((0, 1), (2,), (3,)):
                    inverse_root(batches)
                    normalize_odd(k, batches)
                    evac_ht(k, HT, [b for b in batches if b % 2])

            normalize(4)
            evac(act.copy(QE[:, 0:HALF], full("first_q0")), "first_q0")

            def context_attention_trip(i, last_trip=False):
                def e_exp(b, h):
                    pb = full(f"e.sc{b}{h}", i)
                    act.wait_ge(emax_ready, i * 8 + (2 * b + h + 1))
                    for n in range(TB):
                        k = b * TB + n
                        ins = act.activation(PX[:, b % 2, h, n, :], pb[:, n * S:(n + 1) * S], ACT.Exp, bias=nmx[:, k, h:h + 1],
                                             accum_out=esum[:, k, h:h + 1])
                        if n == TB - 1:
                            evac(ins, f"e.sc{b}{h}", i)
                        else:
                            own.step(ins)

                for name in E_BODY:
                    kind, at_ = name[2:4], name[4:]
                    if kind == "sc":
                        e_exp(int(at_[0]), int(at_[1]))
                    elif kind == "pt" and at_[1] == "0":
                        b = int(at_[0])
                        evac(act.copy(PXT[:, b % 2, 0, :, :].rearrange("p a b -> p (a b)"), full(name, i)), name, i)
                    elif kind == "ct":
                        b = int(at_)
                        dst = CT[:, ds(i, 1), b * S:(b + 1) * S].rearrange("p i s -> p (i s)")
                        evac(act.copy(dst, full(name, i)[:, 0:S]), name, i)
                    elif kind == "q0" and not last_trip:
                        evac(act.copy(QE[:, 0:HALF], full(name, i)), name, i)

            with act.Fori(0, PAIRS - 1) as i:
                own.enter(i, 8)
                context_attention_trip(i)
                own.leave(PAIRS - 1)
            context_attention_trip(PAIRS - 1, last_trip=True)

            normalize(5)
            evac(act.activation(AFF.rearrange("p a b -> p (a b)"), full("lg")[:, 0:NT * E], ACT.Sigmoid), "lg")
            with act.Fori(0, F_TRIPS) as i:
                for e in range(2):
                    act.wait_ge(loaded_fin[e], i * 64 + 64)
                    for half in range(2):
                        name = f"f.g{half}{e}"
                        evac(act.activation(Y[:, e, half * HALF:(half + 1) * HALF], full(name, i), ACT.Gelu,
                                            bias=fgb[:, e]), name, i)

        @block.gpsimd
        def _(pool):
            pool.memset(ctxT[DC:DC + 1, :], 1.0).then_inc(ones_ready, 1)
            pool.wait_ge(ones_ready, 1)
            pool.memset(VV[:, :, DA:DA + 1], 1.0).then_inc(ones_ready, 1)
            pool.wait_ge(loaded_wo, 32)
            pool.tensor_scalar(WO, WO, gnorm[:, 0:1], None, ALU.mult).then_inc(wo_scaled, 1)

        @block.vector
        def _(dve):
            own = Steps(dve, dve_steps)

            def full(name, i=0):
                dve.wait_ge(filled[banks.bank(name)], banks.after(name, i))
                return ps[:, banks.bank(name), :]

            def evac(ins, name, i=0):
                own.mark(ins, evacuated[banks.bank(name)], banks.after(name, i))

            roots, norms = [0], [0]

            def inverse_root(eps, batches=range(B)):
                roots[0] += 1
                tt = slice(batches[0] * TB, (batches[-1] + 1) * TB)
                v, g, r = ve[:, tt], guess[:, tt], rstd[:, tt]
                own.settle()
                own.mark(dve.tensor_scalar(v, mv[:, tt, 1], eps, None, ALU.add), var_ready, roots[0])
                dve.wait_ge(guess_ready, roots[0])
                own.step(dve.tensor_tensor(r, g, g, ALU.mult))
                own.settle()
                own.step(dve.tensor_tensor(r, r, v, ALU.mult))
                own.settle()
                own.step(dve.tensor_scalar(r, r, -0.5, 1.5, ALU.mult, ALU.add))
                own.settle()
                own.step(dve.tensor_tensor(r, r, g, ALU.mult))
                own.settle()

            def layer_norm(k, batches=range(B)):
                norms[0] += 1
                tt = slice(batches[0] * TB, (batches[-1] + 1) * TB)
                for n in range(tt.start, tt.stop):
                    own.step(dve.bn_stats(st6[:, n, :], X[:, n, :]))
                own.settle()
                for n in range(tt.start, tt.stop):
                    own.step(dve.bn_aggr(mv[:, n, :], st6[:, n, :]))
                inverse_root(EPS_LN, batches)
                own.mark(dve.scalar_tensor_tensor(out=nmr[:, tt], in0=mv[:, tt, 0], scalar=-1.0, in1=rstd[:, tt],
                                                    op0=ALU.mult, op1=ALU.mult), nmr_ready, norms[0])
                own.settle()
                for b in batches:
                    n = 2 * b
                    own.mark(dve.tensor_scalar(HN[:, n, :], X[:, n, :], rstd[:, n:n + 1], nmr[:, n:n + 1],
                                                 ALU.mult, ALU.add), h_even, k * B + b + 1)

            def evac_ht(k, dst, batches=range(0, B, 2)):
                for b in batches:
                    src = full(f"ht{k}_{b}")[:, 0:C * S].rearrange("p (c s) -> p c s", c=C)
                    evac(dve.tensor_copy(dst[:, :, b * S:(b + 1) * S], src), f"ht{k}_{b}")

            dve.wait_ge(loaded_x, 16)
            layer_norm(0)
            dve.wait_ge(loaded_const, 16)
            own.mark(dve.tensor_copy(identb[:], ident), identb_ready, 1)
            dve.wait_ge(loaded_ctx, 16 * 4)
            hd = DC // 2
            cv = ctxn.rearrange("p (b n) d -> p b n d", b=B)
            rv = ropet.rearrange("p (b n) d -> p b n d", b=B)
            for n in range(TB):
                for lo, hi in ((0, hd), (hd, DC)):
                    src = (lo + hd) % DC
                    own.step(dve.tensor_tensor(rv[:, :, n, lo:hi], cv[:, :, n, src:src + hd],
                                               rope[:, 1:2, n, lo:hi].to_broadcast([P, B, hd]), ALU.mult))
            krv = kr[:].rearrange("p (b n) a d -> p b n a d", b=B)
            for n in range(TB):
                own.step(dve.tensor_tensor(krv[:, :, n, 0, :], cv[:, :, n, :],
                                           rope[:, 0:1, n, :].to_broadcast([P, B, DC]), ALU.mult))
            own.settle()
            own.step(dve.tensor_tensor(kr[:, :, 0, :], kr[:, :, 0, :], ropet, ALU.add))
            own.settle()
            own.mark(dve.tensor_copy(kr[:, :, 1, :], kr[:, :, 0, :]), kr_ready, 1)
            evac_ht(0, HT)
            for n in range(4):
                name = f"a{'qk'[n // 2]}{n % 2}"
                own.mark(dve.tensor_scalar(amin[:, n, :], full(name), 0.0, None, ALU.min), amin_ready, n + 1)
            for n in range(4):
                name = f"a{'qk'[n // 2]}{n % 2}"
                dve.wait_ge(aexp_ready, n + 1)
                dst = (SQ, SK)[n // 2][:, (n % 2) * HALF:(n % 2 + 1) * HALF]
                evac(dve.scalar_tensor_tensor(out=dst, in0=full(name), scalar=0.0, in1=amin[:, n, :],
                                              op0=ALU.max, op1=ALU.add), name)
            dve.wait_ge(loaded_c, 16)
            own.mark(dve.tensor_reduce(col[:, 0:1], wf, AX.XY, ALU.add, apply_absolute_value=True), wabs_ready, 1)
            evac(dve.tensor_scalar(col[:, 1:2], full("wsum")[:, 0:1], 1.0 / (D * D), 1e-6, ALU.mult, ALU.max), "wsum")
            own.settle()
            own.step(dve.reciprocal(col[:, 2:3], col[:, 1:2]))
            own.settle()
            own.step(dve.tensor_scalar(wf, wf, col[:, 2:3], MAGIC, ALU.mult, ALU.add))
            own.settle()
            own.step(dve.tensor_scalar(wf, wf, -MAGIC, 1.0, ALU.add, ALU.min))
            own.settle()
            own.mark(dve.tensor_scalar(wq8, wf, -1.0, None, ALU.max), wq8_ready, 1)
            own.step(dve.tensor_scalar(col[:, 3:4], col[:, 1:2], 1.0 / 127.0, None, ALU.mult))
            dve.wait_ge(gate_ready, 1)
            own.step(dve.tensor_scalar(gg[:, 1:2], gg[:, 0:1], -1.0, 1.0, ALU.mult, ALU.add))
            own.settle()

            def mask_scores(b):
                evac(dve.tensor_tensor(AT[:, b % 2, :], full(f"at{b}")[:, 0:3 * P], mask3, ALU.mult), f"at{b}")

            def gated_output(n):
                pb = full(f"ml{n}")
                w = DA + 1
                den = col[:, 8 + 2 * n:10 + 2 * n]
                own.step(dve.tensor_scalar(den, pb[:, DA:2 * w:w], EPS_A, None, ALU.add))
                own.settle()
                own.step(dve.reciprocal(den, den))
                own.settle()
                own.step(dve.tensor_tensor(den, den, gg[:], ALU.mult))
                own.settle()
                own.step(dve.tensor_scalar(AO[:, n, :], pb[:, 0:DA], den[:, 0:1], None, ALU.mult))
                own.settle()
                evac(dve.scalar_tensor_tensor(out=AO[:, n, :], in0=pb[:, w:w + DA], scalar=den[:, 1:2],
                                              in1=AO[:, n, :], op0=ALU.mult, op1=ALU.add), f"ml{n}")

            def add_to_x(name, b):
                xb = X[:, b * TB:(b + 1) * TB, :].rearrange("p n d -> p (n d)")
                evac(dve.tensor_tensor(xb, full(name), xb, ALU.add), name)

            for name in A_ORDER:
                n = int(name[2:])
                if name[:2] == "at":
                    mask_scores(n)
                elif name[:2] == "ml":
                    gated_output(n)
                elif name[:2] == "ax":
                    add_to_x(name, n)

            own.settle()
            layer_norm(1)
            evac_ht(1, HT)
            for n in range(NT):
                own.step(dve.bn_stats(st6[:, n, :], full(f"bs{n // TB}")[:, (n % TB) * S:(n % TB + 1) * S]))
            own.settle()
            for n in range(NT):
                own.step(dve.bn_aggr(mv[:, n, :], st6[:, n, :]))
            inverse_root(EPS_SIM)
            dve.wait_ge(loaded_b, 32)
            for n in range(NT):
                ins = dve.tensor_scalar(SIM[:, n, :], full(f"bs{n // TB}")[:, (n % TB) * S:(n % TB + 1) * S],
                                        mv[:, n, 0:1], rstd[:, n:n + 1], ALU.subtract, ALU.mult)
                if n % TB == TB - 1:
                    evac(ins, f"bs{n // TB}")
                else:
                    own.step(ins)
            for b in range(B):
                sl = slice(b * TB, (b + 1) * TB)
                own.settle()
                own.step(dve.tensor_tensor(SIM[:, sl, :], SIM[:, sl, :],
                                           gamma.unsqueeze(1).to_broadcast([P, TB, D]), ALU.mult))
                own.settle()
                own.step(dve.tensor_tensor(SIM[:, sl, :], SIM[:, sl, :],
                                           beta.unsqueeze(1).to_broadcast([P, TB, D]), ALU.add))
                own.settle()
                own.mark(dve.tensor_reduce(col[:, NT + b * TB:NT + (b + 1) * TB], SIM[:, sl, :], AX.X, ALU.max,
                                             negate=True), simmax_ready, b + 1)
            for b in range(B):
                dve.wait_ge(simexp_ready, (b + 1) * TB)
                c0 = 2 * NT + b * TB
                own.step(dve.reciprocal(col[:, c0:c0 + TB], col[:, c0:c0 + TB]))
                own.settle()
                for n in range(b * TB, (b + 1) * TB):
                    own.step(dve.scalar_tensor_tensor(out=X[:, n, :], in0=SIM[:, n, :],
                                                      scalar=col[:, 2 * NT + n:2 * NT + n + 1], in1=X[:, n, :],
                                                      op0=ALU.mult, op1=ALU.add))
            own.settle()

            layer_norm(2)
            dve.wait_ge(h_odd, 3 * B)
            own.settle()
            amax = col[:, 4 * NT:5 * NT]
            qs = col[:, 5 * NT:6 * NT]
            own.step(dve.tensor_reduce(amax, HN[:], AX.X, ALU.max, apply_absolute_value=True))
            own.settle()
            own.step(dve.tensor_scalar(amax, amax, 1e-8, None, ALU.max))
            own.settle()
            own.step(dve.reciprocal(qs, amax))
            own.settle()
            own.step(dve.tensor_scalar(qs, qs, 127.0, None, ALU.mult))
            own.step(dve.tensor_scalar(amax, amax, col[:, 3:4], None, ALU.mult))
            own.settle()
            for n in range(NT):
                own.step(dve.tensor_scalar(HN[:, n, :], HN[:, n, :], qs[:, n:n + 1], MAGIC, ALU.mult, ALU.add))
            own.settle()
            own.step(dve.tensor_scalar(HN[:], HN[:], -MAGIC, 127.0, ALU.add, ALU.min))
            own.settle()
            own.mark(dve.tensor_scalar(XQ, HN[:], -127.0, None, ALU.max), xq_ready, 1)
            for b in range(B):
                for n in range(b * TB, (b + 1) * TB):
                    ins = dve.scalar_tensor_tensor(out=X[:, n, :], in0=full(f"cy{b}")[:, (n % TB) * D:(n % TB + 1) * D],
                                                   scalar=amax[:, n:n + 1], in1=X[:, n, :], op0=ALU.mult, op1=ALU.add)
                    if n % TB == TB - 1:
                        evac(ins, f"cy{b}")
                    else:
                        own.step(ins)
            own.settle()
            own.mark(dve.tensor_copy(col[:, 0:1], col[:, 1:2]), x_after_c, 1)

            layer_norm(3)
            evac_ht(3, HT)

            def clip_s(name, i=0):
                for g in range(2):
                    evac(dve.tensor_scalar(EM[:, 4 * g:4 * g + 4, :].rearrange("p a b -> p (a b)"), full(f"{name}{g}", i),
                                           32.0, -32.0, ALU.min, ALU.max), f"{name}{g}", i)

            def slot_attention_trip(i, last_trip=False):
                for half in range(2):
                    evac(dve.tensor_copy(kT[:, half * HALF:(half + 1) * HALF], full(f"d.k{half}", i)), f"d.k{half}", i)
                for g in range(2):
                    evac(dve.tensor_copy(ET[:, g * HALF:(g + 1) * HALF], full(f"d.et{g}", i)), f"d.et{g}", i)

                def mask(name, dst, j):
                    name = f"d.{name}{j}"
                    evac(dve.tensor_tensor(dst[:, j % 4, :], full(name, i)[:, 0:3 * P], mask3, ALU.mult), name, i)

                def softmax_in(g):
                    sl = slice(4 * g, 4 * g + 4)
                    pm = PM[:, sl, :].rearrange("p a b -> p (a b)")
                    heads = PM[:, sl, :].rearrange("p n (h m) -> p (n h) m", h=2)
                    mx = slotmax[:, 8 * g:8 * g + 8]
                    dve.wait_ge(rc_ready, i * 2 + (g + 1))
                    evac(dve.tensor_tensor(pm, full(f"d.ok{g}", i), RC[:, sl, :].rearrange("p a b -> p (a b)"), ALU.mult),
                         f"d.ok{g}", i)
                    own.settle()
                    own.step(dve.tensor_reduce(mx, heads, AX.X, ALU.max))
                    own.settle()
                    own.mark(dve.tensor_tensor(heads, heads, mx.unsqueeze(2).to_broadcast([P, 8, M]), ALU.subtract),
                               ok_shifted, i * 2 + (g + 1))

                def softmax_out(g):
                    sl = slice(4 * g, 4 * g + 4)
                    pm = PM[:, sl, :]
                    heads = pm.rearrange("p n (h m) -> p (n h) m", h=2)
                    s8 = slice(8 * g, 8 * g + 8)
                    dve.wait_ge(ok_exp, i * 2 + (g + 1))
                    own.step(dve.tensor_reduce(slotsum[:, s8], heads, AX.X, ALU.add))
                    own.settle()
                    own.mark(dve.tensor_tensor(pm, pm, RC[:, sl, :], ALU.mult), p_ready, i * 2 + (g + 1))
                    own.step(dve.reciprocal(rs[:, s8], slotsum[:, s8]))
                    own.settle()
                    own.step(dve.tensor_tensor(rs2[:, s8], rs[:, s8], rs[:, s8], ALU.mult))

                def gate_outputs(b):
                    s4 = slice(4 * b, 4 * b + 4)
                    dve.wait_ge(sumsq_ready, i * B + (b + 1))
                    own.step(dve.tensor_tensor(rmsv[:, s4], sumsq[:, s4], rs2[:, s4], ALU.mult))
                    own.settle()
                    own.mark(dve.tensor_scalar(rmsv[:, s4], rmsv[:, s4], 1.0 / DV, EPS_RMS, ALU.mult, ALU.add),
                             rmsv_ready, i * B + (b + 1))
                    dve.wait_ge(rms_guess, i * B + (b + 1))
                    own.step(dve.tensor_tensor(coef[:, s4], rmsl[:, s4], rs[:, s4], ALU.mult))
                    own.settle()
                    pb = full(f"d.o{b}", i)
                    for j in range(4):
                        n, h = b * TB + j // 2, j % 2
                        hv = slice(h * DV, (h + 1) * DV)
                        ins = dve.scalar_tensor_tensor(out=OD[:, n, hv], in0=pb[:, j * DV:(j + 1) * DV],
                                                       scalar=coef[:, b * 4 + j:b * 4 + j + 1], in1=SG[:, n, hv],
                                                       op0=ALU.mult, op1=ALU.mult)
                        if j == 3:
                            evac(ins, f"d.o{b}", i)
                        else:
                            own.step(ins)

                for j in range(4):
                    mask("at", ATd, j)
                softmax_in(0)
                for j in range(4, 8):
                    mask("at", ATd, j)
                softmax_out(0)
                softmax_in(1)
                for j in range(2):
                    mask("bt", BTd, j)
                softmax_out(1)
                for j in range(2, 4):
                    mask("bt", BTd, j)
                gate_outputs(0)
                gate_outputs(1)
                for j in range(4, 8):
                    mask("bt", BTd, j)
                gate_outputs(2)
                gate_outputs(3)
                if not last_trip:
                    clip_s("d.s", i)

            clip_s("first_s")
            with dve.Fori(0, PAIRS - 1) as i:
                own.enter(i, 2 * (1 + 3) + 4 * (2 + 3))
                slot_attention_trip(i)
                own.leave(PAIRS - 1)
            slot_attention_trip(PAIRS - 1, last_trip=True)

            def add_and_normalize(step, k):
                for batches in ((0, 1), (2,), (3,)):
                    for b in batches:
                        add_to_x(f"{step}{b}", b)
                    own.settle()
                    layer_norm(k, batches)
                    evac_ht(k, HT, [b for b in batches if b == 0])
                evac_ht(k, HT, (2,))

            add_and_normalize("dx", 4)
            own.mark(dve.tensor_copy(col[:, 0:1], col[:, 1:2]), x_after_d, 1)

            evac(dve.tensor_copy(QE[:, HALF:], full("first_q1")), "first_q1")

            def context_attention_trip(i, last_trip=False):
                for name in E_BODY:
                    kind, at_ = name[2:4], name[4:]
                    b = int(at_[0]) if at_ else None
                    if kind == "sc":
                        h = int(at_[1])
                        own.mark(dve.tensor_reduce(nmx[:, b * TB:(b + 1) * TB, h], full(name, i).rearrange("p (n s) -> p n s", n=TB),
                                                     AX.X, ALU.max, negate=True), emax_ready, i * 8 + (2 * b + h + 1))
                    elif kind == "pt" and at_[1] == "1":
                        evac(dve.tensor_copy(PXT[:, b % 2, 1, :, :].rearrange("p a b -> p (a b)"), full(name, i)), name, i)
                    elif kind == "cx":
                        es = esum[:, b * TB:(b + 1) * TB, :].rearrange("p n h -> p (n h)")
                        for h in range(2):
                            dve.wait_ge(evacuated[banks.bank(f"e.sc{b}{h}")], banks.after(f"e.sc{b}{h}", i))
                        own.step(dve.reciprocal(es, es))
                        own.settle()
                        dst = CX[:, b * TB:(b + 1) * TB, :, :].rearrange("p n h c -> p (n h) c")
                        evac(dve.tensor_tensor(dst, full(name, i)[:, 0:4 * DC].rearrange("p (n c) -> p n c", n=4),
                                               es.unsqueeze(2).to_broadcast([P, 4, DC]), ALU.mult), name, i)
                    elif kind == "q1" and not last_trip:
                        evac(dve.tensor_copy(QE[:, HALF:], full(name, i)), name, i)

            with dve.Fori(0, PAIRS - 1) as i:
                own.enter(i, 4)
                context_attention_trip(i)
                own.leave(PAIRS - 1)
            context_attention_trip(PAIRS - 1, last_trip=True)
            add_and_normalize("ex", 5)

            dve.wait_ge(loaded_router, 16 * 4)
            dve.wait_ge(evacuated[banks.bank("lg")], banks.after("lg"))
            revb = rev.unsqueeze(1).to_broadcast([P, NT, E])
            bcast = lambda v: v.unsqueeze(2).to_broadcast([P, NT, E])
            src = AFF
            for k in range(2):
                best, first = tk[:, 2 * k, :], tk[:, 2 * k + 1, :]
                pick = TK[:, k, :, :]
                own.step(dve.tensor_reduce(best, src, AX.X, ALU.max))
                own.settle()
                own.step(dve.tensor_tensor(pick, src, bcast(best), ALU.is_equal))
                own.settle()
                own.step(dve.tensor_tensor(pick, pick, revb, ALU.mult))
                own.settle()
                own.step(dve.tensor_reduce(first, pick, AX.X, ALU.max))
                own.settle()
                own.step(dve.tensor_tensor(pick, pick, bcast(first), ALU.is_equal))
                own.settle()
                if k == 0:
                    own.step(dve.scalar_tensor_tensor(out=TK[:, 2, :, :], in0=pick, scalar=-4.0, in1=AFF, op0=ALU.mult,
                                                      op1=ALU.add))
                    own.settle()
                    src = TK[:, 2, :, :]
            own.step(dve.tensor_tensor(tk[:, 4, :], tk[:, 0, :], tk[:, 2, :], ALU.add))
            own.settle()
            own.step(dve.reciprocal(tk[:, 4, :], tk[:, 4, :]))
            own.settle()
            for k in range(2):
                own.step(dve.tensor_tensor(tk[:, 2 * k, :], tk[:, 2 * k, :], tk[:, 4, :], ALU.mult))
            own.settle()
            for k in range(2):
                own.step(dve.tensor_tensor(TK[:, k, :, :], TK[:, k, :, :], bcast(tk[:, 2 * k, :]), ALU.mult))
            own.step(dve.memset(CB[:, :, E:NE], 1.0))
            own.settle()
            own.mark(dve.tensor_tensor(CB[:, :, 0:E], TK[:, 0, :, :], TK[:, 1, :, :], ALU.add), shares_ready, 1)
            evac(dve.tensor_copy(CBT[:, 0:HALF], full("cb0")[0:NE, :]), "cb0")
            evac(dve.tensor_copy(CBT[:, HALF:], full("cb1")[0:NE, :]), "cb1")
            own.settle()
            own.mark(dve.tensor_copy(col[:, 0:1], col[:, 1:2]), comb_ready, 1)
            own.step(dve.tensor_tensor(X[:], X[:], HN[:], ALU.add))
            with dve.Fori(0, F_TRIPS) as i:
                for e in range(2):
                    dve.wait_ge(loaded_fin[e], i * 64 + 64)
                    for half in range(2):
                        sl = slice(half * HALF, (half + 1) * HALF)
                        g_name, name = f"f.g{half}{e}", f"f.u{half}{e}"
                        dve.wait_ge(evacuated[banks.bank(g_name)], banks.after(g_name, i))
                        evac(dve.scalar_tensor_tensor(out=YC[:, e, sl], in0=full(name, i), scalar=fub[:, e], in1=Y[:, e, sl],
                                                      op0=ALU.add, op1=ALU.mult), name, i)
                        if half == 0:
                            dve.wait_ge(loaded_bc[e], i * 16 + 16)
                        own.settle()
                        own.mark(dve.tensor_tensor(YC[:, e, sl], YC[:, e, sl], BC[:, e, sl], ALU.mult), yc_ready,
                                   i * 4 + (2 * e + half + 1))
            dve.wait_ge(expert_out[1], F_TRIPS)
            for b in range(B):
                xb = X[:, b * TB:(b + 1) * TB, :].rearrange("p n d -> p (n d)")
                own.step(dve.tensor_tensor(xb, ps[:, banks.bank(f"acc{b}"), :], xb, ALU.add))
            own.settle()
            own.mark(dve.tensor_copy(col[:, 0:1], col[:, 1:2]), x_final, 1)


def constants(ctx_shape, experts):
    _, length, dim = ctx_shape
    i = np.arange(P)
    ident = (i[:, None] == i[None, :]).astype(np.float32)
    causal = (i[:, None] <= i[None, :]).astype(np.float32)
    const = np.concatenate([ident, causal, np.ones((P, P), np.float32), causal], axis=1)
    one = np.float32(1.0)
    inv = one / np.float32(10000.0) ** (np.arange(0, dim, 2, dtype=np.float32) / np.float32(dim))
    freqs = np.arange(length, dtype=np.float32)[:, None] * inv[None, :].astype(np.float32)
    cos = np.repeat(np.cos(freqs), 2, axis=-1)
    sin = np.repeat(np.sin(freqs), 2, axis=-1)
    sin[:, : dim // 2] *= -1
    return {"const": const, "rope": np.stack([cos, sin]).astype(np.float32),
            "rev": np.arange(experts, 0, -1).astype(np.float32)}


def kernel(**inputs):
    import numpy as _np
    import concourse.bacc as _bacc
    from concourse import mybir as _mybir
    from concourse.bass_utils import run_bass_kernel_spmd as _run

    nc = _bacc.Bacc("TRN2", target_bir_lowering=False, num_devices=1)
    arrays = {n: _np.ascontiguousarray(a) for n, a in inputs.items()}
    arrays.update(constants(arrays["ctx_512"].shape, arrays["L1_ffn_wa"].shape[1]))
    aps = {n: nc.dram_tensor(f"in_{n}", a.shape, _mybir.dt.from_np(a.dtype), kind="ExternalInput").ap()
           for n, a in arrays.items()}
    shape = arrays["x"].shape
    out = nc.dram_tensor("out_x", shape, _mybir.dt.float32, kind="ExternalOutput").ap()
    decoder_kernel(nc, aps, out)
    r = _run(nc, [{f"in_{n}": a for n, a in arrays.items()}], core_ids=[0])
    return r.results[0]["out_x"]
```

```python
from contextlib import ExitStack

import numpy as np

import concourse.bass as bass
from concourse import mybir

F32 = mybir.dt.float32
F32R = mybir.dt.float32r
BF16 = mybir.dt.bfloat16
ALU = mybir.AluOpType
ACT = mybir.ActivationFunctionType
AX = mybir.AxisListType
ds = bass.ds

P = 128
MAGIC = 1.5 * 2.0**23


class Banks:

    def __init__(self):
        self.count = [0] * 8
        self.at = {}
        self.order = []
        self.turn = 0

    def line(self, names):
        for name in names:
            bank = self.turn % 8
            self.at[name] = (bank, self.count[bank], None)
            self.order.append(name)
            self.count[bank] += 1
            self.turn += 1

    def loop(self, names, trips, banks=range(8), not_in_last=()):
        per = [0] * 8
        for n, name in enumerate(names):
            bank = banks[n % len(banks)]
            self.at[name] = (bank, self.count[bank] + per[bank], per)
            self.order.append(name)
            per[bank] += 1
        self.count = [c + trips * p for c, p in zip(self.count, per)]
        for name in not_in_last:
            self.count[self.bank(name)] -= 1
        self.turn = 0

    def bank(self, name):
        return self.at[name][0]

    def before(self, name, i=0):
        bank, count, per = self.at[name]
        return count if per is None else i * per[bank] + count

    def after(self, name, i=0):
        bank, count, per = self.at[name]
        return count + 1 if per is None else i * per[bank] + (count + 1)

    def after_previous(self, name, i):
        bank, count, per = self.at[name]
        assert count + 1 - per[bank] > 0
        return i * per[bank] + (count + 1 - per[bank])


class Steps:

    def __init__(self, eng, sem):
        self.eng, self.sem, self.n, self.loop, self.last = eng, sem, 0, None, None

    def now(self):
        if self.loop is None:
            return self.n
        i, per, start = self.loop
        return i * per + self.n

    def step(self, ins):
        ins.then_inc(self.sem, 1)
        self.n += 1
        self.last = (self.sem, self.now())

    def mark(self, ins, sem, value):
        ins.then_inc(sem, 1)
        self.last = (sem, value)

    def settle(self):
        self.eng.wait_ge(*self.last)

    def enter(self, i, per):
        self.loop = (i, per, self.n)

    def leave(self, trips):
        _, per, start = self.loop
        assert self.n - start == per, (self.n - start, per)
        self.n = start + trips * per
        self.loop = None
        self.last = (self.sem, self.n)


def decoder_kernel(nc, t, out):
    B, S, D = t["x"].shape
    NT = B * S // P
    TB = S // P
    NTOK = B * S
    C = D // P
    HALF = 512
    DC = t["ctx_512"].shape[2]
    DA = t["L0_attn_w_q"].shape[0]
    H = t["L1_xattn_Wq"].shape[0] // P
    PAIRS = H // 2
    M = t["L1_attn_Ws"].shape[1] // H
    DV = t["L1_attn_Wv"].shape[1] // H
    CQ = t["L1_xattn_w_kc_q"].shape[2]
    R = t["L1_xattn_W_qr"].shape[2]
    QC = CQ // 2
    E = t["L1_ffn_wa"].shape[1]
    SH = t["L1_ffn_sg"].shape[0]
    NE = E + SH
    EPS_LN = 1e-5
    EPS_A = 1e-6
    EPS_SIM = 1e-6
    EPS_RMS = 1e-5

    banks = Banks()
    ht = lambda k: [f"ht{k}_{b}" for b in range(B)]
    banks.line(["w0", "w1", "ctx0", "ctx1", "wk"])
    banks.line(ht(0) + ["aq0", "aq1", "ak0", "ak1", "av0", "av1"])
    banks.line(["kvT0", "kvT1", "kv", "wsum", "wqT"])
    A_ORDER = ["at0", "at1", "ml0", "ml1", "at2", "ml2", "ml3", "ao0", "ax0", "at3", "ml4", "ml5", "ao1", "ax1",
               "ml6", "ml7", "ao2", "ax2", "ao3", "ax3"]
    banks.line(A_ORDER)
    banks.line(["kr0", "kr1"])
    GROUPS = ((0, 1), (2, 3))
    for group in GROUPS:
        banks.line([f"{step}{b}" for step in ("ht1_", "bo", "bs") for b in group])
    for group in GROUPS:
        banks.line([f"{step}{b}" for step in ("ht2_", "cy") for b in group])
    D_BODY = (["q0", "q1", "k0", "k1", "em0", "em1", "v0", "v1", "cu0", "cu1",
               "g0", "g1", "g2", "g3", "wot"]
              + ["at0", "at1", "at2", "at3", "u0", "v2", "ok0", "at4", "at5", "at6", "at7", "u1", "pt0", "ok1"]
              + ["bt0", "bt1", "bt2", "bt3", "v3", "o0", "pt1", "o1", "w2", "bt4", "bt5", "bt6", "bt7",
                 "ot0", "ot1", "V", "o2", "T0", "T1", "o3", "s0", "s1", "ot2", "dx0", "ot3", "dx1", "dx2", "dx3"])
    D_BODY = ["d." + n for n in D_BODY]
    banks.line(ht(3) + ["first_s0", "first_s1"])
    D_BANKS = [n % 8 for n in range(len(D_BODY))]
    D_BANKS[-1] = D_BANKS[D_BODY.index("d.ot2")]
    banks.loop(D_BODY, PAIRS, banks=D_BANKS, not_in_last=("d.s0", "d.s1"))
    banks.line(ht(4) + ["first_q0", "first_q1"])
    E_BODY = ["sc00", "sc01", "sc10", "sc11", "pt00", "sc20", "pt01", "sc21", "pt10", "cx0", "pt11", "sc30", "sc31",
              "cx1", "pt20", "pt21", "q0", "pt30", "cx2", "pt31", "q1", "cx3"]
    E_BODY = ["e." + n for n in E_BODY]
    banks.loop(E_BODY, PAIRS, not_in_last=("e.q0", "e.q1"))
    banks.line(["ex0", "ex1", "ex2", "ht5_0", "ht5_1", "ex3", "ht5_2", "ht5_3"])
    banks.turn = 0
    banks.line(["lg", "cb0", "cb1"])
    banks.turn = 0
    banks.line([f"acc{b}" for b in range(B)])
    F_TRIPS = NE // 2
    F_BODY = [f"f.{x}{half}{e}" for e in range(2) for x in "gu" for half in range(2)]
    banks.loop(F_BODY, F_TRIPS, banks=(4, 5, 6, 7))

    with ExitStack() as ctx:
        def sb(name, shape, dt=F32):
            return ctx.enter_context(nc.sbuf_tensor(name, shape, dt))

        def sem(name):
            return ctx.enter_context(nc.semaphore(name))

        ps = ctx.enter_context(nc.psum_tensor("ps", [P, 8, 512], F32))

        X = sb("X", [P, NT, D])
        HTH = sb("HTH", [P, C, NTOK], F32R)
        HTL = sb("HTL", [P, C, NTOK], F32R)
        WCOLS = C * (2 * 2 * M + 2 * M + 2 * DV + 2 * DV) + 2 * D
        WH = sb("WH", [P, WCOLS], F32R)
        WL = sb("WL", [P, WCOLS], F32R)
        OH = sb("OH", [P, 2, NTOK], F32R)
        OL = sb("OL", [P, 2, NTOK], F32R)
        const = sb("const", [P, 4 * P])
        ident, causal, ones = const[:, 0:P], const[:, P:2 * P], const[:, 2 * P:3 * P]
        mask3 = const[:, P:4 * P]
        identb = sb("identb", [P, P], BF16)
        krT = sb("krT", [P, NTOK])
        kr = sb("kr", [P, NT, 2, DC])
        st6 = sb("st6", [P, NT, 6])
        mv = sb("mv", [P, NT, 2])
        ve = sb("ve", [P, NT])
        guess = sb("guess", [P, NT])
        nt = sb("nt", [P, NT])
        rstd = sb("rstd", [P, NT])
        nmr = sb("nmr", [P, NT])
        gg = sb("gg", [P, 2])
        col = sb("col", [P, 8 * NT])

        ARENA = 26 * 1024
        arena = sb("arena", [P, ARENA])
        CARVED = ARENA - NT * D
        HN = arena[:, CARVED:].rearrange("p (n d) -> p n d", n=NT)
        at = [0]

        def carve(*shape, rows=P):
            n = int(np.prod(shape))
            v = arena[0:rows, at[0]:at[0] + n]
            at[0] += n
            assert at[0] <= CARVED
            if len(shape) == 1:
                return v
            names = "abcd"[:len(shape)]
            return v.rearrange(f"p ({' '.join(names)}) -> p {' '.join(names)}", **dict(zip(names, shape)))

        HT = carve(C, NTOK)
        waraw = carve(3, D)
        woraw = carve(2, P)
        WT = carve(8, P)
        MZ = carve(DA + 1)
        ctxn = carve(NT, DC)
        ctxT = carve(NTOK, rows=DC + 1)
        wkraw = carve(DC, rows=DC)
        wkT = carve(DC, rows=DC + 1)
        kvT = carve(NTOK, rows=DC)
        kvn = carve(NT, DC)
        rope = carve(2, TB, DC)
        ropet = carve(NT, DC)
        gamma = carve(D)
        beta = carve(D)
        wf = carve(2, D)
        wq8 = carve(D).bitcast(BF16).rearrange("p (a b) -> p a b", a=2)
        WQT = carve(D).bitcast(BF16).rearrange("p (a b) -> p a b", a=2)
        amin = carve(4, HALF)
        SQ = carve(NTOK)
        SK = carve(NTOK)
        VV = carve(NT, DA + 1)
        AT = carve(2, 3 * P)
        AO = carve(NT, DA)
        AOT = carve(NTOK)
        BO = carve(NTOK, rows=DC)
        SIM = carve(NT, D)
        XQ = carve(NT * D // 2).bitcast(BF16).rearrange("p (a b) -> p a b", a=NT)
        XQT = carve(C * NTOK // 2).bitcast(BF16).rearrange("p (a b) -> p a b", a=C)
        wqk = sb("wqk", [P, 2, C, 2 * M])
        wsv = sb("wsv", [P, C, 2 * M + 2 * DV])
        wg = sb("wg", [P, C, 2 * DV])
        wo = sb("wo", [P, 2, D])
        EMH = sb("EMH", [P, NT, 2 * M], F32R)
        EML = sb("EML", [P, NT, 2 * M], F32R)
        sums = sb("sums", [P, 2 * P], F32R)
        Tall = sb("Tall", [P, PAIRS, C, 2 * DC])
        W2 = sb("W2", [P, PAIRS, D])
        gnorm = sb("gnorm", [P, 1])
        NH = NT * 2
        slotmax = sb("slotmax", [P, NH])
        slotsum = sb("slotsum", [P, NH])
        rs = sb("rs", [P, NH])
        rs2 = sb("rs2", [P, NH])
        sumsq = sb("sumsq", [P, NH])
        rmsv = sb("rmsv", [P, NH])
        rmsl = sb("rmsl", [P, NH])
        coef = sb("coef", [P, NH])

        at[0] = 0
        qT = carve(NTOK)
        kT = carve(NTOK)
        EM = carve(NT, 2 * M)
        ET = carve(NTOK)
        RC = carve(NT, 2 * M)
        PT = RC.rearrange("p a b -> p (a b)")
        VD = carve(NT, 2 * DV)
        SG = HN
        assert 2 * DV == D
        ATd = carve(4, 3 * P)
        BTd = carve(4, 3 * P)
        PM = carve(NT, 2 * M)
        JUNK = carve(4, DV)
        xwq = carve(2, D)
        xkq = carve(2, CQ)
        xqr = carve(2, 2, R, rows=QC)
        xkr = carve(2, R, rows=DC)
        xkv = carve(2, DC)
        xwo = carve(2, 2 * P)
        WOTe = carve(2, D)
        KRT = carve(DC)
        U = carve(2, 2, D, rows=QC)
        VE = carve(D)

        def split_view(at_col, *shape):
            n = int(np.prod(shape))
            names = "abcd"[:len(shape)]
            return [w[:, at_col:at_col + n].rearrange(f"p ({' '.join(names)}) -> p {' '.join(names)}",
                                                      **dict(zip(names, shape))) for w in (WH, WL)]

        QK_AT, SV_AT, G_AT = 0, 4 * M * C, 4 * M * C + (2 * M + 2 * DV) * C
        WQK = split_view(QK_AT, 2, C, 2 * M)
        WSV = split_view(SV_AT, C, 2 * M + 2 * DV)
        WG = split_view(G_AT, C, 2 * DV)
        O_AT = G_AT + C * 2 * DV
        WO = split_view(O_AT, 2, D)
        O = [OH, OL]
        FGU = split_view(0, 2, 2, C, P)
        F_COLS = 2 * C * P
        assert 2 * F_COLS + C * (2 * DC + E) <= O_AT
        T_AT = 2 * F_COLS
        TS = split_view(T_AT, C, 2 * DC)
        WR = split_view(T_AT + C * 2 * DC, C, E)

        at[0] = 0
        CT = carve(PAIRS, NTOK)
        QE = carve(NTOK)
        PX = carve(2, 2, TB, S)
        PXT = carve(2, 2, TB, S)
        nmx = carve(NT, 2)
        esum = carve(NT, 2)
        wr = carve(C, E)
        rev = carve(E)
        b2 = carve(D, rows=NE)
        fgu = carve(2, 2, C, P)
        fo = carve(2, D)
        fgb = carve(2, 1)
        fub = carve(2, 1)
        BC = carve(2, NTOK)
        Y = carve(2, NTOK)
        YC = carve(2, NTOK)
        AFF = carve(NT, E)
        TK = carve(4, NT, E)
        tk = carve(6, NT)
        CB = carve(NT, NE)
        CBT = carve(NTOK, rows=NE)
        comb_dram = nc.dram_tensor("comb_by_expert", [NE, NTOK], F32, kind="Internal").ap()

        filled = [sem(f"filled{b}") for b in range(8)]
        evacuated = [sem(f"evacuated{b}") for b in range(8)]
        loaded_x = [sem(f"loaded_x{half}") for half in range(2)]
        loaded_const = sem("loaded_const")
        loaded_a = sem("loaded_a")
        loaded_ctx = sem("loaded_ctx")
        loaded_c = sem("loaded_c")
        loaded_b = sem("loaded_b")
        dve_steps = sem("dve_steps")
        act_steps = sem("act_steps")
        var_ready = sem("var_ready")
        guess_ready = sem("guess_ready")
        nmr_ready = sem("nmr_ready")
        h_even = sem("h_even")
        h_odd = sem("h_odd")
        gate_ready = sem("gate_ready")
        ones_ready = sem("ones_ready")
        identb_ready = sem("identb_ready")
        kr_ready = sem("kr_ready")
        wabs_ready = sem("wabs_ready")
        wq8_ready = sem("wq8_ready")
        amin_ready = sem("amin_ready")
        aexp_ready = sem("aexp_ready")
        ao_ready = sem("ao_ready")
        simnorm_ready = sem("simnorm_ready")
        simmax_ready = sem("simmax_ready")
        simexp_ready = sem("simexp_ready")
        xq_ready = sem("xq_ready")
        stored = sem("stored")
        x_final = sem("x_final")
        x_after_c = sem("x_after_c")
        x_after_d = sem("x_after_d")
        loaded_wqk = sem("loaded_wqk")
        loaded_wsv = sem("loaded_wsv")
        loaded_wg = sem("loaded_wg")
        loaded_wo = sem("loaded_wo")
        loaded_comp = sem("loaded_comp")
        loaded_gnorm = sem("loaded_gnorm")
        ht_hi = sem("ht_hi")
        ot_hi = sem("ot_hi")
        em_hi = sem("em_hi")
        sums_ready = sem("sums_ready")
        px_scaled = sem("px_scaled")
        yc_hi = sem("yc_hi")
        yc_lo = sem("yc_lo")
        hi_ready = {n: sem(f"hi_ready_{n}") for n in ("qk", "sv", "g", "o", "t", "r", "f0", "f1", "fo0", "fo1")}
        lo_ready = {n: sem(f"lo_ready_{n}") for n in ("qk", "sv", "g", "o", "t", "r", "f0", "f1", "fo0", "fo1")}
        loaded_fb = [sem(f"loaded_fb{e}") for e in range(2)]
        loaded_router = sem("loaded_router")
        loaded_fin = [sem(f"loaded_fin{e}") for e in range(2)]
        loaded_fout = [sem(f"loaded_fout{e}") for e in range(2)]
        loaded_bc = [sem(f"loaded_bc{e}") for e in range(2)]
        em_exp = sem("em_exp")
        rc_ready = sem("rc_ready")
        ok_shifted = sem("ok_shifted")
        ok_exp = sem("ok_exp")
        p_ready = sem("p_ready")
        sumsq_ready = sem("sumsq_ready")
        rmsv_ready = sem("rmsv_ready")
        rms_guess = sem("rms_guess")
        emax_ready = sem("emax_ready")
        comb_ready = sem("comb_ready")
        shares_ready = sem("shares_ready")
        comb_stored = sem("comb_stored")
        yc_ready = sem("yc_ready")
        experts_out = sem("experts_out")

        block = ctx.enter_context(nc.Block())

        tile = lambda n: slice(n * P, (n + 1) * P)

        @block.sync
        def _(sp):
            xv = t["x"].rearrange("b (h p) d -> p (b h) d", p=P)
            for half in range(2):
                tt = slice(half * NT // 2, (half + 1) * NT // 2)
                sp.dma_start(X[:, tt, :], xv[:, tt, :]).then_inc(loaded_x[half], 16)
            sp.dma_start(const[:], t["const"]).then_inc(loaded_const, 16)
            for n, w in enumerate(("w_q", "w_k", "w_v")):
                sp.dma_start(waraw[:, n, :], t["L0_attn_" + w]).then_inc(loaded_a, 16)
            sp.dma_start(woraw, t["L0_attn_w_o"].rearrange("(n p) d -> p n d", p=P)).then_inc(loaded_a, 16)
            sp.dma_start(MZ[:, 0:DA], t["L0_attn_M"]).then_inc(loaded_a, 16)
            sp.dma_start(MZ[:, DA:DA + 1], t["L0_attn_z"].rearrange("(d o) -> d o", o=1)).then_inc(loaded_a, 16)
            sp.dma_start(gg[:, 0:1], t["L0_attn_gate"].partition_broadcast(P)).then_inc(loaded_a, 16)
            sp.dma_start(ctxn, t["ctx_512"].rearrange("b (h p) d -> p (b h) d", p=P)).then_inc(loaded_ctx, 16)
            sp.dma_start(rope, t["rope"].rearrange("a (h p) d -> p a h d", p=P)).then_inc(loaded_ctx, 16)
            sp.dma_start(wkraw, t["L0_xattn_W_k"]).then_inc(loaded_ctx, 16)
            sp.dma_start(wkT[DC:DC + 1, :], t["L0_xattn_b_k"].unsqueeze(0)).then_inc(loaded_ctx, 16)
            sp.dma_start(wf, t["L0_ffn_weight"].rearrange("(n p) d -> p n d", p=P)).then_inc(loaded_c, 16)
            sp.dma_start(gamma, t["L0_xattn_ln_gamma"].partition_broadcast(P)).then_inc(loaded_b, 16)
            sp.dma_start(beta, t["L0_xattn_ln_beta"].partition_broadcast(P)).then_inc(loaded_b, 16)
            def after(semaphore, value):
                sp.wait_ge(semaphore, value)
                sp.wait_ge(loaded_const, 16)


            def load_wqk(i):
                for n, w in enumerate(("Wq", "Wk")):
                    v = t["L1_attn_" + w].rearrange("(c p) n -> p c n", p=P)
                    sp.dma_start(wqk[:, n, :, :], v[:, :, ds(i * 2 * M, 2 * M)]).then_inc(loaded_wqk, 16)

            def load_wsv(i):
                v = t["L1_attn_Ws"].rearrange("(c p) n -> p c n", p=P)
                sp.dma_start(wsv[:, :, 0:2 * M], v[:, :, ds(i * 2 * M, 2 * M)]).then_inc(loaded_wsv, 16)
                v = t["L1_attn_Wv"].rearrange("(c p) n -> p c n", p=P)
                sp.dma_start(wsv[:, :, 2 * M:], v[:, :, ds(i * 2 * DV, 2 * DV)]).then_inc(loaded_wsv, 16)

            def load_wg(i):
                v = t["L1_attn_Wg"].rearrange("(c p) n -> p c n", p=P)
                sp.dma_start(wg[:], v[:, :, ds(i * 2 * DV, 2 * DV)]).then_inc(loaded_wg, 16)

            def load_wo(i):
                v = t["L1_attn_Wo"].rearrange("(h p) n -> p h n", p=P)
                sp.dma_start(wo[:], v[:, ds(i * 2, 2), :]).then_inc(loaded_wo, 16)

            def load_comp(i):
                two = lambda a: a[ds(i * 2, 2)]
                sp.dma_start(xwq, t["L1_xattn_Wq"].rearrange("(h k) d -> k h d", k=P)[:, ds(i * 2, 2), :]).then_inc(loaded_comp, 16)
                sp.dma_start(xkq, t["L1_xattn_w_kc_q"].rearrange("h k q -> k h q")[:, ds(i * 2, 2), :]).then_inc(loaded_comp, 16)
                qr = t["L1_xattn_W_qr"].rearrange("h (a q) r -> q h a r", q=QC)
                for a in range(2):
                    sp.dma_start(xqr[:, a], qr[:, ds(i * 2, 2), a, :]).then_inc(loaded_comp, 16)
                sp.dma_start(xkr, t["L1_xattn_W_kr"].rearrange("h c r -> c h r")[:, ds(i * 2, 2), :]).then_inc(loaded_comp, 16)
                sp.dma_start(xkv, t["L1_xattn_w_kc_kv"].rearrange("h k c -> k h c")[:, ds(i * 2, 2), :]).then_inc(loaded_comp, 16)
                sp.dma_start(xwo, t["L1_xattn_Wo"].rearrange("(a n) k -> n a k", n=P)[:, :, ds(i * 2 * P, 2 * P)])\
                    .then_inc(loaded_comp, 16)

            load_wqk(0)
            load_wsv(0)
            load_wg(0)
            sp.dma_start(gnorm[:], t["L1_attn_g_norm_weight"].unsqueeze(1)).then_inc(loaded_gnorm, 16)
            load_wo(0)
            sp.wait_ge(x_after_c, 1)
            load_comp(0)
            with sp.Fori(0, PAIRS - 1) as i:
                after(lo_ready["qk"], i + 1)
                load_wqk(i + 1)
                after(lo_ready["sv"], i + 1)
                load_wsv(i + 1)
                after(lo_ready["g"], i + 1)
                load_wg(i + 1)
                after(lo_ready["o"], i + 1)
                load_wo(i + 1)
                after(filled[banks.bank("d.V")], banks.after("d.V", i))
                load_comp(i + 1)
            sp.wait_ge(x_after_d, 1)
            sp.dma_start(wr, t["L1_ffn_wa"].rearrange("(c p) e -> p c e", p=P)).then_inc(loaded_router, 16)
            sp.dma_start(rev, t["rev"].partition_broadcast(P)).then_inc(loaded_router, 16)
            sp.dma_start(b2[0:E, :], t["L1_ffn_rb2"]).then_inc(loaded_router, 16)
            sp.dma_start(b2[E:NE, :], t["L1_ffn_sb2"]).then_inc(loaded_router, 16)

            def load_in(e, g, u, row):
                for x, w in enumerate((g, u)):
                    sp.dma_start(fgu[:, e, x], w.rearrange("e (c p) f -> p (e c) f", p=P)[:, ds(row * C, C), :])\
                        .then_inc(loaded_fin[e], 16)

            def load_biases(e, gb, ub, row):
                for dst, w in ((fgb, gb), (fub, ub)):
                    sp.dma_start(dst[:, e], w.rearrange("e f -> f e")[:, ds(row, 1)]).then_inc(loaded_fb[e], 16)

            def load_out(e, o, row):
                sp.dma_start(fo[:, e], o.rearrange("e f n -> f e n")[:, ds(row, 1), :].rearrange("f e n -> f (e n)"))\
                    .then_inc(loaded_fout[e], 16)

            def load_bc(e, row):
                sp.dma_start(BC[:, e], comb_dram[ds(row, 1), :].rearrange("a n -> (a n)").partition_broadcast(P))\
                    .then_inc(loaded_bc[e], 16)

            routed = [t["L1_ffn_" + n] for n in ("rg", "rw1", "rgb", "rb1")]
            shared = [t["L1_ffn_" + n] for n in ("sg", "sw1", "sgb", "sb1")]
            for e in range(2):
                load_in(e, *routed[:2], e)
                load_biases(e, *routed[2:], e)
                load_out(e, t["L1_ffn_rw2"], e)
            sp.wait_ge(comb_ready, 1)
            sp.dma_start(comb_dram, CBT).then_inc(comb_stored, 16)
            sp.wait_ge(comb_stored, 16)
            for e in range(2):
                load_bc(e, e)

            def next_experts(i, ins, out, row):
                for e in range(2):
                    after(lo_ready[f"f{e}"], i + 1)
                    load_in(e, *ins[:2], row + e)
                for e in range(2):
                    after(yc_ready, 4 * i + 2 * e + 2)
                    load_biases(e, *ins[2:], row + e)
                    load_bc(e, row + e if ins is routed else E + e)
                for e in range(2):
                    after(lo_ready[f"fo{e}"], i + 1)
                    load_out(e, out, row + e)

            with sp.Fori(0, E // 2 - 1) as i:
                next_experts(i, routed, t["L1_ffn_rw2"], i * 2 + 2)
            next_experts(E // 2 - 1, shared, t["L1_ffn_sw2"], 0)
            ov = out.rearrange("b (h p) d -> p (b h) d", p=P)
            for b in range(B):
                tt = slice(b * TB, (b + 1) * TB)
                sp.wait_ge(x_final, b + 1)
                sp.dma_start(ov[:, tt, :], X[:, tt, :]).then_inc(stored, 16)
            sp.wait_ge(stored, 16 * B)

        @block.tensor
        def _(pe):
            def fill(name, i=0):
                if not (banks.at[name][2] is None and banks.before(name) == 0):
                    pe.wait_ge(evacuated[banks.bank(name)], banks.before(name, i))
                return ps[:, banks.bank(name), :]

            def full(ins, name):
                ins.then_inc(filled[banks.bank(name)], 1)

            def evac(name, i=0):
                pe.wait_ge(evacuated[banks.bank(name)], banks.after(name, i))

            def transpose_h(b, dst, bf16=False):
                src, idn = (XQ, identb[:]) if bf16 else (HN, ident)
                for n in range(TB):
                    for c in range(C):
                        last = pe.transpose(dst[:, c * S + n * P:c * S + (n + 1) * P],
                                            src[:, b * TB + n, c * P:(c + 1) * P], idn)
                return last

            pe.wait_ge(loaded_const, 16)
            pe.wait_ge(loaded_a, 16 * 7)
            for half, name in enumerate(("w0", "w1")):
                pb = fill(name)
                for j in range(4):
                    n = half * 4 + j
                    src = waraw[:, n // 2, (n % 2) * P:(n % 2 + 1) * P] if n < 6 else woraw[:, n - 6, :]
                    last = pe.transpose(pb[:, j * P:(j + 1) * P], src, ident)
                full(last, name)
            pe.wait_ge(loaded_ctx, 16 * 4)
            for half, name in enumerate(("ctx0", "ctx1")):
                pb = fill(name)
                for j in range(4):
                    last = pe.transpose(pb[0:DC, j * P:(j + 1) * P], ctxn[:, half * 4 + j, :], ident)
                full(last, name)
            pb = fill("wk")
            full(pe.transpose(pb[0:DC, 0:DC], wkraw, ident[0:DC, 0:DC]), "wk")

            def layer_norm_T(k, batches=range(B)):
                for b in batches:
                    pb = fill(f"ht{k}_{b}")
                    pe.wait_ge(h_even, k * B + b + 1)
                    pe.wait_ge(h_odd, k * B + b + 1)
                    full(transpose_h(b, pb), f"ht{k}_{b}")

            layer_norm_T(0)
            evac("w0")
            evac("w1")
            for b in range(B):
                evac(f"ht0_{b}")
            for n, q in enumerate("qk"):
                for half in range(2):
                    name = f"a{q}{half}"
                    pb = fill(name)
                    for c in range(C):
                        last = pe.matmul(pb, WT[:, 2 * n + c, :], HT[:, c, half * HALF:(half + 1) * HALF],
                                         start=(c == 0), stop=(c == C - 1))
                    full(last, name)
            for half in range(2):
                name = f"av{half}"
                pb = fill(name)
                for j in range(4):
                    n = half * 4 + j
                    for c in range(C):
                        last = pe.matmul(pb[:, j * P:(j + 1) * P], HT[:, c, tile(n)], WT[:, 4 + c, :],
                                         start=(c == 0), stop=(c == C - 1))
                full(last, name)
            evac("ctx0")
            evac("ctx1")
            evac("wk")
            pe.wait_ge(ones_ready, 2)
            for half in range(2):
                name = f"kvT{half}"
                pb = fill(name)
                full(pe.matmul(pb[0:DC, :], wkT, ctxT[:, half * HALF:(half + 1) * HALF], start=True, stop=True), name)
            pb = fill("kv")
            for n in range(NT):
                last = pe.matmul(pb[:, n * DC:(n + 1) * DC], ctxT[:, tile(n)], wkT, start=True, stop=True)
            full(last, "kv")
            pe.wait_ge(wabs_ready, 1)
            pb = fill("wsum")
            full(pe.matmul(pb[:, 0:1], ones, col[:, 0:1], start=True, stop=True), "wsum")
            pe.wait_ge(wq8_ready, 1)
            pe.wait_ge(identb_ready, 1)
            pb = fill("wqT").bitcast(BF16)
            for c in range(C):
                for o in range(2):
                    last = pe.transpose(pb[:, c * D + o * P:c * D + (o + 1) * P], wq8[:, o, c * P:(c + 1) * P],
                                        identb[:])
            full(last, "wqT")

            def scores(b):
                pb = fill(f"at{b}")
                k0, k1 = tile(b * TB), tile(b * TB + 1)
                pe.matmul(pb[:, 0:2 * P], SK[:, k0], SQ[:, b * S:(b + 1) * S], start=True, stop=True)
                full(pe.matmul(pb[:, 2 * P:3 * P], SK[:, k1], SQ[:, k1], start=True, stop=True), f"at{b}")

            def memory_and_local(n):
                pb = fill(f"ml{n}")
                evac(f"at{n // TB}")
                w = DA + 1
                pe.matmul(pb[:, 0:w], SQ[:, tile(n)], MZ, start=True, stop=True)
                a = AT[:, (n // TB) % 2, :]
                if n % TB == 0:
                    last = pe.matmul(pb[:, w:2 * w], a[:, 0:P], VV[:, n, :], start=True, stop=True)
                else:
                    pe.matmul(pb[:, w:2 * w], a[:, P:2 * P], VV[:, n - 1, :], start=True, stop=False)
                    last = pe.matmul(pb[:, w:2 * w], a[:, 2 * P:3 * P], VV[:, n, :], start=False, stop=True)
                full(last, f"ml{n}")

            def output_T(b):
                pb = fill(f"ao{b}")
                evac(f"ml{b * TB + 1}")
                for n in range(TB):
                    last = pe.transpose(pb[:, n * P:(n + 1) * P], AO[:, b * TB + n, :], ident)
                full(last, f"ao{b}")

            def project_out(b):
                pb = fill(f"ax{b}")
                evac(f"ao{b}")
                for n in range(TB):
                    last = pe.matmul(pb[:, n * D:(n + 1) * D], AOT[:, tile(b * TB + n)],
                                     WT[:, 6:8, :].rearrange("p a b -> p (a b)"), start=True, stop=True)
                full(last, f"ax{b}")

            for name in ("aq0", "aq1", "ak0", "ak1", "av0", "av1"):
                evac(name)
            pe.wait_ge(ones_ready, 2)
            step_of = {"at": scores, "ml": memory_and_local, "ao": output_T, "ax": project_out}
            for name in A_ORDER:
                step_of[name[:2]](int(name[2:]))

            pe.wait_ge(kr_ready, 1)
            for half in range(2):
                name = f"kr{half}"
                pb = fill(name)
                for j in range(4):
                    last = pe.transpose(pb[:, j * P:(j + 1) * P],
                                        kr[:, half * 4 + j, :, :].rearrange("p a b -> p (a b)"), ident)
                full(last, name)

            for group in GROUPS:
                layer_norm_T(1, group)
                for b in group:
                    pb = fill(f"bo{b}")
                    evac(f"ht1_{b}")
                    for c in range(C):
                        last = pe.matmul(pb[0:DC, 0:S], kvn[:, b * TB + c, :], HT[:, c, b * S:(b + 1) * S],
                                         start=(c == 0), stop=(c == C - 1))
                    full(last, f"bo{b}")
                for b in group:
                    pb = fill(f"bs{b}")
                    evac(f"bo{b}")
                    for n in range(TB):
                        last = pe.matmul(pb[:, n * S:(n + 1) * S], BO[:, tile(b * TB + n)], kvT[:, b * S:(b + 1) * S],
                                         start=True, stop=True)
                    full(last, f"bs{b}")

            evac("wqT")
            for g, group in enumerate(GROUPS):
                for b in group:
                    pb = fill(f"ht2_{b}").bitcast(BF16)
                    pe.wait_ge(xq_ready, g + 1)
                    full(transpose_h(b, pb, bf16=True), f"ht2_{b}")
                for b in group:
                    pb = fill(f"cy{b}")
                    evac(f"ht2_{b}")
                    for n in range(TB):
                        for c in range(C):
                            last = pe.matmul(pb[:, n * D:(n + 1) * D], XQT[:, c, tile(b * TB + n)], WQT[:, c, :],
                                             start=(c == 0), stop=(c == C - 1))
                    full(last, f"cy{b}")
            layer_norm_T(3)
            for b in range(B):
                evac(f"ht3_{b}")

            def product(dst, stationary, moving, start, stop, more=False):
                (sh, sl), (mh, ml) = stationary, moving
                pe.matmul(dst, sh, mh, start=start, stop=more, skip_group_check=more)
                pe.matmul(dst, sh, ml, start=False, stop=more, skip_group_check=more)
                return pe.matmul(dst, sl, mh, start=False, stop=stop, skip_group_check=more)

            def project(name, steps, w, at_col, width, i=0):
                per = 512 // width
                for j in steps:
                    pb = fill(f"{name}{j}", i)
                    for m in range(per):
                        for c in range(C):
                            last = product(pb[:, m * width:(m + 1) * width], [h[:, c, tile(j * per + m)] for h in (HTH, HTL)],
                                           [v[:, c, at_col:at_col + width] for v in w], start=(c == 0), stop=(c == C - 1))
                    full(last, f"{name}{j}")

            def project_half_T(name, w, half, i=0):
                pb = fill(f"{name}{half}", i)
                for c in range(C):
                    last = product(pb, [v[:, c, :] for v in w], [h[:, c, half * HALF:(half + 1) * HALF] for h in (HTH, HTL)],
                                   start=(c == 0), stop=(c == C - 1))
                full(last, f"{name}{half}")

            def project_T(name, w, i=0):
                for half in range(2):
                    project_half_T(name, w, half, i)

            def slot_attention_trip(i, last_trip=False):
                pe.wait_ge(lo_ready["qk"], i + 1)
                project_T("d.q", [w[:, 0] for w in WQK], i)
                project_T("d.k", [w[:, 1] for w in WQK], i)
                for g in range(2):
                    pe.wait_ge(em_exp, i * 2 + (g + 1))
                    pb = fill(f"d.em{g}", i)
                    for j in range(4):
                        last = pe.transpose(pb[:, j * P:(j + 1) * P], ET[:, tile(4 * g + j)], ident)
                    full(last, f"d.em{g}")
                project("d.v", range(2), WSV, 2 * M, 2 * DV, i)
                for g in range(2):
                    evac(f"d.em{g}", i)
                    pb = fill(f"d.cu{g}", i)
                    odd = pb.rearrange("p (a b) -> p a b", a=4)[:, 1:4:2, :]
                    pe.matmul(pb, sums[:, 0:P], EMH[:, 4 * g:4 * g + 4, :], start=True, stop=True)
                    pe.matmul(pb, sums[:, 0:P], EML[:, 4 * g:4 * g + 4, :], start=False, stop=True, skip_group_check=True)
                    pe.matmul(odd, sums[:, P:], EMH[:, 4 * g:4 * g + 4:2, :], start=False, stop=True, skip_group_check=True)
                    full(pe.matmul(odd, sums[:, P:], EML[:, 4 * g:4 * g + 4:2, :], start=False, stop=True, skip_group_check=True),
                         f"d.cu{g}")
                pe.wait_ge(lo_ready["g"], i + 1)
                project("d.g", range(4), WG, 0, 2 * DV, i)

                pe.wait_ge(loaded_comp, i * (16 * 7) + 16 * 7)
                pb = fill("d.wot", i)
                for h in range(2):
                    for a in range(2):
                        last = pe.transpose(pb[:, h * D + a * P:h * D + (a + 1) * P], xwo[:, a, h * P:(h + 1) * P], ident)
                full(last, "d.wot")

                def weights_u(h):
                    pb = fill(f"d.u{h}", i)
                    for a in range(2):
                        last = pe.matmul(pb[0:QC, a * D:(a + 1) * D], xkq[:, h, a * QC:(a + 1) * QC], xwq[:, h, :],
                                         start=True, stop=True)
                    full(last, f"d.u{h}")

                def weights_v():
                    evac("d.u0", i)
                    evac("d.u1", i)
                    pb = fill("d.V", i)
                    for h in range(2):
                        for a in range(2):
                            last = pe.matmul(pb[h * R:(h + 1) * R, 0:D], xqr[:, a, h, :], U[:, h, a, :],
                                             start=(a == 0), stop=(a == 1))
                    full(last, "d.V")

                def weights_t():
                    evac("d.w2", i)
                    evac("d.V", i)
                    for h in range(2):
                        pb = fill(f"d.T{h}", i)
                        for c in range(C):
                            last = pe.matmul(pb[:, c * DC:(c + 1) * DC], VE[h * R:(h + 1) * R, c * P:(c + 1) * P],
                                             KRT[h * R:(h + 1) * R, :], start=True, stop=True)
                        full(last, f"d.T{h}")

                def weights_2():
                    evac("d.wot", i)
                    pb = fill("d.w2", i)
                    for h in range(2):
                        pe.matmul(pb[h * DC:(h + 1) * DC, 0:D], xkv[:, h, :], WOTe[:, h, :], start=True, stop=True)
                    full(pe.transpose(pb[:, D:D + DC], xkr.rearrange("p a b -> p (a b)"), ident[0:DC, 0:DC]), "d.w2")

                def pairwise(name, j, left, right):
                    b, h = j // 2, j % 2
                    rows = slice(h * M, (h + 1) * M)
                    pb = fill(f"d.{name}{j}", i)
                    pe.matmul(pb[:, 0:2 * P], left[rows, tile(b * TB)], right[rows, b * S:(b + 1) * S], start=True, stop=True)
                    full(pe.matmul(pb[:, 2 * P:3 * P], left[rows, tile(b * TB + 1)], right[rows, tile(b * TB + 1)],
                                   start=True, stop=True), f"d.{name}{j}")

                def apply(pb, at_col, a, n, rhs):
                    w = rhs(n).shape[-1]
                    dst = pb[:, at_col:at_col + w]
                    if n % TB == 0:
                        return pe.matmul(dst, a[:, 0:P], rhs(n), start=True, stop=True)
                    pe.matmul(dst, a[:, P:2 * P], rhs(n - 1), start=True, stop=False)
                    return pe.matmul(dst, a[:, 2 * P:3 * P], rhs(n), start=False, stop=True)

                def slots(g):
                    pb = fill(f"d.ok{g}", i)
                    for j in range(4):
                        evac(f"d.at{4 * g + j}", i)
                    for n in range(4):
                        for h in range(2):
                            last = apply(pb, n * 2 * M + h * M, ATd[:, (n // TB) * 2 + h, :], 4 * g + n,
                                         lambda m: EM[:, m, h * M:(h + 1) * M])
                    full(last, f"d.ok{g}")

                def slots_T(g):
                    pb = fill(f"d.pt{g}", i)
                    pe.wait_ge(p_ready, i * 2 + (g + 1))
                    for j in range(4):
                        last = pe.transpose(pb[:, j * P:(j + 1) * P], EM[:, 4 * g + j, :], ident)
                    full(last, f"d.pt{g}")

                def values(b):
                    pb = fill(f"d.o{b}", i)
                    evac(f"d.bt{2 * b}", i)
                    evac(f"d.bt{2 * b + 1}", i)
                    for n in range(TB):
                        for h in range(2):
                            last = apply(pb, (n * 2 + h) * DV, BTd[:, (b % 2) * 2 + h, :], b * TB + n,
                                         lambda m: VD[:, m, h * DV:(h + 1) * DV])
                    full(last, f"d.o{b}")

                def outputs_T(b):
                    pb = fill(f"d.ot{b}", i)
                    evac(f"d.o{b}", i)
                    for h in range(2):
                        for n in range(TB):
                            last = pe.transpose(pb[:, h * S + n * P:h * S + (n + 1) * P],
                                                SG[:, b * TB + n, h * DV:(h + 1) * DV], ident)
                    full(last, f"d.ot{b}")

                def project_out(b):
                    pb = fill(f"d.dx{b}", i)
                    evac(f"d.ot{b}", i)
                    for n in range(TB):
                        for h in range(2):
                            last = product(pb[:, n * D:(n + 1) * D], [o[:, h, tile(b * TB + n)] for o in O],
                                           [w[:, h, :] for w in WO], start=(h == 0), stop=(h == 1))
                    full(last, f"d.dx{b}")

                for name, next_in_bank in (("q0", "cu0"), ("q1", "cu1"), ("k0", "g0"), ("k1", "g1"), ("v0", "wot"), ("v1", "at0")):
                    assert banks.bank("d." + name) == banks.bank("d." + next_in_bank)
                for g in range(2):
                    for j in range(4 * g, 4 * g + 4):
                        pairwise("at", j, kT, qT)
                    weights_u(g)
                    if g == 0:
                        project("d.v", [2], WSV, 2 * M, 2 * DV, i)
                    else:
                        slots_T(0)
                    slots(g)
                for g in range(2):
                    if g == 1:
                        slots_T(1)
                        values(1)
                        weights_2()
                    evac(f"d.pt{g}", i)
                    for j in range(4 * g, 4 * g + 4):
                        pairwise("bt", j, ET, PT)
                    if g == 0:
                        project("d.v", [3], WSV, 2 * M, 2 * DV, i)
                        values(0)
                    else:
                        outputs_T(0)
                        outputs_T(1)
                        weights_v()
                        values(2)
                        weights_t()
                        values(3)
                        if not last_trip:
                            pe.wait_ge(lo_ready["sv"], i + 2)
                            project_T("d.s", [w[:, :, 0:2 * M] for w in WSV], i)
                        outputs_T(2)
                        pe.wait_ge(lo_ready["o"], i + 1)
                        project_out(0)
                        outputs_T(3)
                        project_out(1)
                        project_out(2)
                        project_out(3)

            pe.wait_ge(sums_ready, 1)
            pe.wait_ge(lo_ready["sv"], 1)
            project_T("first_s", [w[:, :, 0:2 * M] for w in WSV])
            with pe.Fori(0, PAIRS - 1) as i:
                slot_attention_trip(i)
            slot_attention_trip(PAIRS - 1, last_trip=True)

            layer_norm_T(4)
            evac("kr0")
            evac("kr1")

            def context_attention_trip(i, last_trip=False):

                def e_scores(b, h):
                    name = f"e.sc{b}{h}"
                    pb = fill(name, i)
                    if h == 0 and b % 2 == 0:
                        pe.wait_ge(evacuated[banks.bank(f"e.q{b // 2}")], banks.after_previous(f"e.q{b // 2}", i))
                    rows = slice(h * DC, (h + 1) * DC)
                    for n in range(TB):
                        last = pe.matmul(pb[:, n * S:(n + 1) * S], QE[rows, tile(b * TB + n)], krT[rows, b * S:(b + 1) * S],
                                         start=True, stop=True)
                    full(last, name)

                def e_probs_T(b, h):
                    name = f"e.pt{b}{h}"
                    pb = fill(name, i)
                    pe.wait_ge(px_scaled, i * 8 + (2 * b + h + 1))
                    for c in range(TB):
                        for n in range(TB):
                            last = pe.transpose(pb[:, c * S + n * P:c * S + (n + 1) * P],
                                                PX[:, b % 2, h, n, c * P:(c + 1) * P], ident)
                    full(last, name)

                def e_context(b):
                    name = f"e.cx{b}"
                    pb = fill(name, i)
                    evac(f"e.pt{b}0", i)
                    evac(f"e.pt{b}1", i)
                    for h in range(2):
                        for c in range(TB):
                            last = pe.matmul(pb[h * DC:(h + 1) * DC, 0:S], kr[:, b * TB + c, 0, :], PXT[:, b % 2, h, c, :],
                                             start=(c == 0), stop=(c == TB - 1))
                    full(last, name)

                e_step = {"sc": e_scores, "pt": e_probs_T, "cx": e_context}
                for name in E_BODY:
                    if name[2:3] == "q":
                        if not last_trip:
                            if name == "e.q0":
                                pe.wait_ge(lo_ready["t"], i + 2)
                            project_half_T("e.q", TS, int(name[3]), i)
                    elif name[2:4] in e_step:
                        e_step[name[2:4]](*(int(x) for x in name[4:]))

            pe.wait_ge(lo_ready["t"], 1)
            evac("ht4_0")
            evac("ht4_1")
            project_half_T("first_q", TS, 0)
            evac("ht4_2")
            evac("ht4_3")
            project_half_T("first_q", TS, 1)
            for half in range(2):
                evac(f"first_q{half}")
            with pe.Fori(0, PAIRS - 1) as i:
                context_attention_trip(i)
            context_attention_trip(PAIRS - 1, last_trip=True)

            def context_project_out(b):
                pb = fill(f"ex{b}")
                if b == 0:
                    for j in range(B):
                        evac(f"e.cx{j}", PAIRS - 1)
                for n in range(TB):
                    for p in range(PAIRS):
                        last = pe.matmul(pb[:, n * D:(n + 1) * D], CT[:, p, tile(b * TB + n)], W2[:, p, :],
                                         start=(p == 0), stop=(p == PAIRS - 1))
                full(last, f"ex{b}")

            for b in range(3):
                context_project_out(b)

            layer_norm_T(5, (0, 1))
            context_project_out(3)
            layer_norm_T(5, (2,))
            pe.wait_ge(lo_ready["r"], 1)
            pb = fill("lg")
            for n in range(NT):
                if n == 6:
                    layer_norm_T(5, (3,))
                if n % TB == 0:
                    evac(f"ht5_{n // TB}")
                for c in range(C):
                    last = product(pb[:, n * E:(n + 1) * E], [h[:, c, tile(n)] for h in (HTH, HTL)], [w[:, c, :] for w in WR],
                                   start=(c == 0), stop=(c == C - 1))
            full(last, "lg")

            def start_sums():
                pe.wait_ge(loaded_router, 16 * 4)
                pe.wait_ge(shares_ready, 1)
                for half in range(2):
                    pb = fill(f"cb{half}")
                    for j in range(4):
                        last = pe.transpose(pb[0:NE, j * P:(j + 1) * P], CB[:, half * 4 + j, :], ident)
                    full(last, f"cb{half}")
                evac("cb0")
                evac("cb1")
                for b in range(B):
                    pb = fill(f"acc{b}")
                    for n in range(TB):
                        last = pe.matmul(pb[:, n * D:(n + 1) * D], CBT[:, tile(b * TB + n)], b2, start=(n == 0), stop=True,
                                         skip_group_check=True)

            def experts_trip(i, first_trip=False):
                for e in range(2):
                    pe.wait_ge(lo_ready[f"f{e}"], i + 1)
                    for x in range(2):
                        for half in range(2):
                            name = f"f.{'gu'[x]}{half}{e}"
                            pb = fill(name, i)
                            for c in range(C):
                                last = product(pb, [w[:, e, x, c, :] for w in FGU],
                                               [h[:, c, half * HALF:(half + 1) * HALF] for h in (HTH, HTL)],
                                               start=(c == 0), stop=(c == C - 1))
                            full(last, name)
                    if first_trip and e == 0:
                        start_sums()
                for e in range(2):
                    pe.wait_ge(lo_ready[f"fo{e}"], i + 1)
                    for half in range(2):
                        pe.wait_ge(yc_lo, i * 4 + (2 * e + half + 1))
                        for n in range(4 * half, 4 * half + 4):
                            last = product(ps[:, banks.bank(f"acc{n // TB}"), (n % TB) * D:(n % TB + 1) * D],
                                           [o[:, e, tile(n)] for o in O], [w[:, e, :] for w in WO], start=False, stop=True,
                                           more=True)
                last.then_inc(experts_out, 1)

            experts_trip(0, first_trip=True)
            with pe.Fori(0, F_TRIPS - 1) as i:
                experts_trip(i + 1)

        @block.scalar
        def _(act):
            own = Steps(act, act_steps)

            def full(name, i=0):
                act.wait_ge(filled[banks.bank(name)], banks.after(name, i))
                return ps[:, banks.bank(name), :]

            def evac(ins, name, i=0):
                own.mark(ins, evacuated[banks.bank(name)], banks.after(name, i))

            roots, norms = [0], [0]

            def inverse_root(batches=range(B)):
                roots[0] += 1
                tt = slice(batches[0] * TB, (batches[-1] + 1) * TB)
                act.wait_ge(var_ready, roots[0])
                own.step(act.activation(nt[:, tt], ve[:, tt], ACT.Ln))
                own.settle()
                own.mark(act.activation(guess[:, tt], nt[:, tt], ACT.Exp, scale=-0.5), guess_ready, roots[0])

            def normalize_odd(k, batches=range(B)):
                norms[0] += 1
                act.wait_ge(nmr_ready, norms[0])
                for b in batches:
                    n = 2 * b + 1
                    own.mark(act.activation(HN[:, n, :], X[:, n, :], ACT.Identity, bias=nmr[:, n:n + 1],
                                              scale=rstd[:, n:n + 1]), h_odd, k * B + b + 1)

            def evac_ht(k, dst, batches=range(1, B, 2), bf16=False):
                for b in batches:
                    pb = full(f"ht{k}_{b}")
                    pb = pb.bitcast(BF16) if bf16 else pb
                    src = pb[:, 0:C * S].rearrange("p (c s) -> p c s", c=C)
                    evac(act.copy(dst[:, :, b * S:(b + 1) * S], src), f"ht{k}_{b}")

            act.preload_act_table_set("natural_log_exp_and_others")
            for half in range(2):
                inverse_root((2 * half, 2 * half + 1))
                normalize_odd(0, (2 * half, 2 * half + 1))
            act.wait_ge(loaded_a, 16 * 7)
            own.mark(act.activation(gg[:, 0:1], gg[:, 0:1], ACT.Exp, scale=-1.0), gate_ready, 1)
            for half, name in enumerate(("w0", "w1")):
                evac(act.copy(WT[:, half * 4:half * 4 + 4, :].rearrange("p a b -> p (a b)"), full(name)), name)
            for half, name in enumerate(("ctx0", "ctx1")):
                evac(act.copy(ctxT[0:DC, half * HALF:(half + 1) * HALF], full(name)[0:DC, :]), name)
            evac(act.copy(wkT[0:DC, :], full("wk")[0:DC, 0:DC]), "wk")
            evac_ht(0, HT)
            for n in range(4):
                act.wait_ge(amin_ready, n + 1)
                own.mark(act.activation(amin[:, n, :], amin[:, n, :], ACT.Exp), aexp_ready, n + 1)
            for half in range(2):
                evac(act.copy(VV[:, half * 4:half * 4 + 4, 0:DA],
                              full(f"av{half}").rearrange("p (n d) -> p n d", n=4)), f"av{half}")
            for half in range(2):
                evac(act.copy(kvT[:, half * HALF:(half + 1) * HALF], full(f"kvT{half}")[0:DC, :]), f"kvT{half}")
            evac(act.copy(kvn.rearrange("p a b -> p (a b)"), full("kv")), "kv")
            evac(act.copy(WQT.rearrange("p a b -> p (a b)"), full("wqT").bitcast(BF16)[:, 0:C * D]), "wqT")
            for b in range(B):
                evac(act.copy(AOT[:, b * S:(b + 1) * S], full(f"ao{b}")[:, 0:S]), f"ao{b}")
            for half in range(2):
                evac(act.copy(krT[:, half * HALF:(half + 1) * HALF], full(f"kr{half}")), f"kr{half}")

            def attended_out(group):
                for b in group:
                    evac(act.mul(BO[:, b * S:(b + 1) * S], full(f"bo{b}")[0:DC, 0:S], D ** -0.5), f"bo{b}")

            inverse_root(GROUPS[0])
            normalize_odd(1, GROUPS[0])
            inverse_root(GROUPS[1])
            evac_ht(1, HT, GROUPS[0])
            normalize_odd(1, GROUPS[1])
            attended_out(GROUPS[0])
            evac_ht(1, HT, GROUPS[1])
            inverse_root(GROUPS[0])
            attended_out(GROUPS[1])
            inverse_root(GROUPS[1])
            for g, group in enumerate(GROUPS):
                act.wait_ge(simnorm_ready, g + 1)
                for b in group:
                    pb = full(f"bs{b}")
                    for n in range(TB):
                        k = b * TB + n
                        ins = act.activation(SIM[:, k, :], pb[:, n * S:(n + 1) * S], ACT.Identity,
                                             bias=nmr[:, k:k + 1], scale=rstd[:, k:k + 1])
                        if n == TB - 1:
                            evac(ins, f"bs{b}")
                        else:
                            own.step(ins)
            for n in range(NT):
                act.wait_ge(simmax_ready, n // TB + 1)
                own.mark(act.activation(SIM[:, n, :], SIM[:, n, :], ACT.Exp, bias=col[:, NT + n:NT + n + 1],
                                          accum_out=col[:, 2 * NT + n:2 * NT + n + 1]), simexp_ready, n + 1)
            for group in GROUPS:
                inverse_root(group)
                normalize_odd(2, group)
            evac_ht(2, XQT, range(B), bf16=True)
            def split_hi(name, at_col, raw, count):
                own.mark(act.copy(WH[:, at_col:at_col + raw.shape[-1]], raw), hi_ready[name], count)

            flat = lambda v: v.rearrange("p a b -> p (a b)") if len(v.shape) == 3 else v.rearrange("p a b c -> p (a b c)")

            def split_ht_hi(k, batches=range(B)):
                for b in batches:
                    src = full(f"ht{k}_{b}").rearrange("p (c s) -> p c s", c=C)
                    own.mark(act.copy(HTH[:, :, b * S:(b + 1) * S], src), ht_hi, (k - 3) * B + b + 1)

            act.wait_ge(loaded_wsv, 32)
            split_hi("sv", SV_AT, flat(wsv[:]), 1)
            act.wait_ge(loaded_wqk, 32)
            split_hi("qk", QK_AT, flat(wqk[:]), 1)
            act.wait_ge(loaded_wg, 16)
            split_hi("g", G_AT, flat(wg[:]), 1)
            for group in GROUPS:
                inverse_root(group)
                normalize_odd(3, group)
            split_ht_hi(3)
            own.mark(act.copy(sums[:], const[:, P:3 * P]), sums_ready, 1)
            act.wait_ge(loaded_gnorm, 16)

            def exp_s(name, i, trip):
                for g in range(2):
                    act.wait_ge(evacuated[banks.bank(f"{name}{g}")], banks.after(f"{name}{g}", i))
                    et = ET[:, g * HALF:(g + 1) * HALF]
                    own.mark(act.activation(et, et, ACT.Exp), em_exp, trip * 2 + (g + 1))

            def slot_attention_trip(i, last_trip=False):
                for half in range(2):
                    evac(act.copy(qT[:, half * HALF:(half + 1) * HALF], full(f"d.q{half}", i)), f"d.q{half}", i)

                def values_out(b):
                    evac(act.copy(VD[:, b * TB:(b + 1) * TB, :].rearrange("p a b -> p (a b)"), full(f"d.v{b}", i)), f"d.v{b}", i)

                for g in range(2):
                    pb = full(f"d.em{g}", i).rearrange("p (a b) -> p a b", a=4)
                    own.mark(act.copy(EMH[:, 4 * g:4 * g + 4, :], pb), em_hi, i * 2 + (g + 1))
                values_out(0)
                values_out(1)
                for g in range(2):
                    rc = RC[:, 4 * g:4 * g + 4, :].rearrange("p a b -> p (a b)")
                    evac(act.activation(rc, full(f"d.cu{g}", i), ACT.Ln), f"d.cu{g}", i)
                own.settle()
                for g in range(2):
                    rc = RC[:, 4 * g:4 * g + 4, :].rearrange("p a b -> p (a b)")
                    own.mark(act.activation(rc, rc, ACT.Exp, scale=-1.0), rc_ready, i * 2 + (g + 1))
                for b in range(B):
                    sg = SG[:, b * TB:(b + 1) * TB, :].rearrange("p a b -> p (a b)")
                    evac(act.activation(sg, full(f"d.g{b}", i), ACT.Silu), f"d.g{b}", i)
                act.preload_act_table_set("natural_log_exp_and_others")
                if not last_trip:
                    act.wait_ge(loaded_wqk, i * 32 + 64)
                    act.wait_ge(filled[banks.bank("d.k1")], banks.after("d.k1", i))
                    split_hi("qk", QK_AT, flat(wqk[:]), i + 2)
                act.wait_ge(loaded_wo, i * 16 + 16)
                split_hi("o", O_AT, flat(wo[:]), i + 1)
                evac(act.copy(WOTe.rearrange("p a b -> p (a b)"), full("d.wot", i)), "d.wot", i)

                def exp_slots(g):
                    act.wait_ge(ok_shifted, i * 2 + (g + 1))
                    pm = PM[:, 4 * g:4 * g + 4, :]
                    own.mark(act.activation(pm, pm, ACT.Exp, scale=M ** -0.5), ok_exp, i * 2 + (g + 1))

                def root_mean_squares(b):
                    pb = full(f"d.o{b}", i)
                    for j in range(4):
                        k = b * 4 + j
                        ins = act.activation(JUNK[:, j], pb[:, j * DV:(j + 1) * DV], ACT.Square, accum_out=sumsq[:, k:k + 1])
                        if j == 3:
                            own.mark(ins, sumsq_ready, i * B + (b + 1))
                        else:
                            own.step(ins)
                    act.wait_ge(rmsv_ready, i * B + (b + 1))
                    sl = slice(4 * b, 4 * b + 4)
                    own.step(act.activation(rmsl[:, sl], rmsv[:, sl], ACT.Ln))
                    own.settle()
                    own.mark(act.activation(rmsl[:, sl], rmsl[:, sl], ACT.Exp, scale=-0.5), rms_guess, i * B + (b + 1))

                def outputs_T(b):
                    own.mark(act.mul(OH[:, :, b * S:(b + 1) * S], full(f"d.ot{b}", i).rearrange("p (h s) -> p h s", h=2),
                                     gnorm[:, 0:1]), ot_hi, i * B + (b + 1))

                evac(act.copy(U[:, 0, :, :].rearrange("p a b -> p (a b)"), full("d.u0", i)[0:QC, :]), "d.u0", i)
                values_out(2)
                exp_slots(0)
                evac(act.copy(U[:, 1, :, :].rearrange("p a b -> p (a b)"), full("d.u1", i)[0:QC, :]), "d.u1", i)
                evac(act.copy(PT[:, 0:HALF], full("d.pt0", i)), "d.pt0", i)
                exp_slots(1)
                values_out(3)
                root_mean_squares(0)
                evac(act.copy(PT[:, HALF:], full("d.pt1", i)), "d.pt1", i)
                root_mean_squares(1)
                w2 = W2[:, ds(i, 1), :].rearrange("p i n -> p (i n)")
                own.step(act.copy(w2, full("d.w2", i)[:, 0:D]))
                evac(act.copy(KRT, full("d.w2", i)[:, D:D + DC]), "d.w2", i)
                outputs_T(0)
                outputs_T(1)
                evac(act.copy(VE, full("d.V", i)[:, 0:D]), "d.V", i)
                if not last_trip:
                    act.wait_ge(loaded_wsv, i * 32 + 64)
                    split_hi("sv", SV_AT, flat(wsv[:]), i + 2)
                    act.wait_ge(loaded_wg, i * 16 + 32)
                    split_hi("g", G_AT, flat(wg[:]), i + 2)
                root_mean_squares(2)
                root_mean_squares(3)
                for h in range(2):
                    dst = Tall[:, ds(i, 1), :, h * DC:(h + 1) * DC].rearrange("p i c n -> p (i c) n")
                    src = full(f"d.T{h}", i)[:, 0:C * DC].rearrange("p (c n) -> p c n", c=C)
                    evac(act.copy(dst, src), f"d.T{h}", i)
                outputs_T(2)
                if not last_trip:
                    exp_s("d.s", i, i + 1)
                outputs_T(3)

            exp_s("first_s", 0, 0)
            act.preload_act_table_set("natural_log_exp_and_others")
            with act.Fori(0, PAIRS - 1) as i:
                own.enter(i, 1 + 4 * 4)
                slot_attention_trip(i)
                own.leave(PAIRS - 1)
            slot_attention_trip(PAIRS - 1, last_trip=True)

            def normalize(k):
                for batches in ((0, 1), (2,), (3,)):
                    inverse_root(batches)
                    normalize_odd(k, batches)
                    split_ht_hi(k, batches)

            inverse_root()
            normalize_odd(4)

            split_t = lambda i: Tall[:, ds(i, 1), :, :].rearrange("p i c n -> p (i c n)")
            split_hi("t", T_AT, Tall[:, 0].rearrange("p c n -> p (c n)"), 1)
            split_ht_hi(4)
            evac(act.copy(QE[:, 0:HALF], full("first_q0")), "first_q0")

            def context_attention_trip(i, last_trip=False):
                def e_exp(b, h):
                    pb = full(f"e.sc{b}{h}", i)
                    act.wait_ge(emax_ready, i * 8 + (2 * b + h + 1))
                    for n in range(TB):
                        k = b * TB + n
                        ins = act.activation(PX[:, b % 2, h, n, :], pb[:, n * S:(n + 1) * S], ACT.Exp, bias=nmx[:, k, h:h + 1],
                                             accum_out=esum[:, k, h:h + 1])
                        if n == TB - 1:
                            evac(ins, f"e.sc{b}{h}", i)
                        else:
                            own.step(ins)

                for name in E_BODY:
                    kind, at_ = name[2:4], name[4:]
                    if kind == "sc":
                        e_exp(int(at_[0]), int(at_[1]))
                    elif kind == "pt" and at_[1] == "0":
                        b = int(at_[0])
                        evac(act.copy(PXT[:, b % 2, 0, :, :].rearrange("p a b -> p (a b)"), full(name, i)), name, i)
                    elif kind == "cx":
                        b = int(at_)
                        dst = CT[:, ds(i, 1), b * S:(b + 1) * S].rearrange("p i s -> p (i s)")
                        evac(act.copy(dst, full(name, i)[:, 0:S]), name, i)
                    elif kind == "q0" and not last_trip:
                        evac(act.copy(QE[:, 0:HALF], full(name, i)), name, i)
                    if name == "e.sc11" and not last_trip:
                        split_hi("t", T_AT, split_t(i + 1), i + 2)

            with act.Fori(0, PAIRS - 1) as i:
                own.enter(i, 8)
                context_attention_trip(i)
                own.leave(PAIRS - 1)
            context_attention_trip(PAIRS - 1, last_trip=True)

            for e in range(2):
                act.wait_ge(loaded_fin[e], 32)
                split_hi(f"f{e}", e * F_COLS, fgu[:, e].rearrange("p x c f -> p (x c f)"), 1)
            act.wait_ge(loaded_router, 16 * 4)
            split_hi("r", T_AT + C * 2 * DC, flat(wr), 1)
            normalize(5)
            evac(act.activation(AFF.rearrange("p a b -> p (a b)"), full("lg")[:, 0:NT * E], ACT.Sigmoid), "lg")

            def experts_trip(i, last_trip=False):
                def split_yc_hi(e):
                    for half in range(2):
                        sl = slice(half * HALF, (half + 1) * HALF)
                        act.wait_ge(yc_ready, i * 4 + (2 * e + half + 1))
                        own.mark(act.copy(OH[:, e, sl], YC[:, e, sl]), yc_hi, i * 4 + (2 * e + half + 1))

                def split_in_hi(e):
                    if not last_trip:
                        full(f"f.u1{e}", i)
                        act.wait_ge(loaded_fin[e], i * 32 + 64)
                        split_hi(f"f{e}", e * F_COLS, fgu[:, e].rearrange("p x c f -> p (x c f)"), i + 2)

                for e in range(2):
                    act.wait_ge(loaded_fb[e], i * 32 + 32)
                    for half in range(2):
                        name = f"f.g{half}{e}"
                        evac(act.activation(Y[:, e, half * HALF:(half + 1) * HALF], full(name, i), ACT.Gelu,
                                            bias=fgb[:, e]), name, i)
                    if e == 0:
                        for o in range(2):
                            act.wait_ge(loaded_fout[o], i * 16 + 16)
                            split_hi(f"fo{o}", O_AT + o * D, fo[:, o, :], i + 1)
                        split_yc_hi(0)
                split_in_hi(0)
                split_yc_hi(1)
                split_in_hi(1)

            with act.Fori(0, F_TRIPS - 1) as i:
                experts_trip(i)
            experts_trip(F_TRIPS - 1, last_trip=True)

        @block.gpsimd
        def _(pool):
            pool.memset(ctxT[DC:DC + 1, :], 1.0).then_inc(ones_ready, 1)
            pool.wait_ge(ones_ready, 1)
            pool.memset(VV[:, :, DA:DA + 1], 1.0).then_inc(ones_ready, 1)


        @block.vector
        def _(dve):
            own = Steps(dve, dve_steps)

            def full(name, i=0):
                dve.wait_ge(filled[banks.bank(name)], banks.after(name, i))
                return ps[:, banks.bank(name), :]

            def evac(ins, name, i=0):
                own.mark(ins, evacuated[banks.bank(name)], banks.after(name, i))

            roots, norms = [0], [0]

            def inverse_root(eps, batches=range(B)):
                roots[0] += 1
                tt = slice(batches[0] * TB, (batches[-1] + 1) * TB)
                v, g, r = ve[:, tt], guess[:, tt], rstd[:, tt]
                own.settle()
                own.mark(dve.tensor_scalar(v, mv[:, tt, 1], eps, None, ALU.add), var_ready, roots[0])
                dve.wait_ge(guess_ready, roots[0])
                own.step(dve.tensor_tensor(r, g, g, ALU.mult))
                own.settle()
                own.step(dve.tensor_tensor(r, r, v, ALU.mult))
                own.settle()
                own.step(dve.tensor_scalar(r, r, -0.5, 1.5, ALU.mult, ALU.add))
                own.settle()
                own.step(dve.tensor_tensor(r, r, g, ALU.mult))
                own.settle()

            def layer_norm(k, batches=range(B)):
                norms[0] += 1
                tt = slice(batches[0] * TB, (batches[-1] + 1) * TB)
                for n in range(tt.start, tt.stop):
                    own.step(dve.bn_stats(st6[:, n, :], X[:, n, :]))
                own.settle()
                for n in range(tt.start, tt.stop):
                    own.step(dve.bn_aggr(mv[:, n, :], st6[:, n, :]))
                inverse_root(EPS_LN, batches)
                own.mark(dve.scalar_tensor_tensor(out=nmr[:, tt], in0=mv[:, tt, 0], scalar=-1.0, in1=rstd[:, tt],
                                                    op0=ALU.mult, op1=ALU.mult), nmr_ready, norms[0])
                own.settle()
                for b in batches:
                    n = 2 * b
                    own.mark(dve.tensor_scalar(HN[:, n, :], X[:, n, :], rstd[:, n:n + 1], nmr[:, n:n + 1],
                                                 ALU.mult, ALU.add), h_even, k * B + b + 1)

            def evac_ht(k, dst, batches=range(0, B, 2)):
                for b in batches:
                    src = full(f"ht{k}_{b}")[:, 0:C * S].rearrange("p (c s) -> p c s", c=C)
                    evac(dve.tensor_copy(dst[:, :, b * S:(b + 1) * S], src), f"ht{k}_{b}")

            for half in range(2):
                dve.wait_ge(loaded_x[half], 16)
                layer_norm(0, (2 * half, 2 * half + 1))
            dve.wait_ge(loaded_const, 16)
            own.mark(dve.tensor_copy(identb[:], ident), identb_ready, 1)
            dve.wait_ge(loaded_ctx, 16 * 4)
            hd = DC // 2
            cv = ctxn.rearrange("p (b n) d -> p b n d", b=B)
            rv = ropet.rearrange("p (b n) d -> p b n d", b=B)
            for n in range(TB):
                for lo, hi in ((0, hd), (hd, DC)):
                    src = (lo + hd) % DC
                    own.step(dve.tensor_tensor(rv[:, :, n, lo:hi], cv[:, :, n, src:src + hd],
                                               rope[:, 1:2, n, lo:hi].to_broadcast([P, B, hd]), ALU.mult))
            krv = kr[:].rearrange("p (b n) a d -> p b n a d", b=B)
            for n in range(TB):
                own.step(dve.tensor_tensor(krv[:, :, n, 0, :], cv[:, :, n, :],
                                           rope[:, 0:1, n, :].to_broadcast([P, B, DC]), ALU.mult))
            own.settle()
            own.step(dve.tensor_tensor(kr[:, :, 0, :], kr[:, :, 0, :], ropet, ALU.add))
            own.settle()
            own.mark(dve.tensor_copy(kr[:, :, 1, :], kr[:, :, 0, :]), kr_ready, 1)
            evac_ht(0, HT)
            for n in range(4):
                name = f"a{'qk'[n // 2]}{n % 2}"
                own.mark(dve.tensor_scalar(amin[:, n, :], full(name), 0.0, None, ALU.min), amin_ready, n + 1)
            for n in range(4):
                name = f"a{'qk'[n // 2]}{n % 2}"
                dve.wait_ge(aexp_ready, n + 1)
                dst = (SQ, SK)[n // 2][:, (n % 2) * HALF:(n % 2 + 1) * HALF]
                evac(dve.scalar_tensor_tensor(out=dst, in0=full(name), scalar=0.0, in1=amin[:, n, :],
                                              op0=ALU.max, op1=ALU.add), name)
            dve.wait_ge(loaded_c, 16)
            own.mark(dve.tensor_reduce(col[:, 0:1], wf, AX.XY, ALU.add, apply_absolute_value=True), wabs_ready, 1)
            evac(dve.tensor_scalar(col[:, 1:2], full("wsum")[:, 0:1], 1.0 / (D * D), 1e-6, ALU.mult, ALU.max), "wsum")
            own.settle()
            own.step(dve.reciprocal(col[:, 2:3], col[:, 1:2]))
            own.settle()
            own.step(dve.tensor_scalar(wf, wf, col[:, 2:3], MAGIC, ALU.mult, ALU.add))
            own.settle()
            own.step(dve.tensor_scalar(wf, wf, -MAGIC, 1.0, ALU.add, ALU.min))
            own.settle()
            own.mark(dve.tensor_scalar(wq8, wf, -1.0, None, ALU.max), wq8_ready, 1)
            own.step(dve.tensor_scalar(col[:, 3:4], col[:, 1:2], 1.0 / 127.0, None, ALU.mult))
            dve.wait_ge(gate_ready, 1)
            own.step(dve.tensor_scalar(gg[:, 0:1], gg[:, 0:1], 1.0, None, ALU.add))
            own.settle()
            own.step(dve.reciprocal(gg[:, 0:1], gg[:, 0:1]))
            own.settle()
            own.step(dve.tensor_scalar(gg[:, 1:2], gg[:, 0:1], -1.0, 1.0, ALU.mult, ALU.add))
            own.settle()

            def mask_scores(b):
                evac(dve.tensor_tensor(AT[:, b % 2, :], full(f"at{b}")[:, 0:3 * P], mask3, ALU.mult), f"at{b}")

            def gated_outputs(b):
                w = DA + 1
                first = banks.bank(f"ml{b * TB}")
                assert banks.bank(f"ml{b * TB + 1}") == first + 1
                for n in range(b * TB, (b + 1) * TB):
                    full(f"ml{n}")
                den = col[:, 8 + 4 * b:12 + 4 * b].rearrange("p (n g) -> p n g", n=TB)
                own.step(dve.tensor_scalar(den, ps[:, first:first + TB, DA:2 * w:w], EPS_A, None, ALU.add))
                own.settle()
                own.step(dve.reciprocal(den, den))
                own.settle()
                own.step(dve.tensor_tensor(den, den, gg[:].unsqueeze(1).to_broadcast([P, TB, 2]), ALU.mult))
                own.settle()
                for n in range(TB):
                    own.step(dve.tensor_scalar(AO[:, b * TB + n, :], ps[:, first + n, 0:DA], den[:, n, 0:1], None,
                                               ALU.mult))
                own.settle()
                for n in range(TB):
                    ao = AO[:, b * TB + n, :]
                    evac(dve.scalar_tensor_tensor(out=ao, in0=ps[:, first + n, w:w + DA], scalar=den[:, n, 1:2],
                                                  in1=ao, op0=ALU.mult, op1=ALU.add), f"ml{b * TB + n}")

            def add_to_x(name, b, i=0):
                xb = X[:, b * TB:(b + 1) * TB, :].rearrange("p n d -> p (n d)")
                evac(dve.tensor_tensor(xb, full(name, i), xb, ALU.add), name, i)

            for name in A_ORDER:
                n = int(name[2:])
                if name[:2] == "at":
                    mask_scores(n)
                elif name[:2] == "ml" and n % TB == TB - 1:
                    gated_outputs(n // TB)
                elif name[:2] == "ax":
                    add_to_x(name, n)

            own.settle()
            for group in GROUPS:
                layer_norm(1, group)
            for g, group in enumerate(GROUPS):
                tt = slice(group[0] * TB, (group[-1] + 1) * TB)
                for n in range(tt.start, tt.stop):
                    own.step(dve.bn_stats(st6[:, n, :], full(f"bs{n // TB}")[:, (n % TB) * S:(n % TB + 1) * S]))
                own.settle()
                for n in range(tt.start, tt.stop):
                    own.step(dve.bn_aggr(mv[:, n, :], st6[:, n, :]))
                inverse_root(EPS_SIM, group)
                own.mark(dve.scalar_tensor_tensor(out=nmr[:, tt], in0=mv[:, tt, 0], scalar=-1.0, in1=rstd[:, tt],
                                                  op0=ALU.mult, op1=ALU.mult), simnorm_ready, g + 1)
            dve.wait_ge(loaded_b, 32)
            for b in range(B):
                sl = slice(b * TB, (b + 1) * TB)
                dve.wait_ge(evacuated[banks.bank(f"bs{b}")], banks.after(f"bs{b}"))
                own.step(dve.tensor_tensor(SIM[:, sl, :], SIM[:, sl, :],
                                           gamma.unsqueeze(1).to_broadcast([P, TB, D]), ALU.mult))
                own.settle()
                own.step(dve.tensor_tensor(SIM[:, sl, :], SIM[:, sl, :],
                                           beta.unsqueeze(1).to_broadcast([P, TB, D]), ALU.add))
                own.settle()
                own.mark(dve.tensor_reduce(col[:, NT + b * TB:NT + (b + 1) * TB], SIM[:, sl, :], AX.X, ALU.max,
                                             negate=True), simmax_ready, b + 1)

            def add_attended(b):
                dve.wait_ge(simexp_ready, (b + 1) * TB)
                c0 = 2 * NT + b * TB
                own.step(dve.reciprocal(col[:, c0:c0 + TB], col[:, c0:c0 + TB]))
                own.settle()
                for n in range(b * TB, (b + 1) * TB):
                    own.step(dve.scalar_tensor_tensor(out=X[:, n, :], in0=SIM[:, n, :],
                                                      scalar=col[:, 2 * NT + n:2 * NT + n + 1], in1=X[:, n, :],
                                                      op0=ALU.mult, op1=ALU.add))

            def quantize(g):
                group = GROUPS[g]
                tt = slice(group[0] * TB, (group[-1] + 1) * TB)
                amax = col[:, 4 * NT + tt.start:4 * NT + tt.stop]
                qs = col[:, 5 * NT + tt.start:5 * NT + tt.stop]
                dve.wait_ge(h_odd, 2 * B + group[-1] + 1)
                own.settle()
                own.step(dve.tensor_reduce(amax, HN[:, tt, :], AX.X, ALU.max, apply_absolute_value=True))
                own.settle()
                own.step(dve.tensor_scalar(amax, amax, 1e-8, None, ALU.max))
                own.settle()
                own.step(dve.reciprocal(qs, amax))
                own.settle()
                own.step(dve.tensor_scalar(qs, qs, 127.0, None, ALU.mult))
                own.step(dve.tensor_scalar(amax, amax, col[:, 3:4], None, ALU.mult))
                own.settle()
                for n in range(tt.start, tt.stop):
                    own.step(dve.tensor_scalar(HN[:, n, :], HN[:, n, :], col[:, 5 * NT + n:5 * NT + n + 1], MAGIC,
                                               ALU.mult, ALU.add))
                own.settle()
                own.step(dve.tensor_scalar(HN[:, tt, :], HN[:, tt, :], -MAGIC, 127.0, ALU.add, ALU.min))
                own.settle()
                own.mark(dve.tensor_scalar(XQ[:, tt, :], HN[:, tt, :], -127.0, None, ALU.max), xq_ready, g + 1)

            for group in GROUPS:
                for b in group:
                    add_attended(b)
                own.settle()
                layer_norm(2, group)
            for g in range(2):
                quantize(g)

            def add_fed(group):
                for b in group:
                    for n in range(b * TB, (b + 1) * TB):
                        ins = dve.scalar_tensor_tensor(out=X[:, n, :],
                                                       in0=full(f"cy{b}")[:, (n % TB) * D:(n % TB + 1) * D],
                                                       scalar=col[:, 4 * NT + n:4 * NT + n + 1], in1=X[:, n, :],
                                                       op0=ALU.mult, op1=ALU.add)
                        if n % TB == TB - 1:
                            evac(ins, f"cy{b}")
                        else:
                            own.step(ins)
                own.settle()

            add_fed(GROUPS[0])
            layer_norm(3, GROUPS[0])
            add_fed(GROUPS[1])
            own.mark(dve.tensor_copy(col[:, 0:1], col[:, 1:2]), x_after_c, 1)

            WH32, HTH32, OH32, EMH32 = (v[:].bitcast(F32) for v in (WH, HTH, OH, EMH))

            def split_lo(name, at_col, raw, count):
                cols = slice(at_col, at_col + raw.shape[-1])
                dve.wait_ge(hi_ready[name], count)
                own.mark(dve.tensor_tensor(WL[:, cols], raw, WH32[:, cols], ALU.subtract), lo_ready[name], count)

            flat = lambda v: v.rearrange("p a b -> p (a b)") if len(v.shape) == 3 else v.rearrange("p a b c -> p (a b c)")

            def split_ht_lo(k, batches=range(B)):
                for b in batches:
                    tt = slice(b * S, (b + 1) * S)
                    dve.wait_ge(ht_hi, (k - 3) * B + b + 1)
                    src = ps[:, banks.bank(f"ht{k}_{b}"), :].rearrange("p (c s) -> p c s", c=C)
                    evac(dve.tensor_tensor(HTL[:, :, tt], src, HTH32[:, :, tt], ALU.subtract), f"ht{k}_{b}")

            layer_norm(3, GROUPS[1])
            split_lo("sv", SV_AT, flat(wsv[:]), 1)
            split_ht_lo(3)
            split_lo("qk", QK_AT, flat(wqk[:]), 1)
            split_lo("g", G_AT, flat(wg[:]), 1)

            def clip_s(name, i=0):
                for g in range(2):
                    evac(dve.tensor_scalar(ET[:, g * HALF:(g + 1) * HALF], full(f"{name}{g}", i), 32.0, -32.0,
                                           ALU.min, ALU.max), f"{name}{g}", i)

            def slot_attention_trip(i, last_trip=False):
                for half in range(2):
                    evac(dve.tensor_copy(kT[:, half * HALF:(half + 1) * HALF], full(f"d.k{half}", i)), f"d.k{half}", i)
                for g in range(2):
                    pb = ps[:, banks.bank(f"d.em{g}"), :].rearrange("p (a b) -> p a b", a=4)
                    dve.wait_ge(em_hi, i * 2 + (g + 1))
                    own.step(dve.tensor_copy(EM[:, 4 * g:4 * g + 4, :], pb))
                    evac(dve.tensor_tensor(EML[:, 4 * g:4 * g + 4, :], pb, EMH32[:, 4 * g:4 * g + 4, :], ALU.subtract),
                         f"d.em{g}", i)

                def mask(name, dst, j):
                    name = f"d.{name}{j}"
                    evac(dve.tensor_tensor(dst[:, j % 4, :], full(name, i)[:, 0:3 * P], mask3, ALU.mult), name, i)

                def softmax_in(g):
                    sl = slice(4 * g, 4 * g + 4)
                    pm = PM[:, sl, :].rearrange("p a b -> p (a b)")
                    heads = PM[:, sl, :].rearrange("p n (h m) -> p (n h) m", h=2)
                    mx = slotmax[:, 8 * g:8 * g + 8]
                    dve.wait_ge(rc_ready, i * 2 + (g + 1))
                    evac(dve.tensor_tensor(pm, full(f"d.ok{g}", i), RC[:, sl, :].rearrange("p a b -> p (a b)"), ALU.mult),
                         f"d.ok{g}", i)
                    own.settle()
                    own.step(dve.tensor_reduce(mx, heads, AX.X, ALU.max))
                    own.settle()
                    own.mark(dve.tensor_tensor(heads, heads, mx.unsqueeze(2).to_broadcast([P, 8, M]), ALU.subtract),
                               ok_shifted, i * 2 + (g + 1))

                def softmax_out(g):
                    sl = slice(4 * g, 4 * g + 4)
                    pm = PM[:, sl, :]
                    dve.wait_ge(ok_exp, i * 2 + (g + 1))
                    own.mark(dve.tensor_tensor(EM[:, sl, :], pm, RC[:, sl, :], ALU.mult), p_ready, i * 2 + (g + 1))

                def softmax_sums(g):
                    s8 = slice(8 * g, 8 * g + 8)
                    heads = PM[:, 4 * g:4 * g + 4, :].rearrange("p n (h m) -> p (n h) m", h=2)
                    own.step(dve.tensor_reduce(slotsum[:, s8], heads, AX.X, ALU.add))
                    own.settle()
                    own.step(dve.reciprocal(rs[:, s8], slotsum[:, s8]))
                    own.settle()
                    own.step(dve.tensor_tensor(rs2[:, s8], rs[:, s8], rs[:, s8], ALU.mult))

                def split_outputs_lo(b):
                    sl = slice(b * S, (b + 1) * S)
                    dve.wait_ge(ot_hi, i * B + (b + 1))
                    pb = ps[:, banks.bank(f"d.ot{b}"), :].rearrange("p (h s) -> p h s", h=2)
                    evac(dve.scalar_tensor_tensor(out=OL[:, :, sl], in0=pb, scalar=gnorm[:, 0:1], in1=OH32[:, :, sl],
                                                  op0=ALU.mult, op1=ALU.subtract), f"d.ot{b}", i)

                def gate_outputs(b):
                    s4 = slice(4 * b, 4 * b + 4)
                    dve.wait_ge(sumsq_ready, i * B + (b + 1))
                    own.step(dve.tensor_tensor(rmsv[:, s4], sumsq[:, s4], rs2[:, s4], ALU.mult))
                    own.settle()
                    own.mark(dve.tensor_scalar(rmsv[:, s4], rmsv[:, s4], 1.0 / DV, EPS_RMS, ALU.mult, ALU.add),
                             rmsv_ready, i * B + (b + 1))
                    dve.wait_ge(rms_guess, i * B + (b + 1))
                    own.step(dve.tensor_tensor(coef[:, s4], rmsl[:, s4], rs[:, s4], ALU.mult))
                    own.settle()
                    pb = full(f"d.o{b}", i)
                    for j in range(4):
                        n, h = b * TB + j // 2, j % 2
                        hv = slice(h * DV, (h + 1) * DV)
                        ins = dve.scalar_tensor_tensor(out=SG[:, n, hv], in0=pb[:, j * DV:(j + 1) * DV],
                                                       scalar=coef[:, b * 4 + j:b * 4 + j + 1], in1=SG[:, n, hv],
                                                       op0=ALU.mult, op1=ALU.mult)
                        if j == 3:
                            evac(ins, f"d.o{b}", i)
                        else:
                            own.step(ins)

                for j in range(4):
                    mask("at", ATd, j)
                softmax_in(0)
                for j in range(4, 6):
                    mask("at", ATd, j)
                softmax_out(0)
                for j in range(6, 8):
                    mask("at", ATd, j)
                softmax_sums(0)
                softmax_in(1)
                for j in range(2):
                    mask("bt", BTd, j)
                softmax_out(1)
                for j in range(2, 4):
                    mask("bt", BTd, j)
                softmax_sums(1)
                gate_outputs(0)
                gate_outputs(1)
                for j in range(4, 8):
                    mask("bt", BTd, j)
                split_outputs_lo(0)
                split_outputs_lo(1)
                if not last_trip:
                    split_lo("sv", SV_AT, flat(wsv[:]), i + 2)
                    split_lo("qk", QK_AT, flat(wqk[:]), i + 2)
                split_lo("o", O_AT, flat(wo[:]), i + 1)
                gate_outputs(2)
                gate_outputs(3)
                if not last_trip:
                    clip_s("d.s", i)
                for b in range(2, B):
                    split_outputs_lo(b)
                if not last_trip:
                    split_lo("g", G_AT, flat(wg[:]), i + 2)
                for b in range(B):
                    add_to_x(f"d.dx{b}", b, i)

            clip_s("first_s")
            dve.wait_ge(loaded_gnorm, 16)
            with dve.Fori(0, PAIRS - 1) as i:
                own.enter(i, 2 + 2 * (1 + 3) + 4 * (2 + 3))
                slot_attention_trip(i)
                own.leave(PAIRS - 1)
            slot_attention_trip(PAIRS - 1, last_trip=True)
            own.settle()
            layer_norm(4)

            def add_and_normalize(step, k):
                for batches in ((0, 1), (2,), (3,)):
                    for b in batches:
                        add_to_x(f"{step}{b}", b)
                    own.settle()
                    layer_norm(k, batches)
                    split_ht_lo(k, batches)

            split_t = lambda i: Tall[:, ds(i, 1), :, :].rearrange("p i c n -> p (i c n)")
            split_lo("t", T_AT, Tall[:, 0].rearrange("p c n -> p (c n)"), 1)
            split_ht_lo(4)
            own.mark(dve.tensor_copy(col[:, 0:1], col[:, 1:2]), x_after_d, 1)

            evac(dve.tensor_copy(QE[:, HALF:], full("first_q1")), "first_q1")

            def context_attention_trip(i, last_trip=False):
                def scale(b, h):
                    name = f"e.sc{b}{h}"
                    dve.wait_ge(evacuated[banks.bank(name)], banks.after(name, i))
                    es = esum[:, b * TB:(b + 1) * TB, h]
                    own.step(dve.reciprocal(es, es))
                    own.settle()
                    for n in range(TB):
                        px = PX[:, b % 2, h, n, :]
                        ins = dve.tensor_scalar(px, px, esum[:, b * TB + n, h:h + 1], None, ALU.mult)
                        if n == 0:
                            own.step(ins)
                        else:
                            own.mark(ins, px_scaled, i * 8 + (2 * b + h + 1))

                def negated_max(b, h):
                    name = f"e.sc{b}{h}"
                    own.mark(dve.tensor_reduce(nmx[:, b * TB:(b + 1) * TB, h], full(name, i).rearrange("p (n s) -> p n s", n=TB),
                                               AX.X, ALU.max, negate=True), emax_ready, i * 8 + (2 * b + h + 1))

                def probs_T(b, h):
                    name = f"e.pt{b}{h}"
                    evac(dve.tensor_copy(PXT[:, b % 2, h, :, :].rearrange("p a b -> p (a b)"), full(name, i)), name, i)

                for step, b, h in ((negated_max, 0, 0), (negated_max, 0, 1), (scale, 0, 0), (negated_max, 1, 0), (scale, 0, 1),
                                   (negated_max, 1, 1), (scale, 1, 0), (probs_T, 0, 1), (scale, 1, 1), (negated_max, 2, 0),
                                   (negated_max, 2, 1), (scale, 2, 0), (probs_T, 1, 1), (scale, 2, 1), (negated_max, 3, 0),
                                   (negated_max, 3, 1), (scale, 3, 0), (probs_T, 2, 1), (scale, 3, 1), (probs_T, 3, 1)):
                    step(b, h)
                    if (step, b) == (probs_T, 1) and not last_trip:
                        split_lo("t", T_AT, split_t(i + 1), i + 2)
                if not last_trip:
                    evac(dve.tensor_copy(QE[:, HALF:], full("e.q1", i)), "e.q1", i)

            with dve.Fori(0, PAIRS - 1) as i:
                own.enter(i, 8 * 2)
                context_attention_trip(i)
                own.leave(PAIRS - 1)
            context_attention_trip(PAIRS - 1, last_trip=True)
            for e in range(2):
                split_lo(f"f{e}", e * F_COLS, fgu[:, e].rearrange("p x c f -> p (x c f)"), 1)
            split_lo("r", T_AT + C * 2 * DC, flat(wr), 1)
            add_and_normalize("ex", 5)

            dve.wait_ge(loaded_router, 16 * 4)
            dve.wait_ge(evacuated[banks.bank("lg")], banks.after("lg"))
            revb = rev.unsqueeze(1).to_broadcast([P, NT, E])
            bcast = lambda v: v.unsqueeze(2).to_broadcast([P, NT, E])
            src = AFF
            for k in range(2):
                best, first = tk[:, 2 * k, :], tk[:, 2 * k + 1, :]
                pick = TK[:, k, :, :]
                own.step(dve.tensor_reduce(best, src, AX.X, ALU.max))
                own.settle()
                own.step(dve.tensor_tensor(pick, src, bcast(best), ALU.is_equal))
                own.settle()
                own.step(dve.tensor_tensor(pick, pick, revb, ALU.mult))
                own.settle()
                own.step(dve.tensor_reduce(first, pick, AX.X, ALU.max))
                own.settle()
                own.step(dve.tensor_tensor(pick, pick, bcast(first), ALU.is_equal))
                own.settle()
                if k == 0:
                    own.step(dve.scalar_tensor_tensor(out=TK[:, 2, :, :], in0=pick, scalar=-4.0, in1=AFF, op0=ALU.mult,
                                                      op1=ALU.add))
                    own.settle()
                    src = TK[:, 2, :, :]
            own.step(dve.tensor_tensor(tk[:, 4, :], tk[:, 0, :], tk[:, 2, :], ALU.add))
            own.settle()
            own.step(dve.reciprocal(tk[:, 4, :], tk[:, 4, :]))
            own.settle()
            for k in range(2):
                own.step(dve.tensor_tensor(tk[:, 2 * k, :], tk[:, 2 * k, :], tk[:, 4, :], ALU.mult))
            own.settle()
            for k in range(2):
                own.step(dve.tensor_tensor(TK[:, k, :, :], TK[:, k, :, :], bcast(tk[:, 2 * k, :]), ALU.mult))
            own.step(dve.memset(CB[:, :, E:NE], 1.0))
            own.settle()
            own.mark(dve.tensor_tensor(CB[:, :, 0:E], TK[:, 0, :, :], TK[:, 1, :, :], ALU.add), shares_ready, 1)
            evac(dve.tensor_copy(CBT[:, 0:HALF], full("cb0")[0:NE, :]), "cb0")
            evac(dve.tensor_copy(CBT[:, HALF:], full("cb1")[0:NE, :]), "cb1")
            own.settle()
            own.mark(dve.tensor_copy(col[:, 0:1], col[:, 1:2]), comb_ready, 1)
            own.step(dve.tensor_tensor(X[:], X[:], HN[:], ALU.add))

            def experts_trip(i, last_trip=False):
                def split_yc_lo(e):
                    for half in range(2):
                        sl = slice(half * HALF, (half + 1) * HALF)
                        count = i * 4 + (2 * e + half + 1)
                        dve.wait_ge(yc_hi, count)
                        own.mark(dve.tensor_tensor(OL[:, e, sl], YC[:, e, sl], OH32[:, e, sl], ALU.subtract), yc_lo, count)

                for e in range(2):
                    dve.wait_ge(loaded_fb[e], i * 32 + 32)
                    for half in range(2):
                        sl = slice(half * HALF, (half + 1) * HALF)
                        g_name, name = f"f.g{half}{e}", f"f.u{half}{e}"
                        dve.wait_ge(evacuated[banks.bank(g_name)], banks.after(g_name, i))
                        evac(dve.scalar_tensor_tensor(out=YC[:, e, sl], in0=full(name, i), scalar=fub[:, e], in1=Y[:, e, sl],
                                                      op0=ALU.add, op1=ALU.mult), name, i)
                        if half == 0:
                            dve.wait_ge(loaded_bc[e], i * 16 + 16)
                        own.settle()
                        own.mark(dve.tensor_tensor(YC[:, e, sl], YC[:, e, sl], BC[:, e, sl], ALU.mult), yc_ready,
                                   i * 4 + (2 * e + half + 1))
                    if e == 0:
                        for o in range(2):
                            split_lo(f"fo{o}", O_AT + o * D, fo[:, o, :], i + 1)
                    split_yc_lo(e)
                if not last_trip:
                    for e in range(2):
                        split_lo(f"f{e}", e * F_COLS, fgu[:, e].rearrange("p x c f -> p (x c f)"), i + 2)

            with dve.Fori(0, F_TRIPS - 1) as i:
                experts_trip(i)
            experts_trip(F_TRIPS - 1, last_trip=True)
            dve.wait_ge(experts_out, F_TRIPS)
            for b in range(B):
                xb = X[:, b * TB:(b + 1) * TB, :].rearrange("p n d -> p (n d)")
                own.mark(dve.tensor_tensor(xb, ps[:, banks.bank(f"acc{b}"), :], xb, ALU.add), x_final, b + 1)


def constants(ctx_shape, experts):
    _, length, dim = ctx_shape
    i = np.arange(P)
    ident = (i[:, None] == i[None, :]).astype(np.float32)
    causal = (i[:, None] <= i[None, :]).astype(np.float32)
    const = np.concatenate([ident, causal, np.ones((P, P), np.float32), causal], axis=1)
    one = np.float32(1.0)
    inv = one / np.float32(10000.0) ** (np.arange(0, dim, 2, dtype=np.float32) / np.float32(dim))
    freqs = np.arange(length, dtype=np.float32)[:, None] * inv[None, :].astype(np.float32)
    cos = np.repeat(np.cos(freqs), 2, axis=-1)
    sin = np.repeat(np.sin(freqs), 2, axis=-1)
    sin[:, : dim // 2] *= -1
    return {"const": const, "rope": np.stack([cos, sin]).astype(np.float32),
            "rev": np.arange(experts, 0, -1).astype(np.float32)}


def kernel(**inputs):
    import numpy as _np
    import concourse.bacc as _bacc
    from concourse import mybir as _mybir
    from concourse.bass_utils import run_bass_kernel_spmd as _run

    nc = _bacc.Bacc("TRN2", target_bir_lowering=False, num_devices=1)
    arrays = {n: _np.ascontiguousarray(a) for n, a in inputs.items()}
    arrays.update(constants(arrays["ctx_512"].shape, arrays["L1_ffn_wa"].shape[1]))
    aps = {n: nc.dram_tensor(f"in_{n}", a.shape, _mybir.dt.from_np(a.dtype), kind="ExternalInput").ap()
           for n, a in arrays.items()}
    shape = arrays["x"].shape
    out = nc.dram_tensor("out_x", shape, _mybir.dt.float32, kind="ExternalOutput").ap()
    decoder_kernel(nc, aps, out)
    r = _run(nc, [{f"in_{n}": a for n, a in arrays.items()}], core_ids=[0])
    return r.results[0]["out_x"]
```
